# Optimizing a Trainium2 kernel written in Bass

```python
import numpy as np
import jax
import jax.numpy as jnp

def _softmax(x, axis=-1):
    return jax.nn.softmax(x, axis=axis)

def _gelu(x):
    return jax.nn.gelu(x, approximate=True)

def _silu(x):
    return jax.nn.silu(x)

def _sigmoid(x):
    return jax.nn.sigmoid(x)

def _layernorm(x, axis=-1, eps=1e-05):
    m = jnp.mean(x, axis=axis, keepdims=True)
    v = jnp.var(x, axis=axis, keepdims=True)
    return (x - m) / jnp.sqrt(v + eps)

def _scatter_add(tgt, idx, src, axis=0):
    return tgt.at[idx].add(src)

def _segment_sum(src, seg, n):
    return jax.ops.segment_sum(src, seg, n)
kernel_name = 'mk_seq_postln_d1_jaxref_r4_2c5564'

def setup_inputs(seed: int=0):
    np.random.seed(seed)
    _w = jnp.asarray

    def _L0_attn_setup():
        import jax, jax.numpy as jnp
        import numpy as np
        DIM = 256
        N_HEADS = 16
        HEAD_DIM = DIM // N_HEADS
        FREQS = [31.0, 37.0, 41.0, 43.0, 47.0]
        TWO_PI = 2.0 * float(np.pi)
        key = jax.random.key(seed)
        ks = jax.random.split(key, 16)
        B, L = (2, 256)
        s = 0.02
        inp = {'x': jax.random.normal(ks[0], (B, L, DIM), dtype=jnp.float32), 'Wq': jax.random.normal(ks[1], (DIM, DIM), dtype=jnp.float32) * s, 'bq': jnp.zeros((DIM,), dtype=jnp.float32), 'Wk': jax.random.normal(ks[2], (DIM, DIM), dtype=jnp.float32) * s, 'bk': jnp.zeros((DIM,), dtype=jnp.float32), 'Wv': jax.random.normal(ks[3], (DIM, DIM), dtype=jnp.float32) * s, 'bv': jnp.zeros((DIM,), dtype=jnp.float32), 'Wo': jax.random.normal(ks[4], (DIM, DIM), dtype=jnp.float32) * s, 'bo': jnp.zeros((DIM,), dtype=jnp.float32), 'alpha': jax.random.normal(ks[5], (N_HEADS, len(FREQS)), dtype=jnp.float32) * 0.1, 'phi': jax.random.uniform(ks[6], (N_HEADS, len(FREQS)), dtype=jnp.float32) * TWO_PI, 'temperature': jnp.ones((1,), dtype=jnp.float32), 'gamma': jnp.ones((DIM,), dtype=jnp.float32), 'beta': jnp.zeros((DIM,), dtype=jnp.float32)}
        return inp
    _L0_attn_in = _L0_attn_setup()

    def _L0_ffn_setup():
        import jax, jax.numpy as jnp
        import numpy as np
        B, S, D, H, F = (4, 1024, 256, 16, 1024)
        CAP = 0.125
        ROPE_BASE = 10000.0

        def rmsnorm(x, g):
            return x * jax.lax.rsqrt(jnp.mean(x * x, -1, keepdims=True) + 1e-06) * g

        def rope(t, pos):
            hd = t.shape[-1]
            inv = 1.0 / ROPE_BASE ** (jnp.arange(0, hd, 2, dtype=jnp.float32) / hd)
            f = pos[:, None, :, None].astype(jnp.float32) * inv
            emb = jnp.concatenate([f, f], axis=-1)
            cos, sin = (jnp.cos(emb), jnp.sin(emb))
            rot = jnp.concatenate([-t[..., hd // 2:], t[..., :hd // 2]], axis=-1)
            return t * cos + rot * sin
        key = jax.random.key(seed)
        ks = jax.random.split(key, 9)
        scale = 0.02
        x = jax.random.normal(ks[0], (B, S, D), jnp.float32)
        causal = jnp.where(jnp.tril(jnp.ones((S, S), bool)), 0.0, -1000000000.0).astype(jnp.float32)
        attention_mask = jnp.broadcast_to(causal[None, None], (B, 1, S, S))
        position_ids = jnp.broadcast_to(jnp.arange(S, dtype=jnp.int32), (B, S))
        return {'x': x, 'attention_mask': attention_mask, 'position_ids': position_ids, 'router_w': jax.random.normal(ks[1], (D, 1), jnp.float32) * scale, 'router_b': jnp.zeros((1,), jnp.float32), 'wq': jax.random.normal(ks[2], (D, D), jnp.float32) * scale, 'wk': jax.random.normal(ks[3], (D, D), jnp.float32) * scale, 'wv': jax.random.normal(ks[4], (D, D), jnp.float32) * scale, 'wo': jax.random.normal(ks[5], (D, D), jnp.float32) * scale, 'w1': jax.random.normal(ks[6], (D, F), jnp.float32) * scale, 'w2': jax.random.normal(ks[7], (F, D), jnp.float32) * scale, 'ln1': jnp.ones((D,), jnp.float32), 'ln2': jnp.ones((D,), jnp.float32)}
    _L0_ffn_in = _L0_ffn_setup()
    _d = {'L0_attn_x': _L0_attn_in['x'], 'L0_attn_Wq': _L0_attn_in['Wq'], 'L0_attn_bq': _L0_attn_in['bq'], 'L0_attn_Wk': _L0_attn_in['Wk'], 'L0_attn_bk': _L0_attn_in['bk'], 'L0_attn_Wv': _L0_attn_in['Wv'], 'L0_attn_bv': _L0_attn_in['bv'], 'L0_attn_Wo': _L0_attn_in['Wo'], 'L0_attn_bo': _L0_attn_in['bo'], 'L0_attn_alpha': _L0_attn_in['alpha'], 'L0_attn_phi': _L0_attn_in['phi'], 'L0_attn_temperature': _L0_attn_in['temperature'], 'L0_attn_gamma': _L0_attn_in['gamma'], 'L0_attn_beta': _L0_attn_in['beta'], 'L0_ffn_attention_mask': _L0_ffn_in['attention_mask'], 'L0_ffn_position_ids': _L0_ffn_in['position_ids'], 'L0_ffn_router_w': _L0_ffn_in['router_w'], 'L0_ffn_router_b': _L0_ffn_in['router_b'], 'L0_ffn_wq': _L0_ffn_in['wq'], 'L0_ffn_wk': _L0_ffn_in['wk'], 'L0_ffn_wv': _L0_ffn_in['wv'], 'L0_ffn_wo': _L0_ffn_in['wo'], 'L0_ffn_w1': _L0_ffn_in['w1'], 'L0_ffn_w2': _L0_ffn_in['w2'], 'L0_ffn_ln1': _L0_ffn_in['ln1'], 'L0_ffn_ln2': _L0_ffn_in['ln2']}
    _x0 = _d['L0_attn_x']
    _d['L0_attn_x'] = jax.random.normal(jax.random.fold_in(jax.random.key(seed), 1), (8, 1024, 256), dtype=_x0.dtype)
    del _x0
    return _d

def reference(L0_attn_x, L0_attn_Wq, L0_attn_bq, L0_attn_Wk, L0_attn_bk, L0_attn_Wv, L0_attn_bv, L0_attn_Wo, L0_attn_bo, L0_attn_alpha, L0_attn_phi, L0_attn_temperature, L0_attn_gamma, L0_attn_beta, L0_ffn_attention_mask, L0_ffn_position_ids, L0_ffn_router_w, L0_ffn_router_b, L0_ffn_wq, L0_ffn_wk, L0_ffn_wv, L0_ffn_wo, L0_ffn_w1, L0_ffn_w2, L0_ffn_ln1, L0_ffn_ln2):

    def _L0_attn_ref(x, Wq, bq, Wk, bk, Wv, bv, Wo, bo, alpha, phi, temperature, gamma, beta):
        import jax, jax.numpy as jnp
        import numpy as np
        DIM = 256
        N_HEADS = 16
        HEAD_DIM = DIM // N_HEADS
        FREQS = [31.0, 37.0, 41.0, 43.0, 47.0]
        TWO_PI = 2.0 * float(np.pi)
        B, L, D = x.shape
        H, hd = (N_HEADS, HEAD_DIM)
        q = (x @ Wq.T + bq).reshape(B, L, H, hd).transpose(0, 2, 1, 3)
        k = (x @ Wk.T + bk).reshape(B, L, H, hd).transpose(0, 2, 1, 3)
        v = (x @ Wv.T + bv).reshape(B, L, H, hd).transpose(0, 2, 1, 3)
        sim = jnp.einsum('bhid,bhjd->bhij', q, k) / jnp.sqrt(jnp.asarray(hd, x.dtype))
        temp = jnp.abs(temperature)[0] + 0.1
        sim = sim / temp
        scores = jnp.zeros_like(sim)
        for fi, freq in enumerate(FREQS):
            a = alpha[:, fi][None, :, None, None]
            p = phi[:, fi][None, :, None, None]
            scores = scores + a * jnp.sin(TWO_PI * sim / freq + p)
        w = jax.nn.sigmoid(scores)
        w = w / (jnp.sum(w, axis=-1, keepdims=True) + 1e-10)
        out = jnp.einsum('bhij,bhjd->bhid', w, v)
        out = out.transpose(0, 2, 1, 3).reshape(B, L, D)
        out = out @ Wo.T + bo
        mu = jnp.mean(out, axis=-1, keepdims=True)
        var = jnp.mean(jnp.square(out - mu), axis=-1, keepdims=True)
        return (out - mu) / jnp.sqrt(var + 1e-05) * gamma + beta

    def _L0_ffn_ref(x, attention_mask, position_ids, router_w, router_b, wq, wk, wv, wo, w1, w2, ln1, ln2):
        import jax, jax.numpy as jnp
        import numpy as np
        B, S, D, H, F = (4, 1024, 256, 16, 1024)
        CAP = 0.125
        ROPE_BASE = 10000.0

        def rmsnorm(x, g):
            return x * jax.lax.rsqrt(jnp.mean(x * x, -1, keepdims=True) + 1e-06) * g

        def rope(t, pos):
            hd = t.shape[-1]
            inv = 1.0 / ROPE_BASE ** (jnp.arange(0, hd, 2, dtype=jnp.float32) / hd)
            f = pos[:, None, :, None].astype(jnp.float32) * inv
            emb = jnp.concatenate([f, f], axis=-1)
            cos, sin = (jnp.cos(emb), jnp.sin(emb))
            rot = jnp.concatenate([-t[..., hd // 2:], t[..., :hd // 2]], axis=-1)
            return t * cos + rot * sin
        b, s, d = x.shape
        hd = d // H
        weights = (x @ router_w)[..., 0] + router_b[0]
        k = int(CAP * s)
        topv, topi = jax.lax.top_k(weights, k)
        thr = topv[:, -1]
        sel_mask = (weights > thr[:, None]).astype(x.dtype)
        kc = k - 1
        sel_idx = jnp.sort(topi[:, :kc], axis=1)
        bidx = jnp.arange(b)[:, None]
        x_sel = x[bidx, sel_idx]
        pos_sel = position_ids[bidx, sel_idx]
        w_sel = weights[bidx, sel_idx]
        m = attention_mask[:, 0]
        m_sel = m[bidx[:, :, None], sel_idx[:, :, None], sel_idx[:, None, :]]
        hn = rmsnorm(x_sel, ln1)

        def heads(t):
            return t.reshape(b, kc, H, hd).transpose(0, 2, 1, 3)
        q = rope(heads(hn @ wq), pos_sel)
        kk = rope(heads(hn @ wk), pos_sel)
        v = heads(hn @ wv)
        sc = jnp.einsum('bhqd,bhkd->bhqk', q, kk) / np.sqrt(hd).astype(np.float32)
        sc = sc + m_sel[:, None]
        a = jax.nn.softmax(sc, axis=-1)
        o = jnp.einsum('bhqk,bhkd->bhqd', a, v).transpose(0, 2, 1, 3).reshape(b, kc, d) @ wo
        x1 = x_sel + o
        x2 = x1 + jax.nn.gelu(rmsnorm(x1, ln2) @ w1) @ w2
        proc = x2 * w_sel[..., None]
        out = jnp.zeros_like(x).at[bidx, sel_idx].set(proc)
        return out + x * (1.0 - sel_mask)[..., None]
    x = L0_attn_x
    x = _layernorm(x + _L0_attn_ref(x, L0_attn_Wq, L0_attn_bq, L0_attn_Wk, L0_attn_bk, L0_attn_Wv, L0_attn_bv, L0_attn_Wo, L0_attn_bo, L0_attn_alpha, L0_attn_phi, L0_attn_temperature, L0_attn_gamma, L0_attn_beta), axis=-1)
    x = _layernorm(x + _L0_ffn_ref(x, L0_ffn_attention_mask, L0_ffn_position_ids, L0_ffn_router_w, L0_ffn_router_b, L0_ffn_wq, L0_ffn_wk, L0_ffn_wv, L0_ffn_wo, L0_ffn_w1, L0_ffn_w2, L0_ffn_ln1, L0_ffn_ln2), axis=-1)
    return x

_drawn_inputs = setup_inputs


def setup_inputs(seed=0):
    import zlib

    import numpy as np

    out = dict(_drawn_inputs(seed))
    spreads = {'L0_attn_bq': (0.0, 0.8),
     'L0_attn_bk': (0.0, 0.8),
     'L0_attn_bv': (0.0, 0.1),
     'L0_attn_bo': (0.0, 0.1),
     'L0_attn_gamma': (1.0, 0.2),
     'L0_attn_beta': (0.0, 0.1),
     'L0_ffn_ln1': (1.0, 0.6),
     'L0_ffn_ln2': (1.0, 0.6)}
    factors = {'L0_attn_Wq': 8.0,
     'L0_attn_Wk': 8.0,
     'L0_attn_alpha': 8.0,
     'L0_attn_phi': 8.0,
     'L0_ffn_router_w': 5.143,
     'L0_ffn_wq': 8.0,
     'L0_ffn_wk': 8.0,
     'L0_ffn_wv': 8.0,
     'L0_ffn_wo': 8.0,
     'L0_ffn_w1': 6.911,
     'L0_ffn_w2': 6.7}
    for name, (base, spread) in spreads.items():
        noise = np.random.default_rng([zlib.crc32(name.encode()), seed]).standard_normal(out[name].shape)
        drawn = base * np.exp(spread * noise) if base else spread * noise
        out[name] = jnp.asarray(drawn.astype(out[name].dtype))
    for name, factor in factors.items():
        out[name] = (out[name] * factor).astype(out[name].dtype)
    return out
```

```python
import numpy as np
import concourse.bass as bass
from concourse import mybir
from contextlib import ExitStack

FP32 = mybir.dt.float32
BF16 = mybir.dt.bfloat16
I32 = mybir.dt.int32
ALU = mybir.AluOpType
ACT = mybir.ActivationFunctionType
AX = mybir.AxisListType

B, L, D = 8, 1024, 256
H, HD = 16, 16
P = 128
LT = L // P
KC = D // P
HALF = 512
FREQS = [31.0, 37.0, 41.0, 43.0, 47.0]
NF = len(FREQS)
TWO_PI = 2.0 * float(np.pi)
FRAC = 22
TURN = float(2 ** FRAC)
WRAP = 32 - FRAC
ANGLE = float(np.nextafter(np.float32(TWO_PI / TURN), np.float32(0)))

F = 1024
FB = F // P
MB = 4
CAP = L // 8
KSEL = CAP - 1
ROPE_BASE = 10000.0
NROT = HD // 2
EPS_LN = 1e-5
EPS_RMS = 1e-6
EPS_DEN = 1e-10

PARTS = 3
TERMS = [(i, j) for j in range(PARTS) for i in range(PARTS)][:8]
PE_SINES = [4, 3, 4, 4, 3, 4, 3, 4]
ACT_TURNS = [1, 1, 0, 1, 1, 1, 0, 1]
VP = 32
GROUPS = P // VP
RING = 4
HEADS = B * H
VW = HD + 1


class Chain:

    def __init__(self, eng, sem, base, per_turn, turn):
        self.eng, self.sem, self.base, self.per_turn, self.turn, self.n = eng, sem, base, per_turn, turn, 0

    def step(self, ins):
        self.n += 1
        ins.then_inc(self.sem, 1)
        self.eng.wait_ge(self.sem, self.base + self.turn * self.per_turn + self.n)

    def close(self):
        assert self.n == self.per_turn, (self.n, self.per_turn)


def wait_pos(eng, sem, value):
    if not isinstance(value, int) or value > 0:
        eng.wait_ge(sem, value)


def project_qkv(nc, x, wq, bq, wk, bk, wv, bv, temperature, q_d, k_d, v_d):
    with ExitStack() as ctx:
        sb = lambda n, s, d=FP32: ctx.enter_context(nc.sbuf_tensor(n, s, d))
        sem = lambda n: ctx.enter_context(nc.semaphore(n))
        ident = sb("p_ident", [P, P])
        w_in = sb("p_w_in", [P, 3, KC, D])
        w_t = sb("p_w_t", [P, 3, KC, D])
        bias_qk = sb("p_bias_qk", [P, 2, KC])
        bv_row = sb("p_bv_row", [P, D])
        temp = sb("p_temp", [P, 5])
        x_in = sb("p_x_in", [P, 2, LT, D])
        x_t = sb("p_x_t", [P, KC, L])
        qk_sb = sb("p_qk_sb", [P, 2, KC, L])
        rest = sb("p_rest", [P, 2, 2, KC, L])
        parts = sb("p_parts", [P, 2, PARTS, KC, L], BF16)
        v_sb = sb("p_v_sb", [P, LT, D])
        lo = ctx.enter_context(nc.psum_tensor("p_lo", [P, 4, HALF], FP32))
        hi = ctx.enter_context(nc.psum_tensor("p_hi", [P, 4, HALF], FP32))
        w_loaded, b_loaded, ident_zero, ident_done = sem("w_loaded"), sem("b_loaded"), sem("p_id0"), sem("p_id1")
        w_turned, w_ready, temp_step = sem("w_turned"), sem("w_ready"), sem("temp_step")
        x_loaded = [sem("x_loaded0"), sem("x_loaded1")]
        x_turned, x_lo, x_hi = sem("x_turned"), sem("x_lo"), sem("x_hi")
        q_summed, k_summed, v_summed = sem("q_summed"), sem("k_summed"), sem("v_summed")
        q_ready, k_ready, v_ready = sem("q_ready"), sem("k_ready"), sem("v_ready")
        q_kept, k_kept, v_kept = sem("q_kept"), sem("k_kept"), sem("v_kept")
        q_split, k_split, split_step = sem("q_split"), sem("k_split"), sem("split_step")

        with nc.Block() as block:

            @block.sync
            def _(sp):
                for n, w in enumerate((wq, wk, wv)):
                    sp.dma_start(w_in[:, n, :, :], w.rearrange("(m p) i -> p m i", p=P)).then_inc(w_loaded, 16)
                sp.dma_start(bias_qk[:, 0, :], bq.rearrange("(m p) -> p m", p=P), allow_slow_non_contiguous=True).then_inc(b_loaded, 16)
                sp.dma_start(bias_qk[:, 1, :], bk.rearrange("(m p) -> p m", p=P), allow_slow_non_contiguous=True).then_inc(b_loaded, 16)
                sp.dma_start(bv_row[:], bv.partition_broadcast(P)).then_inc(b_loaded, 16)
                sp.dma_start(temp[:, 0:1], temperature.partition_broadcast(P)).then_inc(b_loaded, 16)
                with sp.Fori(0, B // 2, 1) as pair:
                    for k in range(2):
                        b = 2 * pair + k
                        sp.wait_ge(x_turned, 2 * pair + 1)
                        sp.dma_start(x_in[:, k, :, :],
                                     x[b, :, :].rearrange("(t p) d -> p t d", p=P)).then_inc(x_loaded[k], 16)

            @block.gpsimd
            def _(pool):
                nc.gpsimd.memset(ident[:], 0.0).then_inc(ident_zero, 1)
                pool.wait_ge(ident_zero, 1)
                nc.gpsimd.affine_select(out=ident[:], in_=ident[:], compare_op=ALU.not_equal, fill=1.0, base=0,
                                        pattern=[[-1, P]], channel_multiplier=1).then_inc(ident_done, 1)

            @block.tensor
            def _(pe):
                pe.sem_inc(x_turned, 1)
                pe.sem_inc(v_summed, 1)
                pe.wait_ge(ident_done, 1)
                pe.wait_ge(w_loaded, 48)
                for n in range(3):
                    for i in range(KC):
                        for m in range(KC):
                            last = nc.tensor.transpose(lo[:, n, i * D + m * P:i * D + (m + 1) * P],
                                                       w_in[:, n, m, i * P:(i + 1) * P], ident[:])
                last.then_inc(w_turned, 1)
                pe.wait_ge(w_ready, 1)

                with pe.Fori(0, B // 2, 1) as pair:
                    for k in range(2):
                        b = 2 * pair + k
                        pe.wait_ge(x_loaded[k], 16 * pair + 16)
                        pe.wait_ge(k_ready, b + 1)
                        for c in range(KC):
                            for t in range(LT):
                                last = nc.tensor.transpose(
                                    lo[:, 2 * c + t // 4, (t % 4) * P:(t % 4 + 1) * P],
                                    x_in[:, k, t, c * P:(c + 1) * P], ident[:])
                        last.then_inc(x_turned, 1)
                        pe.wait_ge(x_lo, b + 1)
                        pe.wait_ge(x_hi, b + 1)
                        pe.wait_ge(v_ready, b + 1)
                        for n, out, done in ((0, hi, q_summed), (1, lo, k_summed)):
                            for m in range(KC):
                                for half in range(2):
                                    for c in range(KC):
                                        last = nc.tensor.matmul(
                                            out[:, 2 * m + half, :], w_t[:, n, c, m * P:(m + 1) * P],
                                            x_t[:, c, half * HALF:(half + 1) * HALF],
                                            start=(c == 0), stop=(c == KC - 1))
                            last.then_inc(done, 1)
                        pe.wait_ge(q_ready, b + 1)
                        for t in range(LT):
                            for c in range(KC):
                                last = nc.tensor.matmul(hi[:, t // 2, (t % 2) * D:(t % 2 + 1) * D],
                                                        x_t[:, c, t * P:(t + 1) * P], w_t[:, 2, c, :],
                                                        start=(c == 0), stop=(c == KC - 1))
                        last.then_inc(v_summed, 1)

            @block.vector
            def _(dve):
                dve.sem_inc(v_ready, 1)
                dve.sem_inc(k_split, 1)
                dve.wait_ge(b_loaded, 64)
                nc.vector.scalar_tensor_tensor(temp[:, 1:2], temp[:, 0:1], -1.0, temp[:, 0:1], ALU.mult,
                                               ALU.max).then_inc(temp_step, 1)
                dve.wait_ge(temp_step, 1)
                nc.vector.tensor_scalar(temp[:, 4:5], temp[:, 1:2], 0.1, None, ALU.add).then_inc(temp_step, 1)
                dve.wait_ge(temp_step, 2)
                nc.vector.reciprocal(temp[:, 2:3], temp[:, 4:5]).then_inc(temp_step, 1)
                dve.wait_ge(temp_step, 3)
                nc.vector.tensor_scalar(temp[:, 3:4], temp[:, 2:3], 1.0 / float(np.sqrt(HD)), None,
                                        ALU.mult).then_inc(temp_step, 1)
                dve.wait_ge(w_turned, 1)
                nc.vector.tensor_copy(w_t[:].rearrange("p a b c -> p (a b c)"),
                                      lo[:, 0:3, :].rearrange("p a b -> p (a b)")).then_inc(w_ready, 1)
                dve.wait_ge(temp_step, 4)

                def split_in_parts(split, n, done):
                    flat = lambda ap: ap.rearrange("p m l -> p (m l)")
                    whole = qk_sb[:, n, :, :]
                    for i in range(PARTS):
                        ins = nc.vector.tensor_copy(flat(parts[:, n, i, :, :]), flat(whole))
                        if i == PARTS - 1:
                            ins.then_inc(done, 1)
                            break
                        split.step(ins)
                        left = rest[:, n, i, :, :]
                        split.step(nc.vector.tensor_tensor(flat(left), flat(whole), flat(parts[:, n, i, :, :]), ALU.subtract))
                        whole = left

                with dve.Fori(0, B, 1) as b:
                    dve.wait_ge(x_turned, b + 2)
                    dve.wait_ge(v_summed, b + 1)
                    nc.vector.tensor_copy(x_t[:, 0, :], lo[:, 0:2, :].rearrange("p a b -> p (a b)")).then_inc(x_lo, 1)
                    dve.wait_ge(q_summed, b + 1)
                    dve.wait_ge(k_split, b + 1)
                    for m in range(KC):
                        last = nc.vector.tensor_scalar(
                            qk_sb[:, 0, m, :], hi[:, 2 * m:2 * m + 2, :].rearrange("p a b -> p (a b)"),
                            bias_qk[:, 0, m:m + 1], temp[:, 3:4], ALU.add, ALU.mult)
                    last.then_inc(q_ready, 1)
                    split = Chain(dve, split_step, 0, 2 * 2 * (PARTS - 1), b)
                    dve.wait_ge(q_ready, b + 1)
                    dve.wait_ge(q_kept, 16 * PARTS * (b + 1))
                    split_in_parts(split, 0, q_split)
                    dve.wait_ge(v_summed, b + 2)
                    dve.wait_ge(v_kept, 16 * b + 16)
                    for n in range(4):
                        last = nc.vector.tensor_tensor(
                            v_sb[:, 2 * n:2 * n + 2, :], hi[:, n, :].rearrange("p (a b) -> p a b", a=2),
                            bv_row[:].unsqueeze(1).broadcast_to([P, 2, D]), ALU.add)
                    last.then_inc(v_ready, 1)
                    dve.wait_ge(k_ready, b + 2)
                    dve.wait_ge(k_kept, 16 * PARTS * (b + 1))
                    split_in_parts(split, 1, k_split)
                    split.close()

            @block.scalar
            def _(act):
                act.sem_inc(k_ready, 1)
                act.sem_inc(q_kept, 16 * PARTS)
                act.sem_inc(k_kept, 16 * PARTS)
                act.sem_inc(v_kept, 16)
                act.wait_ge(b_loaded, 64)
                with act.Fori(0, B, 1) as b:
                    act.wait_ge(x_turned, b + 2)
                    act.wait_ge(v_summed, b + 1)
                    nc.scalar.activation(x_t[:, 1, :], lo[:, 2:4, :].rearrange("p a b -> p (a b)"),
                                         ACT.Copy).then_inc(x_hi, 1)
                    act.wait_ge(k_summed, b + 1)
                    act.wait_ge(k_split, b + 1)
                    for m in range(KC):
                        last = nc.scalar.activation(
                            qk_sb[:, 1, m, :], lo[:, 2 * m:2 * m + 2, :].rearrange("p a b -> p (a b)"),
                            ACT.Identity, bias=bias_qk[:, 1, m:m + 1])
                    last.then_inc(k_ready, 1)
                    act.wait_ge(q_split, b + 1)
                    for i in range(PARTS):
                        act.dma_start(q_d[b, i, :, :].rearrange("(m p) l -> p m l", p=P), parts[:, 0, i, :, :]).then_inc(q_kept, 16)
                    act.wait_ge(v_ready, b + 2)
                    act.dma_start(v_d[b, :, :, :], v_sb[:]).then_inc(v_kept, 16)
                    act.wait_ge(k_split, b + 2)
                    for i in range(PARTS):
                        act.dma_start(k_d[b, i, :, :].rearrange("(m p) l -> p m l", p=P), parts[:, 1, i, :, :]).then_inc(k_kept, 16)
                act.wait_ge(q_kept, 16 * PARTS * (B + 1))
                act.wait_ge(k_kept, 16 * PARTS * (B + 1))
                act.wait_ge(v_kept, 16 * B + 16)


def oscillatory_attention(nc, alpha, phi, q_d, k_d, v_d, o_d):
    U = LT
    with ExitStack() as ctx:
        sb = lambda n, s, d=FP32: ctx.enter_context(nc.sbuf_tensor(n, s, d))
        ps = lambda n, s: ctx.enter_context(nc.psum_tensor(n, s, FP32))
        sem = lambda n: ctx.enter_context(nc.semaphore(n))
        ident = sb("a_ident", [P, P])
        table = sb("a_table", [P, 2, H, NF])
        table_i = sb("a_table_i", [P, H, NF], I32)
        head_c = sb("a_head_c", [P, 2, 2, NF])
        diag = sb("a_diag", [P, 2, max(PE_SINES), P])
        q_r = sb("a_q_r", [P, 2, L], BF16)
        k_r = sb("a_k_r", [P, 2, L], BF16)
        v_r = sb("a_v_r", [P, 2, LT, VP])
        fold = sb("a_fold", [P, 3, VW])
        early = sb("a_early", [P, 2, L], I32)
        score = sb("a_score", [P, 2, L])
        turn = sb("a_turn", [P, RING, NF, L], I32)
        weight = sb("a_weight", [P, 2, LT, L])
        num = sb("a_num", [P, L])
        den = sb("a_den", [P, 2, LT])
        out = sb("a_out", [P, 2, LT, HD])
        ps_score = ps("a_ps_score", [P, L])
        ps_sum = ps("a_ps_sum", [P, 2, L])
        ps_out = ps("a_ps_out", [P, L])

        table_in, table_step, setup, id_zero = sem("table_in"), sem("table_step"), sem("a_setup"), sem("a_id_zero")
        qk_loaded = [sem("qk_loaded0"), sem("qk_loaded1")]
        v_loaded = [sem("v_loaded0"), sem("v_loaded1")]
        const_ready, diag_ready = sem("const_ready"), sem("diag_ready")
        scored, drawn, scaled, wrapped = sem("scored"), sem("drawn"), sem("scaled"), sem("wrapped")
        sines_pe, sines = sem("sines_pe"), sem("sines")
        part_summed, summed, sum_step = sem("part_summed"), sem("summed"), sem("sum_step")
        sigmoids, weighted, num_drawn, turned = sem("sigmoids"), sem("weighted"), sem("num_drawn"), sem("turned")
        norm_step, normed = sem("norm_step"), sem("normed")
        stored = [sem("stored0"), sem("stored1")]

        def heads_of(eng, body):
            for g in range(4):
                body(g, g % 2)
            with eng.Fori(2, HEADS // 2 - 1, 1) as pair:
                for k in range(2):
                    body(2 * pair + k, k)
            for g in range(HEADS - 2, HEADS + 2):
                body(g, g % 2)

        LOADS = 16 * 2 * len(TERMS)
        SUM_STEPS = sum(NF - 1 - p for p in PE_SINES)
        main = lambda g: not isinstance(g, int) or g < HEADS
        weigh = lambda g: not isinstance(g, int) or 1 <= g <= HEADS
        norm = lambda g: not isinstance(g, int) or g >= 2
        unit_in = lambda n: not isinstance(n, int) or n < HEADS * U

        with nc.Block() as block:

            @block.sync
            def _(sp):
                sp.dma_start(table[:, 0, :, :].rearrange("p h f -> p (h f)"),
                             alpha.rearrange("h f -> (h f)").partition_broadcast(P)).then_inc(table_in, 16)
                sp.dma_start(table[:, 1, :, :].rearrange("p h f -> p (h f)"),
                             phi.rearrange("h f -> (h f)").partition_broadcast(P)).then_inc(table_in, 16)

                def load(g, k):
                    wait_pos(sp, scored, (g - 1) * U)
                    for n, term in enumerate(TERMS):
                        for dst, src, part in ((q_r, q_d, term[0]), (k_r, k_d, term[1])):
                            sp.dma_start(dst[HD * n:HD * (n + 1), k, :],
                                         src[g // H, part, bass.ds((g % H) * HD, HD), :]).then_inc(qk_loaded[k], 16)
                    wait_pos(sp, weighted, g - 1)
                    sp.dma_start(v_r[:, k, :, 0:HD], v_d[g // H, :, :, bass.ds((g % H) * HD, HD)]).then_inc(v_loaded[k], 16)

                def store(g, k):
                    sp.wait_ge(normed, g - 1)
                    sp.dma_start(o_d[(g - 2) // H, :, :, bass.ds(((g - 2) % H) * HD, HD)],
                                 out[:, k, :, :]).then_inc(stored[k], 16)

                sp.wait_ge(setup, 2)
                load(0, 0)

                def body(g, k):
                    if not isinstance(g, int) or g + 1 < HEADS:
                        load(g + 1, 1 - k)
                    if norm(g):
                        store(g, k)
                heads_of(sp, body)
                for k in range(2):
                    sp.wait_ge(stored[k], 16 * HEADS // 2)

            @block.gpsimd
            def _(pool):
                nc.gpsimd.memset(ident[:], 0.0).then_inc(id_zero, 1)
                nc.gpsimd.memset(v_r[:].rearrange("p a b c -> p (a b c)"), 0.0).then_inc(id_zero, 1)
                pool.wait_ge(id_zero, 2)
                nc.gpsimd.memset(v_r[:, :, :, HD], 1.0).then_inc(setup, 1)
                nc.gpsimd.affine_select(out=ident[:], in_=ident[:], compare_op=ALU.not_equal, fill=1.0, base=0,
                                        pattern=[[-1, P]], channel_multiplier=1).then_inc(setup, 1)
                pool.wait_ge(setup, 2)
                group = lambda n: ident[:, VP * n:VP * n + VW]
                for n in range(2):
                    nc.gpsimd.tensor_tensor(fold[:, n, :], group(2 * n), group(2 * n + 1), ALU.add).then_inc(setup, 1)
                pool.wait_ge(setup, 4)
                nc.gpsimd.tensor_tensor(fold[:, 2, :], fold[:, 0, :], fold[:, 1, :], ALU.add).then_inc(setup, 1)
                pool.wait_ge(table_step, 3)

                def constants(g, k):
                    wait_pos(pool, summed, (g - 1) * U)
                    h = g % H
                    nc.gpsimd.tensor_copy(head_c[:, k, :, :], table[:, :, bass.ds(h, 1), :].rearrange(
                        "p a h f -> p a (h f)")).then_inc(const_ready, 1)
                    pool.wait_ge(const_ready, g + 1)
                    for f in range(max(PE_SINES)):
                        last = nc.gpsimd.tensor_tensor(diag[:, k, f, :], ident[:],
                                                       head_c[:, k, 0, f:f + 1].broadcast_to([P, P]), ALU.mult)
                    last.then_inc(diag_ready, 1)

                constants(0, 0)

                def body(g, k):
                    if not isinstance(g, int) or g + 1 < HEADS:
                        constants(g + 1, 1 - k)
                heads_of(pool, body)

            @block.tensor
            def _(pe):
                def scores(n, s, k):
                    wait_pos(pe, drawn, n)
                    for half in range(2):
                        last = nc.tensor.matmul(ps_score[:, half * HALF:(half + 1) * HALF], k_r[:, k, s * P:(s + 1) * P],
                                                q_r[:, k, half * HALF:(half + 1) * HALF], start=True, stop=True)
                    last.then_inc(scored, 1)

                def sum_sines(n, s, k):
                    pe.wait_ge(sines_pe, n + 1)
                    wait_pos(pe, summed, n - 1)
                    for half in range(2):
                        for f in range(PE_SINES[s]):
                            last = nc.tensor.matmul(
                                ps_sum[:, s % 2, half * HALF:(half + 1) * HALF], diag[:, k, f, :],
                                turn[:, s % RING, f, half * HALF:(half + 1) * HALF].bitcast(FP32),
                                start=(f == 0), stop=(f == PE_SINES[s] - 1))
                    last.then_inc(part_summed, 1)

                pe.wait_ge(setup, 5)
                pe.wait_ge(qk_loaded[0], LOADS)
                scores(0, 0, 0)
                scores(1, 1, 0)

                def body(g, k):
                    n0 = g * U
                    for s in range(U):
                        n = n0 + s
                        if main(g):
                            if unit_in(n + 2):
                                if s == U - 2:
                                    pe.wait_ge(qk_loaded[1 - k], next_loads(g, k))
                                scores(n + 2, (s + 2) % U, k if s < U - 2 else 1 - k)
                        if s > 0 and main(g):
                            if s == 1:
                                pe.wait_ge(diag_ready, g + 1)
                            sum_sines(n - 1, s - 1, k)
                        if s == 0 and weigh(g):
                            sum_sines(n - 1, U - 1, 1 - k)
                        if s == 1 and norm(g):
                            pe.wait_ge(num_drawn, g - 1)
                            for t in range(LT):
                                last = nc.tensor.matmul(ps_out[:, t * VW:(t + 1) * VW], num[:, t * P:(t + 1) * P],
                                                        fold[:, 2, :], start=True, stop=True)
                            last.then_inc(turned, 1)
                        if s in (U // 2, U // 2 + 2) and weigh(g):
                            if s == U // 2:
                                pe.wait_ge(sigmoids, g)
                                pe.wait_ge(v_loaded[1 - k], v_loads(g, k))
                                wait_pos(pe, normed, g - 1)
                            first = (s - U // 2) * GROUPS // 2
                            for half in range(2):
                                for j in range(first, first + GROUPS):
                                    at = VP * (j % GROUPS)
                                    last = nc.tensor.matmul(
                                        ps_out[at:at + VP, half * HALF:(half + 1) * HALF], v_r[:, 1 - k, j, :],
                                        weight[:, 1 - k, j, half * HALF:(half + 1) * HALF],
                                        start=(j < GROUPS), stop=(j >= GROUPS))
                            if first:
                                last.then_inc(weighted, 1)

                next_loads = lambda g, k: LOADS // 2 * g + (LOADS if k == 0 else LOADS // 2 * 3)
                v_loads = lambda g, k: 8 * g + (0 if k == 0 else 8)
                heads_of(pe, body)

            @block.scalar
            def _(act):
                def draw(n, s, g, k):
                    act.wait_ge(scored, n + 1)
                    wait_pos(act, scaled, n - 1)
                    if ACT_TURNS[s]:
                        if s == 0:
                            act.wait_ge(const_ready, g + 1)
                        wait_pos(act, wrapped, n - 1)
                        nc.scalar.activation(early[:, s % 2, :], ps_score[:], ACT.Identity,
                                             bias=head_c[:, k, 1, NF - 1:NF], scale=TURN / FREQS[NF - 1])
                    nc.scalar.activation(score[:, s % 2, :], ps_score[:], ACT.Copy).then_inc(drawn, 1)

                draw(0, 0, 0, 0)
                draw(1, 1, 0, 0)

                def body(g, k):
                    for s in range(U):
                        n = g * U + s
                        if s == 0 and norm(g):
                            act.wait_ge(weighted, g - 1)
                            wait_pos(act, turned, g - 2)
                            nc.scalar.activation(num[:], ps_out[:], ACT.Copy).then_inc(num_drawn, 1)
                        if main(g):
                            if unit_in(n + 2):
                                if s < U - 2:
                                    draw(n + 2, s + 2, g, k)
                                else:
                                    draw(n + 2, s + 2 - U, g + 1, 1 - k)
                            act.wait_ge(wrapped, n + 1)
                            for lo, hi, done in ((0, PE_SINES[s], sines_pe), (PE_SINES[s], NF, sines)):
                                nc.scalar.activation(
                                    turn[:, s % RING, lo:hi, :].bitcast(FP32), turn[:, s % RING, lo:hi, :],
                                    ACT.Sin, scale=ANGLE).then_inc(done, 1)
                        if s == 3 and weigh(g):
                            act.wait_ge(summed, g * U)
                            nc.scalar.activation(weight[:, 1 - k, :, :], weight[:, 1 - k, :, :],
                                                 ACT.Sigmoid).then_inc(sigmoids, 1)
                heads_of(act, body)

            @block.vector
            def _(dve):
                dve.wait_ge(table_in, 32)
                nc.vector.tensor_scalar(table_i[:], table[:, 1, :, :], TURN / TWO_PI, None, ALU.mult).then_inc(table_step, 1)
                dve.wait_ge(table_step, 1)
                nc.vector.tensor_scalar(table_i[:], table_i[:], WRAP, WRAP, ALU.logical_shift_left,
                                        ALU.arith_shift_right).then_inc(table_step, 1)
                dve.wait_ge(table_step, 2)
                nc.vector.tensor_copy(table[:, 1, :, :], table_i[:]).then_inc(table_step, 1)

                def wrap(n, s, g, k):
                    if s == 0:
                        dve.wait_ge(const_ready, g + 1)
                    dve.wait_ge(drawn, n + 1)
                    wait_pos(dve, summed, n - RING + 1)
                    scaled_here = NF - ACT_TURNS[s]
                    for f in range(scaled_here):
                        last = nc.vector.tensor_scalar(turn[:, s % RING, f, :], score[:, s % 2, :],
                                                       TURN / FREQS[f], head_c[:, k, 1, f:f + 1], ALU.mult, ALU.add)
                    last.then_inc(scaled, 1)
                    dve.wait_ge(scaled, n + 1)
                    shifts = ALU.logical_shift_left, ALU.arith_shift_right
                    last = nc.vector.tensor_scalar(turn[:, s % RING, 0:scaled_here, :], turn[:, s % RING, 0:scaled_here, :],
                                                   WRAP, WRAP, *shifts)
                    if ACT_TURNS[s]:
                        last = nc.vector.tensor_scalar(turn[:, s % RING, NF - 1, :], early[:, s % 2, :], WRAP, WRAP, *shifts)
                    last.then_inc(wrapped, 1)

                def finish(n, s, g, k):
                    dve.wait_ge(part_summed, n + 1)
                    dve.wait_ge(sines, n + 1)
                    if s == 0:
                        wait_pos(dve, weighted, g - 1)
                    first = PE_SINES[s]
                    for f in range(first, NF):
                        ins = nc.vector.scalar_tensor_tensor(
                            weight[:, k, s, :], turn[:, s % RING, f, :].bitcast(FP32), head_c[:, k, 0, f:f + 1],
                            ps_sum[:, s % 2, :] if f == first else weight[:, k, s, :], ALU.mult, ALU.add)
                        if f < NF - 1:
                            ins.then_inc(sum_step, 1)
                            before = sum(NF - 1 - p for p in PE_SINES[:s])
                            dve.wait_ge(sum_step, g * SUM_STEPS + before + f - first + 1)
                        else:
                            ins.then_inc(summed, 1)

                wrap(0, 0, 0, 0)

                def body(g, k):
                    for s in range(U):
                        n = g * U + s
                        if main(g) and unit_in(n + 1):
                            if s < U - 1:
                                wrap(n + 1, s + 1, g, k)
                            else:
                                wrap(n + 1, 0, g + 1, 1 - k)
                        if s > 1 and main(g):
                            finish(n - 2, s - 2, g, k)
                        if s < 2 and weigh(g):
                            finish(n - 2, U - 2 + s, g - 1, 1 - k)
                        if s == 2 and norm(g):
                            dve.wait_ge(turned, g - 1)
                            wait_pos(dve, stored[k], 8 * (g - k) - 16)
                            rows = ps_out[:, 0:LT * VW].rearrange("p (t c) -> p t c", c=VW)
                            nc.vector.tensor_scalar(den[:, 0, :], rows[:, :, HD], EPS_DEN, None, ALU.add).then_inc(norm_step, 1)
                            dve.wait_ge(norm_step, 2 * (g - 2) + 1)
                            nc.vector.reciprocal(den[:, 1, :], den[:, 0, :]).then_inc(norm_step, 1)
                            dve.wait_ge(norm_step, 2 * (g - 2) + 2)
                            nc.vector.tensor_tensor(out[:, k, :, :], rows[:, :, 0:HD],
                                                    den[:, 1, :].unsqueeze(2).broadcast_to([P, LT, HD]),
                                                    ALU.mult).then_inc(normed, 1)
                dve.wait_ge(table_step, 3)
                heads_of(dve, body)


def routed_block(nc, x, o_d, wo_a, bo, gamma, beta, mask, positions, router_w, router_b, wq, wk, wv, wo, w1, w2,
                 ln1, ln2, y_out):
    QH = 4
    C1 = 6.28125
    C2 = TWO_PI - C1
    ROUND = 1.5 * 2.0 ** 23
    PI_IN = float(np.nextafter(np.float32(np.pi), np.float32(0)))
    with ExitStack() as ctx:
        sb = lambda n, s, d=FP32: ctx.enter_context(nc.sbuf_tensor(n, s, d))
        sem = lambda n: ctx.enter_context(nc.semaphore(n))
        ident, tri, last_row = sb("ident", [P, P]), sb("tri", [P, P]), sb("last_row", [P, P])
        ones = sb("ones", [P, P])
        slot_i, slot = sb("slot_i", [P, P], I32), sb("slot", [P, P])
        tok_i, base_i = sb("tok_i", [P, LT], I32), sb("base_i", [P, B], I32)
        base = sb("base", [P, 2, B])
        pos_i, pos_f = sb("pos_i", [MB * LT, P], I32), sb("pos_f", [MB * LT, P])
        pos = sb("pos", [P, B, LT])
        inv_freq = sb("inv_freq", [P, NROT])
        rows = sb("rows", [P, 6, D])
        r_bias = sb("r_bias", [P, 1])
        woa_in, woa_t = sb("woa_in", [P, KC, D]), sb("woa_t", [P, KC, D])
        wqkv, wo_sb = sb("wqkv", [P, KC, 3 * D]), sb("wo_sb", [P, KC, D])
        w1_sb, w2_sb = sb("w1_sb", [P, KC, F]), sb("w2_sb", [P, FB, D])
        o_in, x_in = sb("o_in", [P, LT, D]), sb("x_in", [P, LT, D])
        o_t = sb("o_t", [P, KC, L])
        mix = sb("mix", [P, LT, D])
        x1 = sb("x1", [P, LT, D])
        dense = sb("dense", [P, LT, D])
        stats, moments = sb("stats", [P, 3, LT, 6]), sb("moments", [P, 3, LT, 2])
        spread = sb("spread", [P, 3, LT])
        dump = sb("dump", [P, L])
        w_col, w_diag, w_row = sb("w_col", [P, 2, LT]), sb("w_diag", [P, LT, P]), sb("w_row", [P, L])
        ahead, rank = sb("ahead", [P, LT, 3]), sb("rank", [P, LT])
        one_hot = sb("one_hot", [P, LT, P])
        ext = sb("ext", [P, LT, 3])
        xs, ext_s = sb("xs", [P, D]), sb("ext_s", [P, 3])
        where = sb("where", [P, 2], mybir.dt.uint32)
        m_row, m_t, m_sel = sb("m_row", [P, L]), sb("m_t", [P, LT, P]), sb("m_sel", [P, P])
        small = sb("small", [P, 16])
        hn, hn_t = sb("hn", [P, D]), sb("hn_t", [P, KC, P])
        qk, v_sb = sb("qk", [P, 2 * H, HD]), sb("v_sb", [P, D])
        ang, ang_r, trig = sb("ang", [P, 4, NROT]), sb("ang_r", [P, 2, NROT]), sb("trig", [P, 2, NROT])
        rot_a, rot_b = sb("rot_a", [P, 2 * H, HD]), sb("rot_b", [P, 2 * H, HD])
        qk_pad = sb("qk_pad", [P, 2 * H, 32])
        qk_t = sb("qk_t", [P, 2 * QH, P])
        logits, probs_t = sb("logits", [P, H, P]), sb("probs_t", [P, H, P])
        peak, total, inv_total = sb("peak", [P, H]), sb("total", [P, H]), sb("inv_total", [P, H])
        att, att_t = sb("att", [P, D]), sb("att_t", [P, KC, P])
        xa, h2, h2_t, g_t = sb("xa", [P, D]), sb("h2", [P, D]), sb("h2_t", [P, KC, P]), sb("g_t", [P, FB, P])
        xm, ys, res = sb("xm", [P, D]), sb("ys", [P, D]), sb("res", [P, D])
        A = ctx.enter_context(nc.psum_tensor("A", [P, 4, HALF], FP32))
        Bk = ctx.enter_context(nc.psum_tensor("Bk", [P, 4, HALF], FP32))

        names = ("in_loaded o_turned ot_lo ot_hi projected var1 dev1 var2 dev2 diag_w w_spread w_drawn "
                 "hot gathered token_ready ms1 dev3 dense_var dense_dev dense_ready normed1 hn_turned hn_drawn "
                 "qkv qk_drawn angles trig_ready padded qk_turned qk_t_drawn mask_rows m_turned m_drawn "
                 "m_picked m_sel_drawn scored shifted exped p_turned p_lo p_hi attended att_ready att_turned "
                 "att_drawn mixed ms2 dev4 normed2 h2_turned h2_drawn up gelu_ready down var5 dev5 "
                 "res_ready dense_stored scattered thr_ready xb_ready").split()
        S = {n: sem("r_" + n) for n in names}
        const_in, const_set, pool_step, setup_pe = sem("const_in"), sem("const_set"), sem("pool_step"), sem("setup_pe")
        setup_dve, dve_step = sem("setup_dve"), sem("dve_step")
        gate_s, gated = sb("gate_s", [P, 2]), sem("gated")
        flat = lambda ap: ap.rearrange("p a b -> p (a b)")

        with nc.Block() as block:

            @block.sync
            def _(sp):
                load = lambda dst, src: sp.dma_start(dst, src).then_inc(const_in, 16)
                load(woa_in[:], wo_a.rearrange("(m p) i -> p m i", p=P))
                for n, v in enumerate((bo, gamma, beta, router_w.rearrange("d o -> (d o)"), ln1, ln2)):
                    load(rows[:, n, :], v.partition_broadcast(P))
                load(r_bias[:], router_b.partition_broadcast(P))
                load(pos_i[:], positions.rearrange("b (t p) -> (b t) p", p=P))
                for n, w in enumerate((wq, wk, wv)):
                    load(wqkv[:, :, n * D:(n + 1) * D], w.rearrange("(c p) n -> p c n", p=P))
                load(wo_sb[:], wo.rearrange("(c p) n -> p c n", p=P))
                load(w1_sb[:], w1.rearrange("(c p) n -> p c n", p=P))
                load(w2_sb[:], w2.rearrange("(c p) n -> p c n", p=P))
                with sp.Fori(0, B, 1) as b:
                    sp.wait_ge(gated, 3 * b + 1)
                    sp.dma_start(o_in[:], o_d[b, :, :, :]).then_inc(S["in_loaded"], 16)
                    sp.dma_start(x_in[:], x[b, :, :].rearrange("(t p) d -> p t d", p=P)).then_inc(S["in_loaded"], 16)
                    sp.wait_ge(S["dense_ready"], b + 1)
                    sp.dma_start(y_out[b, :, :].rearrange("(t p) d -> p t d", p=P), dense[:]).then_inc(S["dense_stored"], 16)
                sp.wait_ge(S["dense_stored"], 16 * B)

            @block.gpsimd
            def _(pool):
                nc.gpsimd.memset(ident[:], 0.0).then_inc(pool_step, 1)
                nc.gpsimd.memset(tri[:], 1.0).then_inc(pool_step, 1)
                nc.gpsimd.memset(last_row[:], 0.0).then_inc(pool_step, 1)
                nc.gpsimd.memset(ones[:], 1.0)
                nc.gpsimd.memset(gate_s[:], 1.0)
                pool.sem_inc(gated, 1)
                nc.gpsimd.memset(flat(qk_pad[:]), 0.0)
                for n in range(NROT):
                    nc.gpsimd.memset(inv_freq[:, n:n + 1], float(np.float32(1.0) / np.float32(ROPE_BASE) ** np.float32(2 * n / HD)))
                nc.gpsimd.iota(slot_i[:], pattern=[[1, P]], base=0, channel_multiplier=0)
                nc.gpsimd.iota(tok_i[:], pattern=[[P, LT]], base=0, channel_multiplier=1)
                nc.gpsimd.iota(base_i[:], pattern=[[L, B]], base=0, channel_multiplier=0).then_inc(pool_step, 1)
                pool.wait_ge(pool_step, 4)
                nc.gpsimd.affine_select(out=ident[:], in_=ident[:], compare_op=ALU.not_equal, fill=1.0, base=0,
                                        pattern=[[-1, P]], channel_multiplier=1)
                nc.gpsimd.affine_select(out=tri[:], in_=tri[:], compare_op=ALU.is_gt, fill=0.0, base=0,
                                        pattern=[[-1, P]], channel_multiplier=1)
                nc.gpsimd.affine_select(out=last_row[:], in_=last_row[:], compare_op=ALU.not_equal, fill=1.0,
                                        base=-KSEL, pattern=[[0, P]], channel_multiplier=1).then_inc(const_set, 1)
                pool.wait_ge(const_in, 16 * CONST_LOADS)

                def gate(n):
                    pool.wait_ge(gated, n + 1)
                    nc.gpsimd.tensor_tensor(gate_s[:, 1:2], gate_s[:, 0:1], gate_s[:, 0:1], ALU.mult).then_inc(gated, 1)

                with pool.Fori(0, B, 1) as b:
                    pool.wait_ge(S["in_loaded"], 32 * b + 32)
                    nc.gpsimd.tensor_tensor(x_in[:], x_in[:], rows[:, 2, :].unsqueeze(1).broadcast_to([P, LT, D]),
                                            ALU.add).then_inc(S["xb_ready"], 1)
                    pool.wait_ge(S["token_ready"], b + 1)
                    gate(3 * b)
                    pool.indirect_dma_start(
                        out=m_row[:], out_offset=None, in_=mask.rearrange("b o q k -> (b o q) k"),
                        in_offset=bass.IndirectOffsetOnAxis(ap=where[:, 1:2], axis=0)).then_inc(S["mask_rows"], 16)
                    pool.wait_ge(S["res_ready"], b + 1)
                    pool.wait_ge(S["dense_stored"], 16 * b + 16)
                    gate(3 * b + 1)
                    pool.indirect_dma_start(
                        out=y_out.rearrange("b l d -> (b l) d"),
                        out_offset=bass.IndirectOffsetOnAxis(ap=where[0:KSEL, 0:1], axis=0),
                        in_=res[0:KSEL, :], in_offset=None).then_inc(S["scattered"], 16)
                    pool.wait_ge(S["scattered"], 16 * b + 16)
                    gate(3 * b + 2)

            @block.tensor
            def _(pe):
                mm, tr = nc.tensor.matmul, nc.tensor.transpose
                pe.wait_ge(const_set, 1)
                pe.wait_ge(const_in, 16 * CONST_LOADS)
                for i in range(KC):
                    for m in range(KC):
                        tr(A[:, 0, i * D + m * P:i * D + (m + 1) * P], woa_in[:, m, i * P:(i + 1) * P], ident[:])
                pe.wait_ge(setup_dve, 1)
                tr(A[:, 1, 0:MB * LT], pos_f[:], ident[0:MB * LT, 0:MB * LT]).then_inc(setup_pe, 1)
                pe.wait_ge(setup_dve, 2)

                def turn_two(out, src, done):
                    for c in range(KC):
                        ins = tr(out[:, c * P:(c + 1) * P], src[:, c * P:(c + 1) * P], ident[:])
                    ins.then_inc(S[done], 1)

                with pe.Fori(0, B, 1) as b:
                    ready = lambda *names: [pe.wait_ge(S[n], b + 1) for n in names]
                    pe.wait_ge(S["in_loaded"], 32 * b + 32)
                    for c in range(KC):
                        for t in range(LT):
                            ins = tr(A[:, 2 * c + t // 4, (t % 4) * P:(t % 4 + 1) * P], o_in[:, t, c * P:(c + 1) * P], ident[:])
                    ins.then_inc(S["o_turned"], 1)
                    ready("ot_lo", "ot_hi")
                    for t in range(LT):
                        for c in range(KC):
                            ins = mm(Bk[:, t // 2, (t % 2) * D:(t % 2 + 1) * D], o_t[:, c, t * P:(t + 1) * P],
                                     woa_t[:, c, :], start=(c == 0), stop=(c == KC - 1))
                    ins.then_inc(S["projected"], 1)
                    ready("diag_w")
                    for t in range(LT):
                        ins = mm(A[:, t // 4, (t % 4) * P:(t % 4 + 1) * P], ones[:], w_diag[:, t, :], start=True, stop=True)
                    ins.then_inc(S["w_spread"], 1)
                    ready("hot")
                    for t in range(LT):
                        mm(A[:, 2, 0:D], one_hot[:, t, :], x1[:, t, :], start=(t == 0), stop=(t == LT - 1))
                    for t in range(LT):
                        ins = mm(A[:, 3, 0:3], one_hot[:, t, :], ext[:, t, :], start=(t == 0), stop=(t == LT - 1))
                    ins.then_inc(S["gathered"], 1)
                    ready("token_ready")
                    mm(Bk[:, 3, 0:1], last_row[:], ext_s[:, 0:1], start=True, stop=True).then_inc(S["thr_ready"], 1)
                    ready("normed1")
                    turn_two(Bk[:, 0, :], hn, "hn_turned")
                    ready("hn_drawn")
                    for c in range(KC):
                        mm(Bk[:, 1, :], hn_t[:, c, :], wqkv[:, c, 0:2 * D], start=(c == 0), stop=(c == KC - 1))
                    for c in range(KC):
                        ins = mm(Bk[:, 2, 0:D], hn_t[:, c, :], wqkv[:, c, 2 * D:3 * D], start=(c == 0), stop=(c == KC - 1))
                    ins.then_inc(S["qkv"], 1)
                    pe.wait_ge(S["mask_rows"], 16 * b + 16)
                    for t in range(LT):
                        ins = tr(A[:, t // 4, (t % 4) * P:(t % 4 + 1) * P], m_row[:, t * P:(t + 1) * P], ident[:])
                    ins.then_inc(S["m_turned"], 1)
                    ready("m_drawn")
                    for t in range(LT):
                        ins = mm(Bk[:, 0, 0:P], m_t[:, t, :], one_hot[:, t, :], start=(t == 0), stop=(t == LT - 1))
                    ins.then_inc(S["m_picked"], 1)
                    ready("padded")
                    for n in range(2 * QH):
                        ins = tr(A[:, 2 + n // 4, (n % 4) * P:(n % 4 + 1) * P],
                                 qk_pad[:, n * QH:(n + 1) * QH, :].rearrange("p a b -> p (a b)"), ident[:])
                    ins.then_inc(S["qk_turned"], 1)
                    ready("qk_t_drawn")
                    for n in range(QH):
                        for r in range(QH):
                            rows_r = slice(32 * r, 32 * r + HD)
                            ins = mm(A[:, r, n * P:(n + 1) * P], qk_t[rows_r, n, :], qk_t[rows_r, QH + n, :], start=True, stop=True)
                    ins.then_inc(S["scored"], 1)
                    ready("exped")
                    for n in range(H):
                        ins = tr(Bk[0:KSEL, n // 4, (n % 4) * P:(n % 4 + 1) * P], logits[:, n, 0:KSEL], ident[:])
                    ins.then_inc(S["p_turned"], 1)
                    ready("p_lo", "p_hi")
                    for n in range(H):
                        h = 4 * (n % 4) + n // 4
                        ins = mm(A[:, 0, h * HD:(h + 1) * HD], probs_t[0:KSEL, n, :], v_sb[0:KSEL, h * HD:(h + 1) * HD],
                                 start=True, stop=True)
                    ins.then_inc(S["attended"], 1)
                    ready("att_ready")
                    turn_two(A[:, 1, :], att, "att_turned")
                    ready("att_drawn")
                    for c in range(KC):
                        ins = mm(A[:, 2, 0:D], att_t[:, c, :], wo_sb[:, c, :], start=(c == 0), stop=(c == KC - 1))
                    ins.then_inc(S["mixed"], 1)
                    ready("normed2")
                    turn_two(A[:, 3, :], h2, "h2_turned")
                    ready("h2_drawn")
                    for n in range(FB):
                        for c in range(KC):
                            ins = mm(Bk[:, n // 4, (n % 4) * P:(n % 4 + 1) * P], w1_sb[:, c, n * P:(n + 1) * P],
                                     h2_t[:, c, :], start=(c == 0), stop=(c == KC - 1))
                    ins.then_inc(S["up"], 1)
                    ready("gelu_ready")
                    for n in range(FB):
                        ins = mm(Bk[:, 2, 0:D], g_t[:, n, :], w2_sb[:, n, :], start=(n == 0), stop=(n == FB - 1))
                    ins.then_inc(S["down"], 1)

            @block.scalar
            def _(act):
                with act.Fori(0, B, 1) as b:
                    ready = lambda *names: [act.wait_ge(S[n], b + 1) for n in names]
                    run = lambda out, src, fn, done: nc.scalar.activation(out, src, fn).then_inc(S[done], 1)
                    ready("o_turned")
                    run(o_t[:, 1, :], flat(A[:, 2:4, :]), ACT.Copy, "ot_hi")
                    ready("var1")
                    run(spread[:, 0, :], spread[:, 0, :], ACT.Sqrt, "dev1")
                    ready("var2")
                    run(spread[:, 1, :], spread[:, 1, :], ACT.Sqrt, "dev2")
                    ready("w_spread")
                    run(w_row[:], flat(A[:, 0:2, :]), ACT.Copy, "w_drawn")
                    ready("ms1")
                    run(small[:, 1:2], small[:, 0:1], ACT.Sqrt, "dev3")
                    ready("dense_var")
                    run(spread[:, 2, :], spread[:, 2, :], ACT.Sqrt, "dense_dev")
                    ready("hn_turned")
                    run(flat(hn_t[:]), Bk[:, 0, 0:D], ACT.Copy, "hn_drawn")
                    ready("qkv")
                    nc.scalar.activation(flat(qk[:]), Bk[:, 1, :], ACT.Copy)
                    run(v_sb[:], Bk[:, 2, 0:D], ACT.Copy, "qk_drawn")
                    ready("angles")
                    run(trig[:], ang_r[:], ACT.Sin, "trig_ready")
                    ready("m_turned")
                    run(flat(m_t[:]), flat(A[:, 0:2, :]), ACT.Copy, "m_drawn")
                    ready("m_picked")
                    run(m_sel[:], Bk[:, 0, 0:P], ACT.Copy, "m_sel_drawn")
                    ready("qk_turned")
                    run(flat(qk_t[:]), flat(A[:, 2:4, :]), ACT.Copy, "qk_t_drawn")
                    ready("shifted")
                    run(logits[:, :, 0:KSEL], logits[:, :, 0:KSEL], ACT.Exp, "exped")
                    ready("p_turned")
                    run(probs_t[0:KSEL, 8:16, :].rearrange("p a b -> p (a b)"), flat(Bk[0:KSEL, 2:4, :]), ACT.Copy, "p_hi")
                    ready("att_turned")
                    run(flat(att_t[:]), A[:, 1, 0:D], ACT.Copy, "att_drawn")
                    ready("ms2")
                    run(small[:, 4:5], small[:, 3:4], ACT.Sqrt, "dev4")
                    ready("h2_turned")
                    run(flat(h2_t[:]), A[:, 3, 0:D], ACT.Copy, "h2_drawn")
                    ready("up")
                    run(flat(g_t[:]), flat(Bk[:, 0:2, :]), ACT.Gelu_apprx_tanh, "gelu_ready")
                    ready("var5")
                    run(small[:, 7:8], small[:, 6:7], ACT.Sqrt, "dev5")

            @block.vector
            def _(dve):
                v = nc.vector
                setup = Chain(dve, sem("dve_setup"), 0, 0, 0)
                dve.wait_ge(const_set, 1)
                dve.wait_ge(const_in, 16 * CONST_LOADS)
                v.tensor_copy(slot[:], slot_i[:])
                v.tensor_copy(ext[:, :, 1], tok_i[:])
                setup.step(v.tensor_copy(base[:, 0, :], base_i[:]))
                v.tensor_scalar(base[:, 1, :], base[:, 0, :], float((MB - 1) * L), None, ALU.min)
                v.tensor_copy(pos_f[:], pos_i[:]).then_inc(setup_dve, 1)
                dve.wait_ge(setup_pe, 1)
                v.tensor_copy(flat(woa_t[:]), A[:, 0, :])
                for n in range(0, B, MB):
                    src = A[:, 1, 0:MB * LT].rearrange("p (b t) -> p b t", b=MB)
                    if n == 0:
                        setup.step(v.tensor_copy(pos[:, 0:MB, :], src))
                    else:
                        setup.step(v.tensor_copy(pos[:, n:n + MB, :], src[:, MB - 1:MB, :].broadcast_to([P, MB, LT])))
                v.tensor_copy(slot[:, 0:1], slot_i[:, 0:1]).then_inc(setup_dve, 1)
                dve.wait_ge(setup_dve, 2)

                with dve.Fori(0, B, 1) as b:
                    ready = lambda *names: [dve.wait_ge(S[n], b + 1) for n in names]
                    chain = Chain(dve, dve_step, 0, DVE_STEPS, b)
                    step = chain.step

                    def moments_of(src, n, name, eps, tiles=LT):
                        for t in range(tiles):
                            ins = v.bn_stats(stats[:, n, t, :], src[:, t, :])
                        step(ins)
                        v.memset(spread[:, n, :], 0.0)
                        for t in range(tiles):
                            ins = v.bn_aggr(moments[:, n, t, :], stats[:, n, t, :])
                        step(ins)
                        v.tensor_scalar(spread[:, n, :], moments[:, n, :, 1], eps, None, ALU.add).then_inc(S[name], 1)

                    ready("o_turned")
                    v.tensor_copy(o_t[:, 0, :], flat(A[:, 0:2, :])).then_inc(S["ot_lo"], 1)
                    ready("projected")
                    for n in range(4):
                        ins = v.tensor_tensor(mix[:, 2 * n:2 * n + 2, :], Bk[:, n, :].rearrange("p (a b) -> p a b", a=2),
                                              rows[:, 0, :].unsqueeze(1).broadcast_to([P, 2, D]), ALU.add)
                    step(ins)
                    moments_of(mix, 0, "var1", EPS_LN)
                    for t in range(LT):
                        ins = v.scalar_tensor_tensor(mix[:, t, :], mix[:, t, :], moments[:, 0, t, 0:1], rows[:, 1, :],
                                                     ALU.subtract, ALU.mult)
                    step(ins)
                    ready("dev1")
                    step(v.reciprocal(spread[:, 0, :], spread[:, 0, :]))
                    ready("xb_ready")
                    for t in range(LT):
                        ins = v.scalar_tensor_tensor(mix[:, t, :], mix[:, t, :], spread[:, 0, t:t + 1], x_in[:, t, :],
                                                     ALU.mult, ALU.add)
                    step(ins)
                    moments_of(mix, 1, "var2", EPS_LN)
                    ready("dev2")
                    step(v.reciprocal(spread[:, 1, :], spread[:, 1, :]))
                    for t in range(LT):
                        ins = v.tensor_scalar(x1[:, t, :], mix[:, t, :], moments[:, 1, t, 0:1], spread[:, 1, t:t + 1],
                                              ALU.subtract, ALU.mult)
                    step(ins)
                    for t in range(LT):
                        ins = v.tensor_tensor_reduce(out=dump[:, 0:D] if t == 0 else dump[:, 0:D], in0=x1[:, t, :],
                                                     in1=rows[:, 3, :], scale=1.0, scalar=0.0, op0=ALU.mult, op1=ALU.add,
                                                     accum_out=w_col[:, 0, t:t + 1])
                        step(ins)
                    step(v.tensor_scalar(w_col[:, 1, :], w_col[:, 0, :], r_bias[:, 0:1], None, ALU.add))
                    v.tensor_copy(ext[:, :, 0], w_col[:, 1, :])
                    v.tensor_copy(ext[:, :, 2], pos[:, bass.ds(b, 1), :].rearrange("p a t -> p (a t)"))
                    for t in range(LT):
                        ins = v.tensor_scalar(w_diag[:, t, :], ident[:], w_col[:, 1, t:t + 1], None, ALU.mult)
                    ins.then_inc(S["diag_w"], 1)
                    ready("w_drawn")
                    step(v.memset(ahead[:, 0, 0:1], 0.0))
                    for t in range(LT):
                        mine = w_col[:, 1, t:t + 1]
                        if t:
                            step(v.tensor_scalar(dump[:, 0:t * P], w_row[:, 0:t * P], mine, None, ALU.is_ge, ALU.add,
                                                 accum_out=ahead[:, t, 0:1]))
                        step(v.tensor_scalar(dump[:, t * P:L], w_row[:, t * P:L], mine, None, ALU.is_gt, ALU.add,
                                             accum_out=ahead[:, t, 1:2]))
                        step(v.scalar_tensor_tensor(dump[:, 0:P], w_row[:, t * P:(t + 1) * P], mine, tri[:],
                                                    ALU.is_equal, ALU.mult, accum_out=ahead[:, t, 2:3]))
                    step(v.tensor_reduce(rank[:], ahead[:], AX.X, ALU.add))
                    for t in range(LT):
                        ins = v.tensor_scalar(one_hot[:, t, :], slot[:], rank[:, t:t + 1], None, ALU.is_equal)
                    ins.then_inc(S["hot"], 1)
                    moments_of(x1, 2, "dense_var", EPS_LN / 4)
                    ready("gathered")
                    step(v.tensor_copy(ext_s[:], A[:, 3, 0:3]))
                    v.tensor_scalar(where[:, 0:1], ext_s[:, 1:2], base[:, 0, bass.ds(b, 1)], None, ALU.add)
                    v.tensor_scalar(where[:, 1:2], ext_s[:, 1:2], base[:, 1, bass.ds(b, 1)], None, ALU.add).then_inc(S["token_ready"], 1)
                    step(v.tensor_copy(xs[:], A[:, 2, 0:D]))
                    step(v.tensor_tensor_reduce(out=dump[:, 0:D], in0=xs[:], in1=xs[:], scale=1.0 / D, scalar=0.0,
                                                op0=ALU.mult, op1=ALU.add, accum_out=small[:, 2:3]))
                    v.tensor_scalar(small[:, 0:1], small[:, 2:3], EPS_RMS, None, ALU.add).then_inc(S["ms1"], 1)
                    ready("dev3")
                    step(v.reciprocal(small[:, 5:6], small[:, 1:2]))
                    v.scalar_tensor_tensor(hn[:], xs[:], small[:, 5:6], rows[:, 4, :], ALU.mult, ALU.mult).then_inc(S["normed1"], 1)
                    ready("dense_dev")
                    step(v.reciprocal(spread[:, 2, :], spread[:, 2, :]))
                    for t in range(LT):
                        ins = v.tensor_scalar(dense[:, t, :], x1[:, t, :], moments[:, 2, t, 0:1], spread[:, 2, t:t + 1],
                                              ALU.subtract, ALU.mult)
                    ins.then_inc(S["dense_ready"], 1)
                    step(v.tensor_scalar(ang[:, 0, :], inv_freq[:], ext_s[:, 2:3], None, ALU.mult))
                    step(v.tensor_scalar(ang[:, 1, :], ang[:, 0, :], 1.0 / TWO_PI, ROUND, ALU.mult, ALU.add))
                    step(v.tensor_scalar(ang[:, 2, :], ang[:, 1, :], ROUND, None, ALU.subtract))
                    step(v.scalar_tensor_tensor(ang[:, 3, :], ang[:, 2, :], -C1, ang[:, 0, :], ALU.mult, ALU.add))
                    step(v.scalar_tensor_tensor(ang[:, 1, :], ang[:, 2, :], -C2, ang[:, 3, :], ALU.mult, ALU.add))
                    step(v.tensor_scalar(ang_r[:, 0, :], ang[:, 1, :], PI_IN, -PI_IN, ALU.min, ALU.max))
                    step(v.scalar_tensor_tensor(ang[:, 2, :], ang_r[:, 0, :], -1.0, ang_r[:, 0, :], ALU.mult, ALU.max))
                    v.tensor_scalar(ang_r[:, 1, :], ang[:, 2, :], -1.0, float(np.pi / 2), ALU.mult, ALU.add).then_inc(S["angles"], 1)
                    ready("qk_drawn", "trig_ready")
                    halves = lambda t: t[:].rearrange("p h (s f) -> p h s f", s=2)
                    cos, sin = (trig[:, n, :].unsqueeze(1).broadcast_to([P, 2 * H, NROT]) for n in (1, 0))
                    q2, a2, b2 = halves(qk), halves(rot_a), halves(rot_b)
                    for s in range(2):
                        v.tensor_tensor(a2[:, :, s, :], q2[:, :, s, :], cos, ALU.mult)
                        ins = v.tensor_tensor(b2[:, :, s, :], q2[:, :, 1 - s, :], sin, ALU.mult)
                    step(ins)
                    v.tensor_tensor(qk_pad[:, :, 0:NROT], a2[:, :, 0, :], b2[:, :, 0, :], ALU.subtract)
                    v.tensor_tensor(qk_pad[:, :, NROT:HD], a2[:, :, 1, :], b2[:, :, 1, :], ALU.add).then_inc(S["padded"], 1)
                    ready("thr_ready")
                    step(v.tensor_scalar(small[:, 8:9], ext_s[:, 0:1], Bk[:, 3, 0:1], -1.0, ALU.is_gt, ALU.mult))
                    step(v.tensor_scalar(small[:, 9:10], small[:, 8:9], 2.0, None, ALU.add))
                    ready("scored", "m_sel_drawn")
                    for r in range(QH):
                        ins = v.scalar_tensor_tensor(logits[:, 4 * r:4 * r + 4, :], A[:, r, :].rearrange("p (a b) -> p a b", a=4),
                                                     1.0 / float(np.sqrt(HD)), m_sel[:].unsqueeze(1).broadcast_to([P, 4, P]),
                                                     ALU.mult, ALU.add)
                    step(ins)
                    step(v.tensor_reduce(peak[:], logits[:, :, 0:KSEL], AX.X, ALU.max))
                    v.tensor_tensor(logits[:, :, 0:KSEL], logits[:, :, 0:KSEL], peak[:].unsqueeze(2).broadcast_to([P, H, KSEL]),
                                    ALU.subtract).then_inc(S["shifted"], 1)
                    ready("exped")
                    step(v.tensor_reduce(total[:], logits[:, :, 0:KSEL], AX.X, ALU.add))
                    step(v.reciprocal(inv_total[:].rearrange("p (n r) -> p r n", r=QH), total[:].rearrange("p (r n) -> p r n", r=QH)))
                    ready("p_turned")
                    v.tensor_copy(probs_t[0:KSEL, 0:8, :].rearrange("p a b -> p (a b)"), flat(Bk[0:KSEL, 0:2, :])).then_inc(S["p_lo"], 1)
                    ready("attended")
                    v.tensor_tensor(att[:].rearrange("p (h d) -> p h d", d=HD), A[:, 0, 0:D].rearrange("p (h d) -> p h d", d=HD),
                                    inv_total[:].unsqueeze(2).broadcast_to([P, H, HD]), ALU.mult).then_inc(S["att_ready"], 1)
                    ready("mixed")
                    step(v.tensor_tensor(xa[:], A[:, 2, 0:D], xs[:], ALU.add))
                    step(v.tensor_tensor_reduce(out=dump[:, 0:D], in0=xa[:], in1=xa[:], scale=1.0 / D, scalar=0.0,
                                                op0=ALU.mult, op1=ALU.add, accum_out=small[:, 10:11]))
                    v.tensor_scalar(small[:, 3:4], small[:, 10:11], EPS_RMS, None, ALU.add).then_inc(S["ms2"], 1)
                    ready("dev4")
                    step(v.reciprocal(small[:, 11:12], small[:, 4:5]))
                    v.scalar_tensor_tensor(h2[:], xa[:], small[:, 11:12], rows[:, 5, :], ALU.mult, ALU.mult).then_inc(S["normed2"], 1)
                    ready("down")
                    step(v.tensor_tensor(xm[:], Bk[:, 2, 0:D], xa[:], ALU.add))
                    step(v.tensor_scalar(xm[:], xm[:], ext_s[:, 0:1], None, ALU.mult))
                    step(v.scalar_tensor_tensor(ys[:], xs[:], small[:, 9:10], xm[:], ALU.mult, ALU.add))
                    step(v.bn_stats(stats[:, 0, 0, :], ys[:]))
                    v.memset(small[:, 6:7], 0.0)
                    step(v.bn_aggr(moments[:, 0, 0, :], stats[:, 0, 0, :]))
                    v.tensor_scalar(small[:, 6:7], moments[:, 0, 0, 1:2], EPS_LN, None, ALU.add).then_inc(S["var5"], 1)
                    ready("dev5")
                    step(v.reciprocal(small[:, 12:13], small[:, 7:8]))
                    v.tensor_scalar(res[:], ys[:], moments[:, 0, 0, 0:1], small[:, 12:13], ALU.subtract, ALU.mult).then_inc(S["res_ready"], 1)
                    chain.close()


DVE_STEPS = 74
CONST_LOADS = 15

_INS = [f"L0_attn_{n}" for n in "x Wq bq Wk bk Wv bv Wo bo alpha phi temperature gamma beta".split()] + \
       [f"L0_ffn_{n}" for n in "attention_mask position_ids router_w router_b wq wk wv wo w1 w2 ln1 ln2".split()]


def build(nc, t, out):
    scratch = lambda n, s, d=FP32: nc.dram_tensor(n, s, d, kind="Internal").ap()
    q_d, k_d = scratch("q_d", [B, PARTS, D, L], BF16), scratch("k_d", [B, PARTS, D, L], BF16)
    v_d, o_d = scratch("v_d", [B, P, LT, D]), scratch("o_d", [B, P, LT, D])
    a = lambda n: t[f"L0_attn_{n}"]
    f = lambda n: t[f"L0_ffn_{n}"]
    project_qkv(nc, a("x"), a("Wq"), a("bq"), a("Wk"), a("bk"), a("Wv"), a("bv"), a("temperature"), q_d, k_d, v_d)
    oscillatory_attention(nc, a("alpha"), a("phi"), q_d, k_d, v_d, o_d)
    routed_block(nc, a("x"), o_d, a("Wo"), a("bo"), a("gamma"), a("beta"), f("attention_mask"), f("position_ids"),
                 f("router_w"), f("router_b"), f("wq"), f("wk"), f("wv"), f("wo"), f("w1"), f("w2"), f("ln1"), f("ln2"), out)


def kernel(**inputs):
    import concourse.bacc as bacc
    from concourse.bass_utils import run_bass_kernel_spmd

    nc = bacc.Bacc("TRN2", target_bir_lowering=False, num_devices=1)
    arrays, t = {}, {}
    for name in _INS:
        v = np.ascontiguousarray(inputs[name])
        arrays[f"in_{name}"] = v
        t[name] = nc.dram_tensor(f"in_{name}", v.shape, mybir.dt.from_np(v.dtype), kind="ExternalInput").ap()
    out = nc.dram_tensor("out_0", (B, L, D), FP32, kind="ExternalOutput").ap()
    build(nc, t, out)
    r = run_bass_kernel_spmd(nc, [arrays], core_ids=[0])
    return r.results[0]["out_0"]
```

```python
import numpy as np
import concourse.bass as bass
from concourse import mybir
from contextlib import ExitStack

FP32 = mybir.dt.float32
BF16 = mybir.dt.bfloat16
I32 = mybir.dt.int32
ALU = mybir.AluOpType
ACT = mybir.ActivationFunctionType
AX = mybir.AxisListType

B, L, D = 8, 1024, 256
H, HD = 16, 16
P = 128
LT = L // P
KC = D // P
HALF = 512
FREQS = [31.0, 37.0, 41.0, 43.0, 47.0]
NF = len(FREQS)
TWO_PI = 2.0 * float(np.pi)
FRAC = 22
TURN = float(2 ** FRAC)
WRAP = 32 - FRAC
ANGLE = float(np.nextafter(np.float32(TWO_PI / TURN), np.float32(0)))

F = 1024
FB = F // P
MB = 4
CAP = L // 8
KSEL = CAP - 1
ROPE_BASE = 10000.0
NROT = HD // 2
EPS_LN = 1e-5
EPS_RMS = 1e-6
EPS_DEN = 1e-10

PARTS = 3
TERMS = [(i, j) for j in range(PARTS) for i in range(PARTS)][:8]
FOURTH = [1, 0, 0, 1, 0, 0, 0, 0]
ACT_TURNS = [1024] * 8
VP = 32
GROUPS = P // VP
SHIFTS = ALU.logical_shift_left, ALU.arith_shift_right
RING = 4
HEADS = B * H
VW = HD + 1


class Chain:

    def __init__(self, eng, sem, base, per_turn, turn):
        self.eng, self.sem, self.base, self.per_turn, self.turn, self.n = eng, sem, base, per_turn, turn, 0

    def step(self, ins):
        self.n += 1
        ins.then_inc(self.sem, 1)
        self.eng.wait_ge(self.sem, self.base + self.turn * self.per_turn + self.n)

    def close(self):
        assert self.n == self.per_turn, (self.n, self.per_turn)


def wait_pos(eng, sem, value):
    if not isinstance(value, int) or value > 0:
        eng.wait_ge(sem, value)


def project_qkv(nc, x, wq, bq, wk, bk, wv, bv, temperature, q_d, k_d, v_d):
    with ExitStack() as ctx:
        sb = lambda n, s, d=FP32: ctx.enter_context(nc.sbuf_tensor(n, s, d))
        sem = lambda n: ctx.enter_context(nc.semaphore(n))
        ident = sb("p_ident", [P, P])
        w_in = sb("p_w_in", [P, 3, KC, D])
        w_t = sb("p_w_t", [P, 3, KC, D])
        bias_qk = sb("p_bias_qk", [P, 2, KC])
        bv_row = sb("p_bv_row", [P, D])
        temp = sb("p_temp", [P, 5])
        x_in = sb("p_x_in", [P, 2, LT, D])
        x_t = sb("p_x_t", [P, KC, L])
        qk_sb = sb("p_qk_sb", [P, 2, KC, L])
        rest = sb("p_rest", [P, 2, 2, KC, L])
        parts = sb("p_parts", [P, 2, PARTS, KC, L], BF16)
        v_sb = sb("p_v_sb", [P, LT, D])
        lo = ctx.enter_context(nc.psum_tensor("p_lo", [P, 4, HALF], FP32))
        hi = ctx.enter_context(nc.psum_tensor("p_hi", [P, 4, HALF], FP32))
        w_loaded, b_loaded, ident_zero, ident_done = sem("w_loaded"), sem("b_loaded"), sem("p_id0"), sem("p_id1")
        w_turned, w_ready, temp_step = sem("w_turned"), sem("w_ready"), sem("temp_step")
        x_loaded = [sem("x_loaded0"), sem("x_loaded1")]
        x_turned, x_lo, x_hi = sem("x_turned"), sem("x_lo"), sem("x_hi")
        q_summed, k_summed, v_summed = sem("q_summed"), sem("k_summed"), sem("v_summed")
        q_ready, k_ready, v_ready = sem("q_ready"), sem("k_ready"), sem("v_ready")
        q_kept, k_kept, v_kept = sem("q_kept"), sem("k_kept"), sem("v_kept")
        q_split, k_split, split_step = sem("q_split"), sem("k_split"), sem("split_step")

        with nc.Block() as block:

            @block.sync
            def _(sp):
                for n, w in enumerate((wq, wk, wv)):
                    sp.dma_start(w_in[:, n, :, :], w.rearrange("(m p) i -> p m i", p=P)).then_inc(w_loaded, 16)
                sp.dma_start(bias_qk[:, 0, :], bq.rearrange("(m p) -> p m", p=P), allow_slow_non_contiguous=True).then_inc(b_loaded, 16)
                sp.dma_start(bias_qk[:, 1, :], bk.rearrange("(m p) -> p m", p=P), allow_slow_non_contiguous=True).then_inc(b_loaded, 16)
                sp.dma_start(bv_row[:], bv.partition_broadcast(P)).then_inc(b_loaded, 16)
                sp.dma_start(temp[:, 0:1], temperature.partition_broadcast(P)).then_inc(b_loaded, 16)
                with sp.Fori(0, B // 2, 1) as pair:
                    for k in range(2):
                        b = 2 * pair + k
                        sp.wait_ge(x_turned, 2 * pair + 1)
                        sp.dma_start(x_in[:, k, :, :],
                                     x[b, :, :].rearrange("(t p) d -> p t d", p=P)).then_inc(x_loaded[k], 16)

            @block.gpsimd
            def _(pool):
                nc.gpsimd.memset(ident[:], 0.0).then_inc(ident_zero, 1)
                pool.wait_ge(ident_zero, 1)
                nc.gpsimd.affine_select(out=ident[:], in_=ident[:], compare_op=ALU.not_equal, fill=1.0, base=0,
                                        pattern=[[-1, P]], channel_multiplier=1).then_inc(ident_done, 1)

            @block.tensor
            def _(pe):
                pe.sem_inc(x_turned, 1)
                pe.sem_inc(v_summed, 1)
                pe.wait_ge(ident_done, 1)
                pe.wait_ge(w_loaded, 48)
                for n in range(3):
                    for i in range(KC):
                        for m in range(KC):
                            last = nc.tensor.transpose(lo[:, n, i * D + m * P:i * D + (m + 1) * P],
                                                       w_in[:, n, m, i * P:(i + 1) * P], ident[:])
                last.then_inc(w_turned, 1)
                pe.wait_ge(w_ready, 1)

                with pe.Fori(0, B // 2, 1) as pair:
                    for k in range(2):
                        b = 2 * pair + k
                        pe.wait_ge(x_loaded[k], 16 * pair + 16)
                        pe.wait_ge(k_ready, b + 1)
                        for c in range(KC):
                            for t in range(LT):
                                last = nc.tensor.transpose(
                                    lo[:, 2 * c + t // 4, (t % 4) * P:(t % 4 + 1) * P],
                                    x_in[:, k, t, c * P:(c + 1) * P], ident[:])
                        last.then_inc(x_turned, 1)
                        pe.wait_ge(x_lo, b + 1)
                        pe.wait_ge(x_hi, b + 1)
                        pe.wait_ge(v_ready, b + 1)
                        for n, out, done in ((0, hi, q_summed), (1, lo, k_summed)):
                            for m in range(KC):
                                for half in range(2):
                                    for c in range(KC):
                                        last = nc.tensor.matmul(
                                            out[:, 2 * m + half, :], w_t[:, n, c, m * P:(m + 1) * P],
                                            x_t[:, c, half * HALF:(half + 1) * HALF],
                                            start=(c == 0), stop=(c == KC - 1))
                            last.then_inc(done, 1)
                        pe.wait_ge(q_ready, b + 1)
                        for t in range(LT):
                            for c in range(KC):
                                last = nc.tensor.matmul(hi[:, t // 2, (t % 2) * D:(t % 2 + 1) * D],
                                                        x_t[:, c, t * P:(t + 1) * P], w_t[:, 2, c, :],
                                                        start=(c == 0), stop=(c == KC - 1))
                        last.then_inc(v_summed, 1)

            @block.vector
            def _(dve):
                dve.sem_inc(v_ready, 1)
                dve.sem_inc(k_split, 1)
                dve.wait_ge(b_loaded, 64)
                nc.vector.scalar_tensor_tensor(temp[:, 1:2], temp[:, 0:1], -1.0, temp[:, 0:1], ALU.mult,
                                               ALU.max).then_inc(temp_step, 1)
                dve.wait_ge(temp_step, 1)
                nc.vector.tensor_scalar(temp[:, 4:5], temp[:, 1:2], 0.1, None, ALU.add).then_inc(temp_step, 1)
                dve.wait_ge(temp_step, 2)
                nc.vector.reciprocal(temp[:, 2:3], temp[:, 4:5]).then_inc(temp_step, 1)
                dve.wait_ge(temp_step, 3)
                nc.vector.tensor_scalar(temp[:, 3:4], temp[:, 2:3], 1.0 / float(np.sqrt(HD)), None,
                                        ALU.mult).then_inc(temp_step, 1)
                dve.wait_ge(w_turned, 1)
                nc.vector.tensor_copy(w_t[:].rearrange("p a b c -> p (a b c)"),
                                      lo[:, 0:3, :].rearrange("p a b -> p (a b)")).then_inc(w_ready, 1)
                dve.wait_ge(temp_step, 4)

                def split_in_parts(split, n, done):
                    flat = lambda ap: ap.rearrange("p m l -> p (m l)")
                    whole = qk_sb[:, n, :, :]
                    for i in range(PARTS):
                        ins = nc.vector.tensor_copy(flat(parts[:, n, i, :, :]), flat(whole))
                        if i == PARTS - 1:
                            ins.then_inc(done, 1)
                            break
                        split.step(ins)
                        left = rest[:, n, i, :, :]
                        split.step(nc.vector.tensor_tensor(flat(left), flat(whole), flat(parts[:, n, i, :, :]), ALU.subtract))
                        whole = left

                with dve.Fori(0, B, 1) as b:
                    dve.wait_ge(x_turned, b + 2)
                    dve.wait_ge(v_summed, b + 1)
                    nc.vector.tensor_copy(x_t[:, 0, :], lo[:, 0:2, :].rearrange("p a b -> p (a b)")).then_inc(x_lo, 1)
                    dve.wait_ge(q_summed, b + 1)
                    dve.wait_ge(k_split, b + 1)
                    for m in range(KC):
                        last = nc.vector.tensor_scalar(
                            qk_sb[:, 0, m, :], hi[:, 2 * m:2 * m + 2, :].rearrange("p a b -> p (a b)"),
                            bias_qk[:, 0, m:m + 1], temp[:, 3:4], ALU.add, ALU.mult)
                    last.then_inc(q_ready, 1)
                    split = Chain(dve, split_step, 0, 2 * 2 * (PARTS - 1), b)
                    dve.wait_ge(q_ready, b + 1)
                    dve.wait_ge(q_kept, 16 * PARTS * (b + 1))
                    split_in_parts(split, 0, q_split)
                    dve.wait_ge(v_summed, b + 2)
                    dve.wait_ge(v_kept, 16 * b + 16)
                    for n in range(4):
                        last = nc.vector.tensor_tensor(
                            v_sb[:, 2 * n:2 * n + 2, :], hi[:, n, :].rearrange("p (a b) -> p a b", a=2),
                            bv_row[:].unsqueeze(1).broadcast_to([P, 2, D]), ALU.add)
                    last.then_inc(v_ready, 1)
                    dve.wait_ge(k_ready, b + 2)
                    dve.wait_ge(k_kept, 16 * PARTS * (b + 1))
                    split_in_parts(split, 1, k_split)
                    split.close()

            @block.scalar
            def _(act):
                act.sem_inc(k_ready, 1)
                act.sem_inc(q_kept, 16 * PARTS)
                act.sem_inc(k_kept, 16 * PARTS)
                act.sem_inc(v_kept, 16)
                act.wait_ge(b_loaded, 64)
                with act.Fori(0, B, 1) as b:
                    act.wait_ge(x_turned, b + 2)
                    act.wait_ge(v_summed, b + 1)
                    nc.scalar.activation(x_t[:, 1, :], lo[:, 2:4, :].rearrange("p a b -> p (a b)"),
                                         ACT.Copy).then_inc(x_hi, 1)
                    act.wait_ge(k_summed, b + 1)
                    act.wait_ge(k_split, b + 1)
                    for m in range(KC):
                        last = nc.scalar.activation(
                            qk_sb[:, 1, m, :], lo[:, 2 * m:2 * m + 2, :].rearrange("p a b -> p (a b)"),
                            ACT.Identity, bias=bias_qk[:, 1, m:m + 1])
                    last.then_inc(k_ready, 1)
                    act.wait_ge(q_split, b + 1)
                    for i in range(PARTS):
                        act.dma_start(q_d[b, i, :, :].rearrange("(m p) l -> p m l", p=P), parts[:, 0, i, :, :]).then_inc(q_kept, 16)
                    act.wait_ge(v_ready, b + 2)
                    act.dma_start(v_d[b, :, :, :], v_sb[:]).then_inc(v_kept, 16)
                    act.wait_ge(k_split, b + 2)
                    for i in range(PARTS):
                        act.dma_start(k_d[b, i, :, :].rearrange("(m p) l -> p m l", p=P), parts[:, 1, i, :, :]).then_inc(k_kept, 16)
                act.wait_ge(q_kept, 16 * PARTS * (B + 1))
                act.wait_ge(k_kept, 16 * PARTS * (B + 1))
                act.wait_ge(v_kept, 16 * B + 16)


def oscillatory_attention(nc, alpha, phi, q_d, k_d, v_d, o_d):
    U = LT
    with ExitStack() as ctx:
        sb = lambda n, s, d=FP32: ctx.enter_context(nc.sbuf_tensor(n, s, d))
        ps = lambda n, s: ctx.enter_context(nc.psum_tensor(n, s, FP32))
        sem = lambda n: ctx.enter_context(nc.semaphore(n))
        ident = sb("a_ident", [P, P])
        table = sb("a_table", [P, 2, H, NF])
        table_i = sb("a_table_i", [P, H, NF], I32)
        head_c = sb("a_head_c", [P, 2, 2, NF])
        diag = sb("a_diag", [P, 2, NF - 1, P])
        q_r = sb("a_q_r", [P, 2, L], BF16)
        k_r = sb("a_k_r", [P, 2, L], BF16)
        v_r = sb("a_v_r", [P, 2, LT, VP])
        fold = sb("a_fold", [P, 3, VW])
        ones = sb("a_ones", [P, P])
        one_set = sb("a_one_set", [P, 1])
        v_part = sb("a_v_part", [P, 2, 7, HD])
        v_sum = sb("a_v_sum", [P, HD])
        early = sb("a_early", [P, 2, L], I32)
        score = sb("a_score", [P, 2, L])
        turn = sb("a_turn", [P, RING, NF, L], I32)
        weight = sb("a_weight", [P, LT, L])
        num = sb("a_num", [P, L])
        den = sb("a_den", [P, 2, LT])
        raised = sb("a_raised", [P, LT, HD])
        out = sb("a_out", [P, 2, LT, HD])
        ps_score = ps("a_ps_score", [P, L])
        ps_sum = ps("a_ps_sum", [P, 2, L])
        ps_out = ps("a_ps_out", [P, L])

        table_in, table_step, setup, id_zero = sem("table_in"), sem("table_step"), sem("a_setup"), sem("a_id_zero")
        qk_loaded = [sem("qk_loaded0"), sem("qk_loaded1")]
        v_loaded = [sem("v_loaded0"), sem("v_loaded1")]
        const_ready, diag_ready = sem("const_ready"), sem("diag_ready")
        scored, drawn, scaled, wrapped = sem("scored"), sem("drawn"), sem("scaled"), sem("wrapped")
        sines_pe, sines = sem("sines_pe"), sem("sines")
        part_summed, summed, sum_step = sem("part_summed"), sem("summed"), sem("sum_step")
        squashed, weighted, num_drawn, turned = sem("squashed"), sem("weighted"), sem("num_drawn"), sem("turned")
        v_step, v_parted = sem("v_step"), sem("v_parted")
        norm_step, normed = sem("norm_step"), sem("normed")
        stored = [sem("stored0"), sem("stored1")]

        def heads_of(eng, body):
            for g in range(4):
                body(g, g % 2)
            with eng.Fori(2, HEADS // 2 - 1, 1) as pair:
                for k in range(2):
                    body(2 * pair + k, k)
            for g in range(HEADS - 2, HEADS + 1):
                body(g, g % 2)

        LOADS = 16 * 2 * len(TERMS)
        SUM_STEPS = U - sum(FOURTH)
        next_loads = lambda g, k: LOADS // 2 * g + (LOADS if k == 0 else LOADS // 2 * 3)
        v_loads = lambda g, k: 8 * g + (16 if k == 0 else 8)
        main = lambda g: not isinstance(g, int) or g < HEADS
        after = lambda g: not isinstance(g, int) or g >= 1
        unit_in = lambda n: not isinstance(n, int) or n < HEADS * U

        with nc.Block() as block:

            @block.sync
            def _(sp):
                sp.dma_start(table[:, 0, :, :].rearrange("p h f -> p (h f)"),
                             alpha.rearrange("h f -> (h f)").partition_broadcast(P)).then_inc(table_in, 16)
                sp.dma_start(table[:, 1, :, :].rearrange("p h f -> p (h f)"),
                             phi.rearrange("h f -> (h f)").partition_broadcast(P)).then_inc(table_in, 16)

                def load(g, k):
                    wait_pos(sp, scored, (g - 1) * U)
                    for n, term in enumerate(TERMS):
                        for dst, src, part in ((q_r, q_d, term[0]), (k_r, k_d, term[1])):
                            sp.dma_start(dst[HD * n:HD * (n + 1), k, :],
                                         src[g // H, part, bass.ds((g % H) * HD, HD), :]).then_inc(qk_loaded[k], 16)
                    wait_pos(sp, turned, g - 1)
                    sp.dma_start(v_r[:, k, :, 0:HD], v_d[g // H, :, :, bass.ds((g % H) * HD, HD)]).then_inc(v_loaded[k], 16)

                def store(g, k):
                    sp.wait_ge(normed, g)
                    sp.dma_start(o_d[(g - 1) // H, :, :, bass.ds(((g - 1) % H) * HD, HD)],
                                 out[:, 1 - k, :, :]).then_inc(stored[1 - k], 16)

                sp.wait_ge(setup, 3)
                load(0, 0)

                def body(g, k):
                    if not isinstance(g, int) or g + 1 < HEADS:
                        load(g + 1, 1 - k)
                    if after(g):
                        store(g, k)
                heads_of(sp, body)
                for k in range(2):
                    sp.wait_ge(stored[k], 16 * HEADS // 2)

            @block.gpsimd
            def _(pool):
                nc.gpsimd.memset(ident[:], 0.0).then_inc(id_zero, 1)
                nc.gpsimd.memset(ones[:], 1.0).then_inc(setup, 1)
                nc.gpsimd.memset(v_r[:].rearrange("p a b c -> p (a b c)"), 0.0).then_inc(id_zero, 1)
                pool.wait_ge(id_zero, 2)
                nc.gpsimd.memset(v_r[:, :, :, HD], 1.0).then_inc(setup, 1)
                nc.gpsimd.affine_select(out=ident[:], in_=ident[:], compare_op=ALU.not_equal, fill=1.0, base=0,
                                        pattern=[[-1, P]], channel_multiplier=1).then_inc(setup, 1)
                pool.wait_ge(setup, 3)
                group = lambda n: ident[:, VP * n:VP * n + VW]
                for n in range(2):
                    nc.gpsimd.tensor_tensor(fold[:, n, :], group(2 * n), group(2 * n + 1), ALU.add).then_inc(setup, 1)
                pool.wait_ge(setup, 5)
                nc.gpsimd.tensor_tensor(fold[:, 2, :], fold[:, 0, :], fold[:, 1, :], ALU.add).then_inc(setup, 1)
                pool.wait_ge(table_step, 3)

                def constants(g, k):
                    wait_pos(pool, summed, (g - 1) * U)
                    h = g % H
                    nc.gpsimd.tensor_copy(head_c[:, k, :, :], table[:, :, bass.ds(h, 1), :].rearrange(
                        "p a h f -> p a (h f)")).then_inc(const_ready, 1)
                    pool.wait_ge(const_ready, g + 1)
                    for f in range(NF - 1):
                        last = nc.gpsimd.tensor_tensor(diag[:, k, f, :], ident[:],
                                                       head_c[:, k, 0, f:f + 1].broadcast_to([P, P]), ALU.mult)
                    last.then_inc(diag_ready, 1)

                constants(0, 0)

                def body(g, k):
                    if main(g):
                        pool.wait_ge(v_loaded[k], v_loads(g, k))
                        wait_pos(pool, turned, g - 1)
                        part = v_part[:, k, :, :]
                        nc.gpsimd.tensor_tensor(part[:, 0:4, :], v_r[:, k, 0:4, 0:HD], v_r[:, k, 4:8, 0:HD],
                                                ALU.add).then_inc(v_step, 1)
                        pool.wait_ge(v_step, 2 * g + 1)
                        nc.gpsimd.tensor_tensor(part[:, 4:6, :], part[:, 0:2, :], part[:, 2:4, :], ALU.add).then_inc(v_step, 1)
                        pool.wait_ge(v_step, 2 * g + 2)
                        nc.gpsimd.tensor_tensor(part[:, 6, :], part[:, 4, :], part[:, 5, :], ALU.add).then_inc(v_parted, 1)
                    if not isinstance(g, int) or g + 1 < HEADS:
                        constants(g + 1, 1 - k)
                heads_of(pool, body)

            @block.tensor
            def _(pe):
                def scores(n, s, k):
                    wait_pos(pe, drawn, n)
                    for half in range(2):
                        last = nc.tensor.matmul(ps_score[:, half * HALF:(half + 1) * HALF], k_r[:, k, s * P:(s + 1) * P],
                                                q_r[:, k, half * HALF:(half + 1) * HALF], start=True, stop=True)
                    last.then_inc(scored, 1)

                def sum_sines(n, s, k, half):
                    if half == 0:
                        pe.wait_ge(sines_pe, n + 1)
                        wait_pos(pe, summed, n - 1)
                    sines_here = NF - 1 if half == 0 or FOURTH[s] else NF - 2
                    for f in range(sines_here):
                        last = nc.tensor.matmul(
                            ps_sum[:, s % 2, half * HALF:(half + 1) * HALF], diag[:, k, f, :],
                            turn[:, s % RING, f, half * HALF:(half + 1) * HALF].bitcast(FP32),
                            start=(f == 0), stop=(f == sines_here - 1))
                    if half:
                        last.then_inc(part_summed, 1)

                def times_v(part, k):
                    for half in range(2):
                        for j in range(GROUPS * part, GROUPS * (part + 1)):
                            at = VP * (j % GROUPS)
                            last = nc.tensor.matmul(
                                ps_out[at:at + VP, half * HALF:(half + 1) * HALF], v_r[:, k, j, :],
                                weight[:, j, half * HALF:(half + 1) * HALF], start=(part == 0), stop=(part == 1))
                    last.then_inc(weighted, 1)

                pe.wait_ge(setup, 6)
                pe.wait_ge(qk_loaded[0], LOADS)
                scores(0, 0, 0)
                scores(1, 1, 0)
                scores(2, 2, 0)

                def body(g, k):
                    n0 = g * U
                    for s in range(U):
                        n = n0 + s
                        if s == 3 and after(g):
                            pe.wait_ge(squashed, n0)
                            times_v(1, 1 - k)
                        if s == 5 and after(g):
                            pe.wait_ge(num_drawn, g)
                            for t in range(LT):
                                nc.tensor.matmul(ps_out[:, t * VW:(t + 1) * VW], num[:, t * P:(t + 1) * P],
                                                 fold[:, 2, :], start=True, stop=True)
                            pe.wait_ge(v_parted, g)
                            nc.tensor.matmul(ps_out[:, LT * VW:LT * VW + HD], ones[:], v_part[:, 1 - k, 6, :],
                                             start=True, stop=True).then_inc(turned, 1)
                        if s == U - 1 and main(g):
                            pe.wait_ge(squashed, n0 + GROUPS)
                            pe.wait_ge(v_loaded[k], v_loads(g, k))
                            wait_pos(pe, normed, g)
                            times_v(0, k)
                        for half in range(2):
                            if s > 0 and main(g):
                                if s == 1 and half == 0:
                                    pe.wait_ge(diag_ready, g + 1)
                                sum_sines(n - 1, s - 1, k, half)
                            if s == 0 and after(g):
                                sum_sines(n - 1, U - 1, 1 - k, half)
                            if half == 0 and main(g) and unit_in(n + 3):
                                if s == U - 3:
                                    pe.wait_ge(qk_loaded[1 - k], next_loads(g, k))
                                scores(n + 3, (s + 3) % U, k if s < U - 3 else 1 - k)

                heads_of(pe, body)

            @block.scalar
            def _(act):
                def draw(n, s, g, k):
                    act.wait_ge(scored, n + 1)
                    wait_pos(act, scaled, n - 1)
                    copied = nc.scalar.activation(score[:, s % 2, :], ps_score[:], ACT.Copy)
                    if ACT_TURNS[s]:
                        if s == 0:
                            act.wait_ge(const_ready, g + 1)
                        wait_pos(act, wrapped, n - 1)
                        copied = nc.scalar.activation(
                            early[:, s % 2, L - ACT_TURNS[s]:L], ps_score[:, L - ACT_TURNS[s]:L], ACT.Identity,
                            bias=head_c[:, k, 1, NF - 1:NF], scale=TURN / FREQS[NF - 1])
                    copied.then_inc(drawn, 1)

                act.wait_ge(setup, 3)
                nc.scalar.activation(one_set[:], ones[:, 0:1], ACT.Silu)
                draw(0, 0, 0, 0)
                draw(1, 1, 0, 0)

                def body(g, k):
                    for s in range(U):
                        n = g * U + s
                        if s == 4 and after(g):
                            act.wait_ge(weighted, 2 * g)
                            wait_pos(act, turned, g - 1)
                            nc.scalar.activation(num[:], ps_out[:], ACT.Copy).then_inc(num_drawn, 1)
                        if (s >= 3 and main(g)) or (s < 3 and after(g)):
                            act.wait_ge(summed, n - 2)
                            nc.scalar.activation(weight[:, (s - 3) % U, :], weight[:, (s - 3) % U, :], ACT.Tanh,
                                                 scale=0.5).then_inc(squashed, 1)
                        if main(g):
                            if unit_in(n + 2):
                                if s < U - 2:
                                    draw(n + 2, s + 2, g, k)
                                else:
                                    draw(n + 2, s + 2 - U, g + 1, 1 - k)
                            act.wait_ge(wrapped, n + 1)
                            for lo, hi, done in ((0, NF - 1, sines_pe), (NF - 1, NF, sines)):
                                nc.scalar.activation(
                                    turn[:, s % RING, lo:hi, :].bitcast(FP32), turn[:, s % RING, lo:hi, :],
                                    ACT.Sin, scale=ANGLE).then_inc(done, 1)
                heads_of(act, body)

            @block.vector
            def _(dve):
                dve.wait_ge(table_in, 32)
                nc.vector.tensor_scalar(table_i[:], table[:, 1, :, :], TURN / TWO_PI, None, ALU.mult).then_inc(table_step, 1)
                dve.wait_ge(table_step, 1)
                nc.vector.tensor_scalar(table_i[:], table_i[:], WRAP, WRAP, ALU.logical_shift_left,
                                        ALU.arith_shift_right).then_inc(table_step, 1)
                dve.wait_ge(table_step, 2)
                nc.vector.tensor_copy(table[:, 1, :, :], table_i[:]).then_inc(table_step, 1)

                def scale(n, s, g, k):
                    if s == 0:
                        dve.wait_ge(const_ready, g + 1)
                    dve.wait_ge(drawn, n + 1)
                    wait_pos(dve, summed, n - RING + 1)
                    own = L - ACT_TURNS[s]
                    for f in range(NF):
                        cols = L if f < NF - 1 else own
                        if cols:
                            last = nc.vector.tensor_scalar(turn[:, s % RING, f, 0:cols], score[:, s % 2, 0:cols],
                                                           TURN / FREQS[f], head_c[:, k, 1, f:f + 1], ALU.mult, ALU.add)
                    last.then_inc(scaled, 1)

                def wrap(n, s):
                    dve.wait_ge(scaled, n + 1)
                    own = L - ACT_TURNS[s]
                    whole = turn[:, s % RING, :, :].rearrange("p f l -> p (f l)")[:, 0:NF * L - ACT_TURNS[s]]
                    last = nc.vector.tensor_scalar(whole, whole, WRAP, WRAP, *SHIFTS)
                    if ACT_TURNS[s]:
                        last = nc.vector.tensor_scalar(turn[:, s % RING, NF - 1, own:L], early[:, s % 2, own:L],
                                                       WRAP, WRAP, *SHIFTS)
                    last.then_inc(wrapped, 1)

                def finish(n, s, g, k):
                    dve.wait_ge(part_summed, n + 1)
                    dve.wait_ge(sines, n + 1)
                    if s % GROUPS == 0:
                        wait_pos(dve, weighted, 2 * g - 1 + s // GROUPS)
                    last = nc.vector.scalar_tensor_tensor(
                        weight[:, s, :], turn[:, s % RING, NF - 1, :].bitcast(FP32), head_c[:, k, 0, NF - 1:NF],
                        ps_sum[:, s % 2, :], ALU.mult, ALU.add)
                    if not FOURTH[s]:
                        last.then_inc(sum_step, 1)
                        dve.wait_ge(sum_step, g * SUM_STEPS + s + 1 - sum(FOURTH[:s]))
                        last = nc.vector.scalar_tensor_tensor(
                            weight[:, s, HALF:L], turn[:, s % RING, NF - 2, HALF:L].bitcast(FP32),
                            head_c[:, k, 0, NF - 2:NF - 1], weight[:, s, HALF:L], ALU.mult, ALU.add)
                    last.then_inc(summed, 1)

                scale(0, 0, 0, 0)
                wrap(0, 0)

                def body(g, k):
                    for s in range(U):
                        n = g * U + s
                        if s == 6 and after(g):
                            dve.wait_ge(turned, g)
                            wait_pos(dve, stored[1 - k], 8 * g - (16 if k == 0 else 8))
                            rows = ps_out[:, 0:LT * VW].rearrange("p (t c) -> p t c", c=VW)
                            nc.vector.tensor_copy(v_sum[:], ps_out[:, LT * VW:LT * VW + HD]).then_inc(norm_step, 1)
                            nc.vector.tensor_scalar(den[:, 0, :], rows[:, :, HD], float(L), 2 * EPS_DEN, ALU.add,
                                                    ALU.add).then_inc(norm_step, 1)
                            dve.wait_ge(norm_step, 4 * (g - 1) + 2)
                            nc.vector.reciprocal(den[:, 1, :], den[:, 0, :]).then_inc(norm_step, 1)
                            nc.vector.tensor_tensor(raised[:], rows[:, :, 0:HD], v_sum[:].unsqueeze(1).broadcast_to(
                                [P, LT, HD]), ALU.add).then_inc(norm_step, 1)
                            dve.wait_ge(norm_step, 4 * (g - 1) + 4)
                            nc.vector.tensor_tensor(out[:, 1 - k, :, :], raised[:],
                                                    den[:, 1, :].unsqueeze(2).broadcast_to([P, LT, HD]),
                                                    ALU.mult).then_inc(normed, 1)
                        if main(g) and unit_in(n + 1):
                            if s < U - 1:
                                scale(n + 1, s + 1, g, k)
                            else:
                                scale(n + 1, 0, g + 1, 1 - k)
                        if s > 1 and main(g):
                            finish(n - 2, s - 2, g, k)
                        if s < 2 and after(g):
                            finish(n - 2, U - 2 + s, g - 1, 1 - k)
                        if main(g) and unit_in(n + 1):
                            wrap(n + 1, (s + 1) % U)
                dve.wait_ge(table_step, 3)
                heads_of(dve, body)


def routed_block(nc, x, o_d, wo_a, bo, gamma, beta, mask, positions, router_w, router_b, wq, wk, wv, wo, w1, w2,
                 ln1, ln2, y_out):
    QH = 4
    C1 = 6.28125
    C2 = TWO_PI - C1
    ROUND = 1.5 * 2.0 ** 23
    PI_IN = float(np.nextafter(np.float32(np.pi), np.float32(0)))
    with ExitStack() as ctx:
        sb = lambda n, s, d=FP32: ctx.enter_context(nc.sbuf_tensor(n, s, d))
        sem = lambda n: ctx.enter_context(nc.semaphore(n))
        ident, tri, last_row = sb("ident", [P, P]), sb("tri", [P, P]), sb("last_row", [P, P])
        ones = sb("ones", [P, P])
        slot_i, slot = sb("slot_i", [P, P], I32), sb("slot", [P, P])
        tok_i, base_i = sb("tok_i", [P, LT], I32), sb("base_i", [P, B], I32)
        base = sb("base", [P, 2, B])
        pos_i, pos_f = sb("pos_i", [MB * LT, P], I32), sb("pos_f", [MB * LT, P])
        pos = sb("pos", [P, B, LT])
        inv_freq = sb("inv_freq", [P, NROT])
        rows = sb("rows", [P, 6, D])
        r_bias = sb("r_bias", [P, 1])
        woa_in, woa_t = sb("woa_in", [P, KC, D]), sb("woa_t", [P, KC, D])
        wqkv, wo_sb = sb("wqkv", [P, KC, 3 * D]), sb("wo_sb", [P, KC, D])
        w1_sb, w2_sb = sb("w1_sb", [P, KC, F]), sb("w2_sb", [P, FB, D])
        o_in, x_in = sb("o_in", [P, LT, D]), sb("x_in", [P, LT, D])
        o_t = sb("o_t", [P, KC, L])
        mix = sb("mix", [P, LT, D])
        x1 = sb("x1", [P, LT, D])
        dense = sb("dense", [P, LT, D])
        stats, moments = sb("stats", [P, 3, LT, 6]), sb("moments", [P, 3, LT, 2])
        spread = sb("spread", [P, 3, LT])
        dump = sb("dump", [P, L])
        w_col, w_diag, w_row = sb("w_col", [P, 2, LT]), sb("w_diag", [P, LT, P]), sb("w_row", [P, L])
        ahead, rank = sb("ahead", [P, LT, 3]), sb("rank", [P, LT])
        one_hot = sb("one_hot", [P, LT, P])
        ext = sb("ext", [P, LT, 3])
        xs, ext_s = sb("xs", [P, D]), sb("ext_s", [P, 3])
        where = sb("where", [P, 2], mybir.dt.uint32)
        m_row, m_t, m_sel = sb("m_row", [P, L]), sb("m_t", [P, LT, P]), sb("m_sel", [P, P])
        small = sb("small", [P, 16])
        hn, hn_t = sb("hn", [P, D]), sb("hn_t", [P, KC, P])
        qk, v_sb = sb("qk", [P, 2 * H, HD]), sb("v_sb", [P, D])
        ang, ang_r, trig = sb("ang", [P, 4, NROT]), sb("ang_r", [P, 2, NROT]), sb("trig", [P, 2, NROT])
        rot_a, rot_b = sb("rot_a", [P, 2 * H, HD]), sb("rot_b", [P, 2 * H, HD])
        qk_pad = sb("qk_pad", [P, 2 * H, 32])
        qk_t = sb("qk_t", [P, 2 * QH, P])
        logits, probs_t = sb("logits", [P, H, P]), sb("probs_t", [P, H, P])
        peak, total, inv_total = sb("peak", [P, H]), sb("total", [P, H]), sb("inv_total", [P, H])
        att, att_t = sb("att", [P, D]), sb("att_t", [P, KC, P])
        xa, h2, h2_t, g_t = sb("xa", [P, D]), sb("h2", [P, D]), sb("h2_t", [P, KC, P]), sb("g_t", [P, FB, P])
        xm, ys, res = sb("xm", [P, D]), sb("ys", [P, D]), sb("res", [P, D])
        A = ctx.enter_context(nc.psum_tensor("A", [P, 4, HALF], FP32))
        Bk = ctx.enter_context(nc.psum_tensor("Bk", [P, 4, HALF], FP32))

        names = ("in_loaded o_turned ot_lo ot_hi projected var1 dev1 var2 dev2 diag_w w_spread w_drawn "
                 "hot gathered token_ready ms1 dev3 dense_var dense_dev dense_ready normed1 hn_turned hn_drawn "
                 "qkv qk_drawn angles trig_ready padded qk_turned qk_t_drawn mask_rows m_turned m_drawn "
                 "m_picked m_sel_drawn scored shifted exped p_turned p_lo p_hi attended att_ready att_turned "
                 "att_drawn mixed ms2 dev4 normed2 h2_turned h2_drawn up gelu_ready down var5 dev5 "
                 "res_ready dense_stored scattered thr_ready xb_ready").split()
        S = {n: sem("r_" + n) for n in names}
        const_in, const_set, pool_step, setup_pe = sem("const_in"), sem("const_set"), sem("pool_step"), sem("setup_pe")
        setup_dve, dve_step = sem("setup_dve"), sem("dve_step")
        gate_s, gated = sb("gate_s", [P, 2]), sem("gated")
        flat = lambda ap: ap.rearrange("p a b -> p (a b)")

        with nc.Block() as block:

            @block.sync
            def _(sp):
                load = lambda dst, src: sp.dma_start(dst, src).then_inc(const_in, 16)
                load(woa_in[:], wo_a.rearrange("(m p) i -> p m i", p=P))
                for n, v in enumerate((bo, gamma, beta, router_w.rearrange("d o -> (d o)"), ln1, ln2)):
                    load(rows[:, n, :], v.partition_broadcast(P))
                load(r_bias[:], router_b.partition_broadcast(P))
                load(pos_i[:], positions.rearrange("b (t p) -> (b t) p", p=P))
                for n, w in enumerate((wq, wk, wv)):
                    load(wqkv[:, :, n * D:(n + 1) * D], w.rearrange("(c p) n -> p c n", p=P))
                load(wo_sb[:], wo.rearrange("(c p) n -> p c n", p=P))
                load(w1_sb[:], w1.rearrange("(c p) n -> p c n", p=P))
                load(w2_sb[:], w2.rearrange("(c p) n -> p c n", p=P))
                with sp.Fori(0, B, 1) as b:
                    sp.wait_ge(gated, 3 * b + 1)
                    sp.dma_start(o_in[:], o_d[b, :, :, :]).then_inc(S["in_loaded"], 16)
                    sp.dma_start(x_in[:], x[b, :, :].rearrange("(t p) d -> p t d", p=P)).then_inc(S["in_loaded"], 16)
                    sp.wait_ge(S["dense_ready"], b + 1)
                    sp.dma_start(y_out[b, :, :].rearrange("(t p) d -> p t d", p=P), dense[:]).then_inc(S["dense_stored"], 16)
                sp.wait_ge(S["dense_stored"], 16 * B)

            @block.gpsimd
            def _(pool):
                nc.gpsimd.memset(ident[:], 0.0).then_inc(pool_step, 1)
                nc.gpsimd.memset(tri[:], 1.0).then_inc(pool_step, 1)
                nc.gpsimd.memset(last_row[:], 0.0).then_inc(pool_step, 1)
                nc.gpsimd.memset(ones[:], 1.0)
                nc.gpsimd.memset(gate_s[:], 1.0)
                pool.sem_inc(gated, 1)
                nc.gpsimd.memset(flat(qk_pad[:]), 0.0)
                for n in range(NROT):
                    nc.gpsimd.memset(inv_freq[:, n:n + 1], float(np.float32(1.0) / np.float32(ROPE_BASE) ** np.float32(2 * n / HD)))
                nc.gpsimd.iota(slot_i[:], pattern=[[1, P]], base=0, channel_multiplier=0)
                nc.gpsimd.iota(tok_i[:], pattern=[[P, LT]], base=0, channel_multiplier=1)
                nc.gpsimd.iota(base_i[:], pattern=[[L, B]], base=0, channel_multiplier=0).then_inc(pool_step, 1)
                pool.wait_ge(pool_step, 4)
                nc.gpsimd.affine_select(out=ident[:], in_=ident[:], compare_op=ALU.not_equal, fill=1.0, base=0,
                                        pattern=[[-1, P]], channel_multiplier=1)
                nc.gpsimd.affine_select(out=tri[:], in_=tri[:], compare_op=ALU.is_gt, fill=0.0, base=0,
                                        pattern=[[-1, P]], channel_multiplier=1)
                nc.gpsimd.affine_select(out=last_row[:], in_=last_row[:], compare_op=ALU.not_equal, fill=1.0,
                                        base=-KSEL, pattern=[[0, P]], channel_multiplier=1).then_inc(const_set, 1)
                pool.wait_ge(const_in, 16 * CONST_LOADS)

                def gate(n):
                    pool.wait_ge(gated, n + 1)
                    nc.gpsimd.tensor_tensor(gate_s[:, 1:2], gate_s[:, 0:1], gate_s[:, 0:1], ALU.mult).then_inc(gated, 1)

                with pool.Fori(0, B, 1) as b:
                    pool.wait_ge(S["in_loaded"], 32 * b + 32)
                    nc.gpsimd.tensor_tensor(x_in[:], x_in[:], rows[:, 2, :].unsqueeze(1).broadcast_to([P, LT, D]),
                                            ALU.add).then_inc(S["xb_ready"], 1)
                    pool.wait_ge(S["token_ready"], b + 1)
                    gate(3 * b)
                    pool.indirect_dma_start(
                        out=m_row[:], out_offset=None, in_=mask.rearrange("b o q k -> (b o q) k"),
                        in_offset=bass.IndirectOffsetOnAxis(ap=where[:, 1:2], axis=0)).then_inc(S["mask_rows"], 16)
                    pool.wait_ge(S["res_ready"], b + 1)
                    pool.wait_ge(S["dense_stored"], 16 * b + 16)
                    gate(3 * b + 1)
                    pool.indirect_dma_start(
                        out=y_out.rearrange("b l d -> (b l) d"),
                        out_offset=bass.IndirectOffsetOnAxis(ap=where[0:KSEL, 0:1], axis=0),
                        in_=res[0:KSEL, :], in_offset=None).then_inc(S["scattered"], 16)
                    pool.wait_ge(S["scattered"], 16 * b + 16)
                    gate(3 * b + 2)

            @block.tensor
            def _(pe):
                mm, tr = nc.tensor.matmul, nc.tensor.transpose
                pe.wait_ge(const_set, 1)
                pe.wait_ge(const_in, 16 * CONST_LOADS)
                for i in range(KC):
                    for m in range(KC):
                        tr(A[:, 0, i * D + m * P:i * D + (m + 1) * P], woa_in[:, m, i * P:(i + 1) * P], ident[:])
                pe.wait_ge(setup_dve, 1)
                tr(A[:, 1, 0:MB * LT], pos_f[:], ident[0:MB * LT, 0:MB * LT]).then_inc(setup_pe, 1)
                pe.wait_ge(setup_dve, 2)

                def turn_two(out, src, done):
                    for c in range(KC):
                        ins = tr(out[:, c * P:(c + 1) * P], src[:, c * P:(c + 1) * P], ident[:])
                    ins.then_inc(S[done], 1)

                with pe.Fori(0, B, 1) as b:
                    ready = lambda *names: [pe.wait_ge(S[n], b + 1) for n in names]
                    pe.wait_ge(S["in_loaded"], 32 * b + 32)
                    for c in range(KC):
                        for t in range(LT):
                            ins = tr(A[:, 2 * c + t // 4, (t % 4) * P:(t % 4 + 1) * P], o_in[:, t, c * P:(c + 1) * P], ident[:])
                    ins.then_inc(S["o_turned"], 1)
                    ready("ot_lo", "ot_hi")
                    for t in range(LT):
                        for c in range(KC):
                            ins = mm(Bk[:, t // 2, (t % 2) * D:(t % 2 + 1) * D], o_t[:, c, t * P:(t + 1) * P],
                                     woa_t[:, c, :], start=(c == 0), stop=(c == KC - 1))
                    ins.then_inc(S["projected"], 1)
                    ready("diag_w")
                    for t in range(LT):
                        ins = mm(A[:, t // 4, (t % 4) * P:(t % 4 + 1) * P], ones[:], w_diag[:, t, :], start=True, stop=True)
                    ins.then_inc(S["w_spread"], 1)
                    ready("hot")
                    for t in range(LT):
                        mm(A[:, 2, 0:D], one_hot[:, t, :], x1[:, t, :], start=(t == 0), stop=(t == LT - 1))
                    for t in range(LT):
                        ins = mm(A[:, 3, 0:3], one_hot[:, t, :], ext[:, t, :], start=(t == 0), stop=(t == LT - 1))
                    ins.then_inc(S["gathered"], 1)
                    ready("token_ready")
                    mm(Bk[:, 3, 0:1], last_row[:], ext_s[:, 0:1], start=True, stop=True).then_inc(S["thr_ready"], 1)
                    ready("normed1")
                    turn_two(Bk[:, 0, :], hn, "hn_turned")
                    ready("hn_drawn")
                    for c in range(KC):
                        mm(Bk[:, 1, :], hn_t[:, c, :], wqkv[:, c, 0:2 * D], start=(c == 0), stop=(c == KC - 1))
                    for c in range(KC):
                        ins = mm(Bk[:, 2, 0:D], hn_t[:, c, :], wqkv[:, c, 2 * D:3 * D], start=(c == 0), stop=(c == KC - 1))
                    ins.then_inc(S["qkv"], 1)
                    pe.wait_ge(S["mask_rows"], 16 * b + 16)
                    for t in range(LT):
                        ins = tr(A[:, t // 4, (t % 4) * P:(t % 4 + 1) * P], m_row[:, t * P:(t + 1) * P], ident[:])
                    ins.then_inc(S["m_turned"], 1)
                    ready("m_drawn")
                    for t in range(LT):
                        ins = mm(Bk[:, 0, 0:P], m_t[:, t, :], one_hot[:, t, :], start=(t == 0), stop=(t == LT - 1))
                    ins.then_inc(S["m_picked"], 1)
                    ready("padded")
                    for n in range(2 * QH):
                        ins = tr(A[:, 2 + n // 4, (n % 4) * P:(n % 4 + 1) * P],
                                 qk_pad[:, n * QH:(n + 1) * QH, :].rearrange("p a b -> p (a b)"), ident[:])
                    ins.then_inc(S["qk_turned"], 1)
                    ready("qk_t_drawn")
                    for n in range(QH):
                        for r in range(QH):
                            rows_r = slice(32 * r, 32 * r + HD)
                            ins = mm(A[:, r, n * P:(n + 1) * P], qk_t[rows_r, n, :], qk_t[rows_r, QH + n, :], start=True, stop=True)
                    ins.then_inc(S["scored"], 1)
                    ready("exped")
                    for n in range(H):
                        ins = tr(Bk[0:KSEL, n // 4, (n % 4) * P:(n % 4 + 1) * P], logits[:, n, 0:KSEL], ident[:])
                    ins.then_inc(S["p_turned"], 1)
                    ready("p_lo", "p_hi")
                    for n in range(H):
                        h = 4 * (n % 4) + n // 4
                        ins = mm(A[:, 0, h * HD:(h + 1) * HD], probs_t[0:KSEL, n, :], v_sb[0:KSEL, h * HD:(h + 1) * HD],
                                 start=True, stop=True)
                    ins.then_inc(S["attended"], 1)
                    ready("att_ready")
                    turn_two(A[:, 1, :], att, "att_turned")
                    ready("att_drawn")
                    for c in range(KC):
                        ins = mm(A[:, 2, 0:D], att_t[:, c, :], wo_sb[:, c, :], start=(c == 0), stop=(c == KC - 1))
                    ins.then_inc(S["mixed"], 1)
                    ready("normed2")
                    turn_two(A[:, 3, :], h2, "h2_turned")
                    ready("h2_drawn")
                    for n in range(FB):
                        for c in range(KC):
                            ins = mm(Bk[:, n // 4, (n % 4) * P:(n % 4 + 1) * P], w1_sb[:, c, n * P:(n + 1) * P],
                                     h2_t[:, c, :], start=(c == 0), stop=(c == KC - 1))
                    ins.then_inc(S["up"], 1)
                    ready("gelu_ready")
                    for n in range(FB):
                        ins = mm(Bk[:, 2, 0:D], g_t[:, n, :], w2_sb[:, n, :], start=(n == 0), stop=(n == FB - 1))
                    ins.then_inc(S["down"], 1)

            @block.scalar
            def _(act):
                with act.Fori(0, B, 1) as b:
                    ready = lambda *names: [act.wait_ge(S[n], b + 1) for n in names]
                    run = lambda out, src, fn, done: nc.scalar.activation(out, src, fn).then_inc(S[done], 1)
                    ready("o_turned")
                    run(o_t[:, 1, :], flat(A[:, 2:4, :]), ACT.Copy, "ot_hi")
                    ready("var1")
                    run(spread[:, 0, :], spread[:, 0, :], ACT.Sqrt, "dev1")
                    ready("var2")
                    run(spread[:, 1, :], spread[:, 1, :], ACT.Sqrt, "dev2")
                    ready("w_spread")
                    run(w_row[:], flat(A[:, 0:2, :]), ACT.Copy, "w_drawn")
                    ready("ms1")
                    run(small[:, 1:2], small[:, 0:1], ACT.Sqrt, "dev3")
                    ready("dense_var")
                    run(spread[:, 2, :], spread[:, 2, :], ACT.Sqrt, "dense_dev")
                    ready("hn_turned")
                    run(flat(hn_t[:]), Bk[:, 0, 0:D], ACT.Copy, "hn_drawn")
                    ready("qkv")
                    nc.scalar.activation(flat(qk[:]), Bk[:, 1, :], ACT.Copy)
                    run(v_sb[:], Bk[:, 2, 0:D], ACT.Copy, "qk_drawn")
                    ready("angles")
                    run(trig[:], ang_r[:], ACT.Sin, "trig_ready")
                    ready("m_turned")
                    run(flat(m_t[:]), flat(A[:, 0:2, :]), ACT.Copy, "m_drawn")
                    ready("m_picked")
                    run(m_sel[:], Bk[:, 0, 0:P], ACT.Copy, "m_sel_drawn")
                    ready("qk_turned")
                    run(flat(qk_t[:]), flat(A[:, 2:4, :]), ACT.Copy, "qk_t_drawn")
                    ready("shifted")
                    run(logits[:, :, 0:KSEL], logits[:, :, 0:KSEL], ACT.Exp, "exped")
                    ready("p_turned")
                    run(probs_t[0:KSEL, 8:16, :].rearrange("p a b -> p (a b)"), flat(Bk[0:KSEL, 2:4, :]), ACT.Copy, "p_hi")
                    ready("att_turned")
                    run(flat(att_t[:]), A[:, 1, 0:D], ACT.Copy, "att_drawn")
                    ready("ms2")
                    run(small[:, 4:5], small[:, 3:4], ACT.Sqrt, "dev4")
                    ready("h2_turned")
                    run(flat(h2_t[:]), A[:, 3, 0:D], ACT.Copy, "h2_drawn")
                    ready("up")
                    run(flat(g_t[:]), flat(Bk[:, 0:2, :]), ACT.Gelu_apprx_tanh, "gelu_ready")
                    ready("var5")
                    run(small[:, 7:8], small[:, 6:7], ACT.Sqrt, "dev5")

            @block.vector
            def _(dve):
                v = nc.vector
                setup = Chain(dve, sem("dve_setup"), 0, 0, 0)
                dve.wait_ge(const_set, 1)
                dve.wait_ge(const_in, 16 * CONST_LOADS)
                v.tensor_copy(slot[:], slot_i[:])
                v.tensor_copy(ext[:, :, 1], tok_i[:])
                setup.step(v.tensor_copy(base[:, 0, :], base_i[:]))
                v.tensor_scalar(base[:, 1, :], base[:, 0, :], float((MB - 1) * L), None, ALU.min)
                v.tensor_copy(pos_f[:], pos_i[:]).then_inc(setup_dve, 1)
                dve.wait_ge(setup_pe, 1)
                v.tensor_copy(flat(woa_t[:]), A[:, 0, :])
                for n in range(0, B, MB):
                    src = A[:, 1, 0:MB * LT].rearrange("p (b t) -> p b t", b=MB)
                    if n == 0:
                        setup.step(v.tensor_copy(pos[:, 0:MB, :], src))
                    else:
                        setup.step(v.tensor_copy(pos[:, n:n + MB, :], src[:, MB - 1:MB, :].broadcast_to([P, MB, LT])))
                v.tensor_copy(slot[:, 0:1], slot_i[:, 0:1]).then_inc(setup_dve, 1)
                dve.wait_ge(setup_dve, 2)

                with dve.Fori(0, B, 1) as b:
                    ready = lambda *names: [dve.wait_ge(S[n], b + 1) for n in names]
                    chain = Chain(dve, dve_step, 0, DVE_STEPS, b)
                    step = chain.step

                    def moments_of(src, n, name, eps, tiles=LT):
                        for t in range(tiles):
                            ins = v.bn_stats(stats[:, n, t, :], src[:, t, :])
                        step(ins)
                        v.memset(spread[:, n, :], 0.0)
                        for t in range(tiles):
                            ins = v.bn_aggr(moments[:, n, t, :], stats[:, n, t, :])
                        step(ins)
                        v.tensor_scalar(spread[:, n, :], moments[:, n, :, 1], eps, None, ALU.add).then_inc(S[name], 1)

                    ready("o_turned")
                    v.tensor_copy(o_t[:, 0, :], flat(A[:, 0:2, :])).then_inc(S["ot_lo"], 1)
                    ready("projected")
                    for n in range(4):
                        ins = v.tensor_tensor(mix[:, 2 * n:2 * n + 2, :], Bk[:, n, :].rearrange("p (a b) -> p a b", a=2),
                                              rows[:, 0, :].unsqueeze(1).broadcast_to([P, 2, D]), ALU.add)
                    step(ins)
                    moments_of(mix, 0, "var1", EPS_LN)
                    for t in range(LT):
                        ins = v.scalar_tensor_tensor(mix[:, t, :], mix[:, t, :], moments[:, 0, t, 0:1], rows[:, 1, :],
                                                     ALU.subtract, ALU.mult)
                    step(ins)
                    ready("dev1")
                    step(v.reciprocal(spread[:, 0, :], spread[:, 0, :]))
                    ready("xb_ready")
                    for t in range(LT):
                        ins = v.scalar_tensor_tensor(mix[:, t, :], mix[:, t, :], spread[:, 0, t:t + 1], x_in[:, t, :],
                                                     ALU.mult, ALU.add)
                    step(ins)
                    moments_of(mix, 1, "var2", EPS_LN)
                    ready("dev2")
                    step(v.reciprocal(spread[:, 1, :], spread[:, 1, :]))
                    for t in range(LT):
                        ins = v.tensor_scalar(x1[:, t, :], mix[:, t, :], moments[:, 1, t, 0:1], spread[:, 1, t:t + 1],
                                              ALU.subtract, ALU.mult)
                    step(ins)
                    for t in range(LT):
                        ins = v.tensor_tensor_reduce(out=dump[:, 0:D] if t == 0 else dump[:, 0:D], in0=x1[:, t, :],
                                                     in1=rows[:, 3, :], scale=1.0, scalar=0.0, op0=ALU.mult, op1=ALU.add,
                                                     accum_out=w_col[:, 0, t:t + 1])
                        step(ins)
                    step(v.tensor_scalar(w_col[:, 1, :], w_col[:, 0, :], r_bias[:, 0:1], None, ALU.add))
                    v.tensor_copy(ext[:, :, 0], w_col[:, 1, :])
                    v.tensor_copy(ext[:, :, 2], pos[:, bass.ds(b, 1), :].rearrange("p a t -> p (a t)"))
                    for t in range(LT):
                        ins = v.tensor_scalar(w_diag[:, t, :], ident[:], w_col[:, 1, t:t + 1], None, ALU.mult)
                    ins.then_inc(S["diag_w"], 1)
                    ready("w_drawn")
                    step(v.memset(ahead[:, 0, 0:1], 0.0))
                    for t in range(LT):
                        mine = w_col[:, 1, t:t + 1]
                        if t:
                            step(v.tensor_scalar(dump[:, 0:t * P], w_row[:, 0:t * P], mine, None, ALU.is_ge, ALU.add,
                                                 accum_out=ahead[:, t, 0:1]))
                        step(v.tensor_scalar(dump[:, t * P:L], w_row[:, t * P:L], mine, None, ALU.is_gt, ALU.add,
                                             accum_out=ahead[:, t, 1:2]))
                        step(v.scalar_tensor_tensor(dump[:, 0:P], w_row[:, t * P:(t + 1) * P], mine, tri[:],
                                                    ALU.is_equal, ALU.mult, accum_out=ahead[:, t, 2:3]))
                    step(v.tensor_reduce(rank[:], ahead[:], AX.X, ALU.add))
                    for t in range(LT):
                        ins = v.tensor_scalar(one_hot[:, t, :], slot[:], rank[:, t:t + 1], None, ALU.is_equal)
                    ins.then_inc(S["hot"], 1)
                    moments_of(x1, 2, "dense_var", EPS_LN / 4)
                    ready("gathered")
                    step(v.tensor_copy(ext_s[:], A[:, 3, 0:3]))
                    v.tensor_scalar(where[:, 0:1], ext_s[:, 1:2], base[:, 0, bass.ds(b, 1)], None, ALU.add)
                    v.tensor_scalar(where[:, 1:2], ext_s[:, 1:2], base[:, 1, bass.ds(b, 1)], None, ALU.add).then_inc(S["token_ready"], 1)
                    step(v.tensor_copy(xs[:], A[:, 2, 0:D]))
                    step(v.tensor_tensor_reduce(out=dump[:, 0:D], in0=xs[:], in1=xs[:], scale=1.0 / D, scalar=0.0,
                                                op0=ALU.mult, op1=ALU.add, accum_out=small[:, 2:3]))
                    v.tensor_scalar(small[:, 0:1], small[:, 2:3], EPS_RMS, None, ALU.add).then_inc(S["ms1"], 1)
                    ready("dev3")
                    step(v.reciprocal(small[:, 5:6], small[:, 1:2]))
                    v.scalar_tensor_tensor(hn[:], xs[:], small[:, 5:6], rows[:, 4, :], ALU.mult, ALU.mult).then_inc(S["normed1"], 1)
                    ready("dense_dev")
                    step(v.reciprocal(spread[:, 2, :], spread[:, 2, :]))
                    for t in range(LT):
                        ins = v.tensor_scalar(dense[:, t, :], x1[:, t, :], moments[:, 2, t, 0:1], spread[:, 2, t:t + 1],
                                              ALU.subtract, ALU.mult)
                    ins.then_inc(S["dense_ready"], 1)
                    step(v.tensor_scalar(ang[:, 0, :], inv_freq[:], ext_s[:, 2:3], None, ALU.mult))
                    step(v.tensor_scalar(ang[:, 1, :], ang[:, 0, :], 1.0 / TWO_PI, ROUND, ALU.mult, ALU.add))
                    step(v.tensor_scalar(ang[:, 2, :], ang[:, 1, :], ROUND, None, ALU.subtract))
                    step(v.scalar_tensor_tensor(ang[:, 3, :], ang[:, 2, :], -C1, ang[:, 0, :], ALU.mult, ALU.add))
                    step(v.scalar_tensor_tensor(ang[:, 1, :], ang[:, 2, :], -C2, ang[:, 3, :], ALU.mult, ALU.add))
                    step(v.tensor_scalar(ang_r[:, 0, :], ang[:, 1, :], PI_IN, -PI_IN, ALU.min, ALU.max))
                    step(v.scalar_tensor_tensor(ang[:, 2, :], ang_r[:, 0, :], -1.0, ang_r[:, 0, :], ALU.mult, ALU.max))
                    v.tensor_scalar(ang_r[:, 1, :], ang[:, 2, :], -1.0, float(np.pi / 2), ALU.mult, ALU.add).then_inc(S["angles"], 1)
                    ready("qk_drawn", "trig_ready")
                    halves = lambda t: t[:].rearrange("p h (s f) -> p h s f", s=2)
                    cos, sin = (trig[:, n, :].unsqueeze(1).broadcast_to([P, 2 * H, NROT]) for n in (1, 0))
                    q2, a2, b2 = halves(qk), halves(rot_a), halves(rot_b)
                    for s in range(2):
                        v.tensor_tensor(a2[:, :, s, :], q2[:, :, s, :], cos, ALU.mult)
                        ins = v.tensor_tensor(b2[:, :, s, :], q2[:, :, 1 - s, :], sin, ALU.mult)
                    step(ins)
                    v.tensor_tensor(qk_pad[:, :, 0:NROT], a2[:, :, 0, :], b2[:, :, 0, :], ALU.subtract)
                    v.tensor_tensor(qk_pad[:, :, NROT:HD], a2[:, :, 1, :], b2[:, :, 1, :], ALU.add).then_inc(S["padded"], 1)
                    ready("thr_ready")
                    step(v.tensor_scalar(small[:, 8:9], ext_s[:, 0:1], Bk[:, 3, 0:1], -1.0, ALU.is_gt, ALU.mult))
                    step(v.tensor_scalar(small[:, 9:10], small[:, 8:9], 2.0, None, ALU.add))
                    ready("scored", "m_sel_drawn")
                    for r in range(QH):
                        ins = v.scalar_tensor_tensor(logits[:, 4 * r:4 * r + 4, :], A[:, r, :].rearrange("p (a b) -> p a b", a=4),
                                                     1.0 / float(np.sqrt(HD)), m_sel[:].unsqueeze(1).broadcast_to([P, 4, P]),
                                                     ALU.mult, ALU.add)
                    step(ins)
                    step(v.tensor_reduce(peak[:], logits[:, :, 0:KSEL], AX.X, ALU.max))
                    v.tensor_tensor(logits[:, :, 0:KSEL], logits[:, :, 0:KSEL], peak[:].unsqueeze(2).broadcast_to([P, H, KSEL]),
                                    ALU.subtract).then_inc(S["shifted"], 1)
                    ready("exped")
                    step(v.tensor_reduce(total[:], logits[:, :, 0:KSEL], AX.X, ALU.add))
                    step(v.reciprocal(inv_total[:].rearrange("p (n r) -> p r n", r=QH), total[:].rearrange("p (r n) -> p r n", r=QH)))
                    ready("p_turned")
                    v.tensor_copy(probs_t[0:KSEL, 0:8, :].rearrange("p a b -> p (a b)"), flat(Bk[0:KSEL, 0:2, :])).then_inc(S["p_lo"], 1)
                    ready("attended")
                    v.tensor_tensor(att[:].rearrange("p (h d) -> p h d", d=HD), A[:, 0, 0:D].rearrange("p (h d) -> p h d", d=HD),
                                    inv_total[:].unsqueeze(2).broadcast_to([P, H, HD]), ALU.mult).then_inc(S["att_ready"], 1)
                    ready("mixed")
                    step(v.tensor_tensor(xa[:], A[:, 2, 0:D], xs[:], ALU.add))
                    step(v.tensor_tensor_reduce(out=dump[:, 0:D], in0=xa[:], in1=xa[:], scale=1.0 / D, scalar=0.0,
                                                op0=ALU.mult, op1=ALU.add, accum_out=small[:, 10:11]))
                    v.tensor_scalar(small[:, 3:4], small[:, 10:11], EPS_RMS, None, ALU.add).then_inc(S["ms2"], 1)
                    ready("dev4")
                    step(v.reciprocal(small[:, 11:12], small[:, 4:5]))
                    v.scalar_tensor_tensor(h2[:], xa[:], small[:, 11:12], rows[:, 5, :], ALU.mult, ALU.mult).then_inc(S["normed2"], 1)
                    ready("down")
                    step(v.tensor_tensor(xm[:], Bk[:, 2, 0:D], xa[:], ALU.add))
                    step(v.tensor_scalar(xm[:], xm[:], ext_s[:, 0:1], None, ALU.mult))
                    step(v.scalar_tensor_tensor(ys[:], xs[:], small[:, 9:10], xm[:], ALU.mult, ALU.add))
                    step(v.bn_stats(stats[:, 0, 0, :], ys[:]))
                    v.memset(small[:, 6:7], 0.0)
                    step(v.bn_aggr(moments[:, 0, 0, :], stats[:, 0, 0, :]))
                    v.tensor_scalar(small[:, 6:7], moments[:, 0, 0, 1:2], EPS_LN, None, ALU.add).then_inc(S["var5"], 1)
                    ready("dev5")
                    step(v.reciprocal(small[:, 12:13], small[:, 7:8]))
                    v.tensor_scalar(res[:], ys[:], moments[:, 0, 0, 0:1], small[:, 12:13], ALU.subtract, ALU.mult).then_inc(S["res_ready"], 1)
                    chain.close()


DVE_STEPS = 74
CONST_LOADS = 15

_INS = [f"L0_attn_{n}" for n in "x Wq bq Wk bk Wv bv Wo bo alpha phi temperature gamma beta".split()] + \
       [f"L0_ffn_{n}" for n in "attention_mask position_ids router_w router_b wq wk wv wo w1 w2 ln1 ln2".split()]


def build(nc, t, out):
    scratch = lambda n, s, d=FP32: nc.dram_tensor(n, s, d, kind="Internal").ap()
    q_d, k_d = scratch("q_d", [B, PARTS, D, L], BF16), scratch("k_d", [B, PARTS, D, L], BF16)
    v_d, o_d = scratch("v_d", [B, P, LT, D]), scratch("o_d", [B, P, LT, D])
    a = lambda n: t[f"L0_attn_{n}"]
    f = lambda n: t[f"L0_ffn_{n}"]
    project_qkv(nc, a("x"), a("Wq"), a("bq"), a("Wk"), a("bk"), a("Wv"), a("bv"), a("temperature"), q_d, k_d, v_d)
    oscillatory_attention(nc, a("alpha"), a("phi"), q_d, k_d, v_d, o_d)
    routed_block(nc, a("x"), o_d, a("Wo"), a("bo"), a("gamma"), a("beta"), f("attention_mask"), f("position_ids"),
                 f("router_w"), f("router_b"), f("wq"), f("wk"), f("wv"), f("wo"), f("w1"), f("w2"), f("ln1"), f("ln2"), out)


def kernel(**inputs):
    import concourse.bacc as bacc
    from concourse.bass_utils import run_bass_kernel_spmd

    nc = bacc.Bacc("TRN2", target_bir_lowering=False, num_devices=1)
    arrays, t = {}, {}
    for name in _INS:
        v = np.ascontiguousarray(inputs[name])
        arrays[f"in_{name}"] = v
        t[name] = nc.dram_tensor(f"in_{name}", v.shape, mybir.dt.from_np(v.dtype), kind="ExternalInput").ap()
    out = nc.dram_tensor("out_0", (B, L, D), FP32, kind="ExternalOutput").ap()
    build(nc, t, out)
    r = run_bass_kernel_spmd(nc, [arrays], core_ids=[0])
    return r.results[0]["out_0"]
```

```python
import numpy as np
import concourse.bass as bass
from concourse import mybir
from contextlib import ExitStack

FP32 = mybir.dt.float32
BF16 = mybir.dt.bfloat16
I32 = mybir.dt.int32
ALU = mybir.AluOpType
ACT = mybir.ActivationFunctionType
AX = mybir.AxisListType

B, L, D = 8, 1024, 256
H, HD = 16, 16
P = 128
LT = L // P
KC = D // P
HALF = 512
FREQS = [31.0, 37.0, 41.0, 43.0, 47.0]
NF = len(FREQS)
TWO_PI = 2.0 * float(np.pi)
FRAC = 22
TURN = float(2 ** FRAC)
WRAP = 32 - FRAC
ANGLE = float(np.nextafter(np.float32(TWO_PI / TURN), np.float32(0)))

F = 1024
FB = F // P
MB = 4
CAP = L // 8
KSEL = CAP - 1
ROPE_BASE = 10000.0
NROT = HD // 2
EPS_LN = 1e-5
EPS_RMS = 1e-6
EPS_DEN = 1e-10

PARTS = 3
TERMS = [(i, j) for j in range(PARTS) for i in range(PARTS)][:8]
FOURTH = [1, 0, 0, 1, 0, 0, 0, 0]
ACT_TURNS = [1024] * 8
VP = 32
GROUPS = P // VP
SHIFTS = ALU.logical_shift_left, ALU.arith_shift_right
RING = 4
HEADS = B * H
VW = HD + 1


class Chain:

    def __init__(self, eng, sem, base, per_turn, turn):
        self.eng, self.sem, self.base, self.per_turn, self.turn, self.n = eng, sem, base, per_turn, turn, 0

    def step(self, ins):
        self.n += 1
        ins.then_inc(self.sem, 1)
        self.eng.wait_ge(self.sem, self.base + self.turn * self.per_turn + self.n)

    def close(self):
        assert self.n == self.per_turn, (self.n, self.per_turn)


def wait_pos(eng, sem, value):
    if not isinstance(value, int) or value > 0:
        eng.wait_ge(sem, value)


def project_qkv(nc, x, wq, bq, wk, bk, wv, bv, temperature, q_d, k_d, v_d):
    with ExitStack() as ctx:
        sb = lambda n, s, d=FP32: ctx.enter_context(nc.sbuf_tensor(n, s, d))
        sem = lambda n: ctx.enter_context(nc.semaphore(n))
        ident = sb("p_ident", [P, P])
        w_in = sb("p_w_in", [P, 3, KC, D])
        w_t = sb("p_w_t", [P, 3, KC, D])
        bias_qk = sb("p_bias_qk", [P, 2, KC])
        bv_row = sb("p_bv_row", [P, D])
        temp = sb("p_temp", [P, 5])
        x_in = sb("p_x_in", [P, 2, LT, D])
        x_t = sb("p_x_t", [P, KC, L])
        qk_sb = sb("p_qk_sb", [P, 2, KC, L])
        rest = sb("p_rest", [P, 2, 2, KC, L])
        parts = sb("p_parts", [P, 2, PARTS, KC, L], BF16)
        v_sb = sb("p_v_sb", [P, LT, D])
        lo = ctx.enter_context(nc.psum_tensor("p_lo", [P, 4, HALF], FP32))
        hi = ctx.enter_context(nc.psum_tensor("p_hi", [P, 4, HALF], FP32))
        w_loaded, b_loaded, ident_zero, ident_done = sem("w_loaded"), sem("b_loaded"), sem("p_id0"), sem("p_id1")
        w_turned, w_ready, temp_step = sem("w_turned"), sem("w_ready"), sem("temp_step")
        x_loaded = [sem("x_loaded0"), sem("x_loaded1")]
        x_turned, x_drawn = sem("x_turned"), sem("x_drawn")
        q_summed, k_summed, v_summed = sem("q_summed"), sem("k_summed"), sem("v_summed")
        q_ready, k_ready, v_ready = sem("q_ready"), sem("k_ready"), sem("v_ready")
        q_kept, k_kept, v_kept = sem("q_kept"), sem("k_kept"), sem("v_kept")
        q_split, k_split, split_step = sem("q_split"), sem("k_split"), sem("split_step")

        with nc.Block() as block:

            @block.sync
            def _(sp):
                for n, w in enumerate((wq, wk, wv)):
                    sp.dma_start(w_in[:, n, :, :], w.rearrange("(m p) i -> p m i", p=P)).then_inc(w_loaded, 16)
                sp.dma_start(bias_qk[:, 0, :], bq.rearrange("(m p) -> p m", p=P), allow_slow_non_contiguous=True).then_inc(b_loaded, 16)
                sp.dma_start(bias_qk[:, 1, :], bk.rearrange("(m p) -> p m", p=P), allow_slow_non_contiguous=True).then_inc(b_loaded, 16)
                sp.dma_start(bv_row[:], bv.partition_broadcast(P)).then_inc(b_loaded, 16)
                sp.dma_start(temp[:, 0:1], temperature.partition_broadcast(P)).then_inc(b_loaded, 16)
                sp.sem_inc(q_kept, 16)
                sp.sem_inc(k_kept, 16)
                sp.sem_inc(v_kept, 16)

                def load(b, k):
                    sp.dma_start(x_in[:, k, :, :], x[b, :, :].rearrange("(t p) d -> p t d", p=P)).then_inc(x_loaded[k], 16)

                def keep(b):
                    sp.wait_ge(q_split, b + 1)
                    sp.dma_start(q_d[b, :, :, :].rearrange("i (m p) l -> p (i m) l", p=P),
                                 parts[:, 0, :, :, :].rearrange("p i m l -> p (i m) l")).then_inc(q_kept, 16)
                    sp.wait_ge(v_ready, b + 2)
                    sp.dma_start(v_d[b, :, :, :], v_sb[:]).then_inc(v_kept, 16)
                    sp.wait_ge(k_split, b + 2)
                    sp.dma_start(k_d[b, :, :, :].rearrange("i (m p) l -> p (i m) l", p=P),
                                 parts[:, 1, :, :, :].rearrange("p i m l -> p (i m) l")).then_inc(k_kept, 16)

                load(0, 0)
                load(1, 1)
                with sp.Fori(0, B // 2 - 1, 1) as pair:
                    for k in range(2):
                        sp.wait_ge(x_turned, 2 * pair + k + 2)
                        load(2 * pair + k + 2, k)
                        keep(2 * pair + k)
                keep(B - 2)
                keep(B - 1)
                sp.wait_ge(q_kept, 16 * (B + 1))
                sp.wait_ge(k_kept, 16 * (B + 1))
                sp.wait_ge(v_kept, 16 * B + 16)

            @block.gpsimd
            def _(pool):
                nc.gpsimd.memset(ident[:], 0.0).then_inc(ident_zero, 1)
                pool.wait_ge(ident_zero, 1)
                nc.gpsimd.affine_select(out=ident[:], in_=ident[:], compare_op=ALU.not_equal, fill=1.0, base=0,
                                        pattern=[[-1, P]], channel_multiplier=1).then_inc(ident_done, 1)

            @block.tensor
            def _(pe):
                pe.sem_inc(x_turned, 1)
                pe.sem_inc(v_summed, 1)
                pe.wait_ge(ident_done, 1)
                pe.wait_ge(w_loaded, 48)
                for n in range(3):
                    for i in range(KC):
                        for m in range(KC):
                            last = nc.tensor.transpose(lo[:, n, i * D + m * P:i * D + (m + 1) * P],
                                                       w_in[:, n, m, i * P:(i + 1) * P], ident[:])
                last.then_inc(w_turned, 1)
                pe.wait_ge(w_ready, 1)

                with pe.Fori(0, B // 2, 1) as pair:
                    for k in range(2):
                        b = 2 * pair + k
                        pe.wait_ge(x_loaded[k], 16 * pair + 16)
                        pe.wait_ge(k_ready, b + 1)
                        for c in range(KC):
                            for t in range(LT):
                                last = nc.tensor.transpose(
                                    lo[:, 2 * c + t // 4, (t % 4) * P:(t % 4 + 1) * P],
                                    x_in[:, k, t, c * P:(c + 1) * P], ident[:])
                        last.then_inc(x_turned, 1)
                        pe.wait_ge(x_drawn, b + 1)
                        pe.wait_ge(v_ready, b + 1)
                        for n, out, done in ((0, hi, q_summed), (1, lo, k_summed)):
                            for m in range(KC):
                                for half in range(2):
                                    for c in range(KC):
                                        last = nc.tensor.matmul(
                                            out[:, 2 * m + half, :], w_t[:, n, c, m * P:(m + 1) * P],
                                            x_t[:, c, half * HALF:(half + 1) * HALF],
                                            start=(c == 0), stop=(c == KC - 1))
                            last.then_inc(done, 1)
                        pe.wait_ge(q_ready, b + 1)
                        for t in range(LT):
                            for c in range(KC):
                                last = nc.tensor.matmul(hi[:, t // 2, (t % 2) * D:(t % 2 + 1) * D],
                                                        x_t[:, c, t * P:(t + 1) * P], w_t[:, 2, c, :],
                                                        start=(c == 0), stop=(c == KC - 1))
                        last.then_inc(v_summed, 1)

            @block.vector
            def _(dve):
                dve.sem_inc(v_ready, 1)
                dve.sem_inc(k_split, 1)
                dve.wait_ge(b_loaded, 64)
                nc.vector.scalar_tensor_tensor(temp[:, 1:2], temp[:, 0:1], -1.0, temp[:, 0:1], ALU.mult,
                                               ALU.max).then_inc(temp_step, 1)
                dve.wait_ge(temp_step, 1)
                nc.vector.tensor_scalar(temp[:, 4:5], temp[:, 1:2], 0.1, None, ALU.add).then_inc(temp_step, 1)
                dve.wait_ge(temp_step, 2)
                nc.vector.reciprocal(temp[:, 2:3], temp[:, 4:5]).then_inc(temp_step, 1)
                dve.wait_ge(temp_step, 3)
                nc.vector.tensor_scalar(temp[:, 3:4], temp[:, 2:3], 1.0 / float(np.sqrt(HD)), None,
                                        ALU.mult).then_inc(temp_step, 1)
                dve.wait_ge(w_turned, 1)
                nc.vector.tensor_copy(w_t[:].rearrange("p a b c -> p (a b c)"),
                                      lo[:, 0:3, :].rearrange("p a b -> p (a b)")).then_inc(w_ready, 1)
                dve.wait_ge(temp_step, 4)

                def split_in_parts(split, n, done):
                    flat = lambda ap: ap.rearrange("p m l -> p (m l)")
                    whole = qk_sb[:, n, :, :]
                    for i in range(PARTS):
                        ins = nc.vector.tensor_copy(flat(parts[:, n, i, :, :]), flat(whole))
                        if i == PARTS - 1:
                            ins.then_inc(done, 1)
                            break
                        split.step(ins)
                        left = rest[:, n, i, :, :]
                        split.step(nc.vector.tensor_tensor(flat(left), flat(whole), flat(parts[:, n, i, :, :]), ALU.subtract))
                        whole = left

                with dve.Fori(0, B, 1) as b:
                    dve.wait_ge(q_summed, b + 1)
                    dve.wait_ge(k_split, b + 1)
                    for m in range(KC):
                        last = nc.vector.tensor_scalar(
                            qk_sb[:, 0, m, :], hi[:, 2 * m:2 * m + 2, :].rearrange("p a b -> p (a b)"),
                            bias_qk[:, 0, m:m + 1], temp[:, 3:4], ALU.add, ALU.mult)
                    last.then_inc(q_ready, 1)
                    split = Chain(dve, split_step, 0, 2 * 2 * (PARTS - 1), b)
                    dve.wait_ge(q_ready, b + 1)
                    dve.wait_ge(q_kept, 16 * (b + 1))
                    split_in_parts(split, 0, q_split)
                    dve.wait_ge(v_summed, b + 2)
                    dve.wait_ge(v_kept, 16 * b + 16)
                    for n in range(4):
                        last = nc.vector.tensor_tensor(
                            v_sb[:, 2 * n:2 * n + 2, :], hi[:, n, :].rearrange("p (a b) -> p a b", a=2),
                            bv_row[:].unsqueeze(1).broadcast_to([P, 2, D]), ALU.add)
                    last.then_inc(v_ready, 1)
                    dve.wait_ge(k_ready, b + 2)
                    dve.wait_ge(k_kept, 16 * (b + 1))
                    split_in_parts(split, 1, k_split)
                    split.close()

            @block.scalar
            def _(act):
                act.sem_inc(k_ready, 1)
                act.wait_ge(b_loaded, 64)
                with act.Fori(0, B, 1) as b:
                    act.wait_ge(x_turned, b + 2)
                    act.wait_ge(v_summed, b + 1)
                    nc.scalar.activation(x_t[:].rearrange("p c l -> p (c l)"), lo[:].rearrange("p a b -> p (a b)"),
                                         ACT.Copy).then_inc(x_drawn, 1)
                    act.wait_ge(k_summed, b + 1)
                    act.wait_ge(k_split, b + 1)
                    for m in range(KC):
                        last = nc.scalar.activation(
                            qk_sb[:, 1, m, :], lo[:, 2 * m:2 * m + 2, :].rearrange("p a b -> p (a b)"),
                            ACT.Identity, bias=bias_qk[:, 1, m:m + 1])
                    last.then_inc(k_ready, 1)


def oscillatory_attention(nc, alpha, phi, q_d, k_d, v_d, o_d):
    U = LT
    with ExitStack() as ctx:
        sb = lambda n, s, d=FP32: ctx.enter_context(nc.sbuf_tensor(n, s, d))
        ps = lambda n, s: ctx.enter_context(nc.psum_tensor(n, s, FP32))
        sem = lambda n: ctx.enter_context(nc.semaphore(n))
        ident = sb("a_ident", [P, P])
        table = sb("a_table", [P, 2, H, NF])
        table_i = sb("a_table_i", [P, H, NF], I32)
        head_c = sb("a_head_c", [P, 2, 2, NF])
        diag = sb("a_diag", [P, 2, NF - 1, P])
        q_r = sb("a_q_r", [P, 2, L], BF16)
        k_r = sb("a_k_r", [P, 2, L], BF16)
        v_r = sb("a_v_r", [P, 2, LT, VP])
        fold = sb("a_fold", [P, 3, VW])
        ones = sb("a_ones", [P, P])
        one_set = sb("a_one_set", [P, 1])
        v_part = sb("a_v_part", [P, 2, 7, HD])
        v_sum = sb("a_v_sum", [P, HD])
        early = sb("a_early", [P, 2, L], I32)
        score = sb("a_score", [P, 2, L])
        turn = sb("a_turn", [P, RING, NF, L], I32)
        weight = sb("a_weight", [P, LT, L])
        num = sb("a_num", [P, L])
        den = sb("a_den", [P, 2, LT])
        raised = sb("a_raised", [P, LT, HD])
        out = sb("a_out", [P, 2, LT, HD])
        ps_score = ps("a_ps_score", [P, L])
        ps_sum = ps("a_ps_sum", [P, 2, L])
        ps_out = ps("a_ps_out", [P, L])

        table_in, table_step, setup, id_zero = sem("table_in"), sem("table_step"), sem("a_setup"), sem("a_id_zero")
        qk_loaded = [sem("qk_loaded0"), sem("qk_loaded1")]
        v_loaded = [sem("v_loaded0"), sem("v_loaded1")]
        const_ready, diag_ready = sem("const_ready"), sem("diag_ready")
        scored, drawn, scaled, wrapped = sem("scored"), sem("drawn"), sem("scaled"), sem("wrapped")
        sines = sem("sines")
        part_summed, summed, sum_step = sem("part_summed"), sem("summed"), sem("sum_step")
        squashed, weighted, num_drawn, turned = sem("squashed"), sem("weighted"), sem("num_drawn"), sem("turned")
        v_step, v_parted = sem("v_step"), sem("v_parted")
        norm_step, normed = sem("norm_step"), sem("normed")
        stored = [sem("stored0"), sem("stored1")]

        def heads_of(eng, body):
            for g in range(4):
                body(g, g % 2)
            with eng.Fori(2, HEADS // 2 - 1, 1) as pair:
                for k in range(2):
                    body(2 * pair + k, k)
            for g in range(HEADS - 2, HEADS + 1):
                body(g, g % 2)

        LOADS = 16 * 2 * PARTS
        SUM_STEPS = U - sum(FOURTH)
        next_loads = lambda g, k: LOADS // 2 * g + (LOADS if k == 0 else LOADS // 2 * 3)
        v_loads = lambda g, k: 8 * g + (16 if k == 0 else 8)
        main = lambda g: not isinstance(g, int) or g < HEADS
        after = lambda g: not isinstance(g, int) or g >= 1
        unit_in = lambda n: not isinstance(n, int) or n < HEADS * U

        with nc.Block() as block:

            @block.sync
            def _(sp):
                sp.dma_start(table[:, 0, :, :].rearrange("p h f -> p (h f)"),
                             alpha.rearrange("h f -> (h f)").partition_broadcast(P)).then_inc(table_in, 16)
                sp.dma_start(table[:, 1, :, :].rearrange("p h f -> p (h f)"),
                             phi.rearrange("h f -> (h f)").partition_broadcast(P)).then_inc(table_in, 16)

                def load(g, k):
                    wait_pos(sp, scored, (g - 1) * U)
                    dims = bass.ds((g % H) * HD, HD)
                    for j in range(PARTS):
                        many = sum(term[1] == j for term in TERMS)
                        rows = slice(HD * PARTS * j, HD * (PARTS * j + many))
                        sp.dma_start(q_r[rows, k, :], q_d[g // H, 0:many, dims, :]).then_inc(qk_loaded[k], 16)
                        sp.dma_start(k_r[rows, k, :], k_d[g // H, j:j + 1, dims, :].broadcast_to(
                            [many, HD, L])).then_inc(qk_loaded[k], 16)
                    wait_pos(sp, turned, g - 1)
                    sp.dma_start(v_r[:, k, :, 0:HD], v_d[g // H, :, :, bass.ds((g % H) * HD, HD)]).then_inc(v_loaded[k], 16)

                def store(g, k):
                    sp.wait_ge(normed, g)
                    sp.dma_start(o_d[(g - 1) // H, :, :, bass.ds(((g - 1) % H) * HD, HD)],
                                 out[:, 1 - k, :, :]).then_inc(stored[1 - k], 16)

                sp.wait_ge(setup, 3)
                load(0, 0)

                def body(g, k):
                    if not isinstance(g, int) or g + 1 < HEADS:
                        load(g + 1, 1 - k)
                    if after(g):
                        store(g, k)
                heads_of(sp, body)
                for k in range(2):
                    sp.wait_ge(stored[k], 16 * HEADS // 2)

            @block.gpsimd
            def _(pool):
                nc.gpsimd.memset(ident[:], 0.0).then_inc(id_zero, 1)
                nc.gpsimd.memset(ones[:], 1.0).then_inc(setup, 1)
                nc.gpsimd.memset(v_r[:].rearrange("p a b c -> p (a b c)"), 0.0).then_inc(id_zero, 1)
                pool.wait_ge(id_zero, 2)
                nc.gpsimd.memset(v_r[:, :, :, HD], 1.0).then_inc(setup, 1)
                nc.gpsimd.affine_select(out=ident[:], in_=ident[:], compare_op=ALU.not_equal, fill=1.0, base=0,
                                        pattern=[[-1, P]], channel_multiplier=1).then_inc(setup, 1)
                pool.wait_ge(setup, 3)
                group = lambda n: ident[:, VP * n:VP * n + VW]
                for n in range(2):
                    nc.gpsimd.tensor_tensor(fold[:, n, :], group(2 * n), group(2 * n + 1), ALU.add).then_inc(setup, 1)
                pool.wait_ge(setup, 5)
                nc.gpsimd.tensor_tensor(fold[:, 2, :], fold[:, 0, :], fold[:, 1, :], ALU.add).then_inc(setup, 1)
                pool.wait_ge(table_step, 3)

                def constants(g, k):
                    wait_pos(pool, summed, (g - 1) * U)
                    h = g % H
                    nc.gpsimd.tensor_copy(head_c[:, k, :, :], table[:, :, bass.ds(h, 1), :].rearrange(
                        "p a h f -> p a (h f)")).then_inc(const_ready, 1)
                    pool.wait_ge(const_ready, g + 1)
                    for f in range(NF - 1):
                        last = nc.gpsimd.tensor_tensor(diag[:, k, f, :], ident[:],
                                                       head_c[:, k, 0, f:f + 1].broadcast_to([P, P]), ALU.mult)
                    last.then_inc(diag_ready, 1)

                constants(0, 0)

                def body(g, k):
                    if main(g):
                        pool.wait_ge(v_loaded[k], v_loads(g, k))
                        wait_pos(pool, turned, g - 1)
                        part = v_part[:, k, :, :]
                        nc.gpsimd.tensor_tensor(part[:, 0:4, :], v_r[:, k, 0:4, 0:HD], v_r[:, k, 4:8, 0:HD],
                                                ALU.add).then_inc(v_step, 1)
                        pool.wait_ge(v_step, 2 * g + 1)
                        nc.gpsimd.tensor_tensor(part[:, 4:6, :], part[:, 0:2, :], part[:, 2:4, :], ALU.add).then_inc(v_step, 1)
                        pool.wait_ge(v_step, 2 * g + 2)
                        nc.gpsimd.tensor_tensor(part[:, 6, :], part[:, 4, :], part[:, 5, :], ALU.add).then_inc(v_parted, 1)
                    if not isinstance(g, int) or g + 1 < HEADS:
                        constants(g + 1, 1 - k)
                heads_of(pool, body)

            @block.tensor
            def _(pe):
                def scores(n, s, k):
                    wait_pos(pe, drawn, n)
                    for half in range(2):
                        last = nc.tensor.matmul(ps_score[:, half * HALF:(half + 1) * HALF], k_r[:, k, s * P:(s + 1) * P],
                                                q_r[:, k, half * HALF:(half + 1) * HALF], start=True, stop=True)
                    last.then_inc(scored, 1)

                def sum_sines(n, s, k, half):
                    if half == 0:
                        pe.wait_ge(sines, n + 1)
                        wait_pos(pe, summed, n - 1)
                    sines_here = NF - 1 if half == 0 or FOURTH[s] else NF - 2
                    for f in range(sines_here):
                        last = nc.tensor.matmul(
                            ps_sum[:, s % 2, half * HALF:(half + 1) * HALF], diag[:, k, f, :],
                            turn[:, s % RING, f, half * HALF:(half + 1) * HALF].bitcast(FP32),
                            start=(f == 0), stop=(f == sines_here - 1))
                    if half:
                        last.then_inc(part_summed, 1)

                def times_v(part, k):
                    for half in range(2):
                        for j in range(GROUPS * part, GROUPS * (part + 1)):
                            at = VP * (j % GROUPS)
                            last = nc.tensor.matmul(
                                ps_out[at:at + VP, half * HALF:(half + 1) * HALF], v_r[:, k, j, :],
                                weight[:, j, half * HALF:(half + 1) * HALF], start=(part == 0), stop=(part == 1))
                    last.then_inc(weighted, 1)

                pe.wait_ge(setup, 6)
                pe.wait_ge(qk_loaded[0], LOADS)
                scores(0, 0, 0)
                scores(1, 1, 0)
                scores(2, 2, 0)

                def body(g, k):
                    n0 = g * U
                    for s in range(U):
                        n = n0 + s
                        if s == 3 and after(g):
                            pe.wait_ge(squashed, n0)
                            times_v(1, 1 - k)
                        if s == 5 and after(g):
                            pe.wait_ge(num_drawn, g)
                            for t in range(LT):
                                nc.tensor.matmul(ps_out[:, t * VW:(t + 1) * VW], num[:, t * P:(t + 1) * P],
                                                 fold[:, 2, :], start=True, stop=True)
                            pe.wait_ge(v_parted, g)
                            nc.tensor.matmul(ps_out[:, LT * VW:LT * VW + HD], ones[:], v_part[:, 1 - k, 6, :],
                                             start=True, stop=True).then_inc(turned, 1)
                        if s == U - 1 and main(g):
                            pe.wait_ge(squashed, n0 + GROUPS)
                            pe.wait_ge(v_loaded[k], v_loads(g, k))
                            wait_pos(pe, normed, g)
                            times_v(0, k)
                        for half in range(2):
                            if s > 0 and main(g):
                                if s == 1 and half == 0:
                                    pe.wait_ge(diag_ready, g + 1)
                                sum_sines(n - 1, s - 1, k, half)
                            if s == 0 and after(g):
                                sum_sines(n - 1, U - 1, 1 - k, half)
                            if half == 0 and main(g) and unit_in(n + 3):
                                if s == U - 3:
                                    pe.wait_ge(qk_loaded[1 - k], next_loads(g, k))
                                scores(n + 3, (s + 3) % U, k if s < U - 3 else 1 - k)

                heads_of(pe, body)

            @block.scalar
            def _(act):
                def draw(n, s, g, k):
                    act.wait_ge(scored, n + 1)
                    wait_pos(act, scaled, n - 1)
                    copied = nc.scalar.activation(score[:, s % 2, :], ps_score[:], ACT.Copy)
                    if ACT_TURNS[s]:
                        if s == 0:
                            act.wait_ge(const_ready, g + 1)
                        wait_pos(act, wrapped, n - 1)
                        copied = nc.scalar.activation(
                            early[:, s % 2, L - ACT_TURNS[s]:L], ps_score[:, L - ACT_TURNS[s]:L], ACT.Identity,
                            bias=head_c[:, k, 1, NF - 1:NF], scale=TURN / FREQS[NF - 1])
                    copied.then_inc(drawn, 1)

                act.wait_ge(setup, 3)
                nc.scalar.activation(one_set[:], ones[:, 0:1], ACT.Silu)
                draw(0, 0, 0, 0)
                draw(1, 1, 0, 0)

                def body(g, k):
                    for s in range(U):
                        n = g * U + s
                        if s == 4 and after(g):
                            act.wait_ge(weighted, 2 * g)
                            wait_pos(act, turned, g - 1)
                            nc.scalar.activation(num[:], ps_out[:], ACT.Copy).then_inc(num_drawn, 1)
                        if (s >= 3 and main(g)) or (s < 3 and after(g)):
                            act.wait_ge(summed, n - 2)
                            nc.scalar.activation(weight[:, (s - 3) % U, :], weight[:, (s - 3) % U, :], ACT.Tanh,
                                                 scale=0.5).then_inc(squashed, 1)
                        if main(g):
                            if unit_in(n + 2):
                                if s < U - 2:
                                    draw(n + 2, s + 2, g, k)
                                else:
                                    draw(n + 2, s + 2 - U, g + 1, 1 - k)
                            act.wait_ge(wrapped, n + 1)
                            nc.scalar.activation(turn[:, s % RING, :, :].bitcast(FP32), turn[:, s % RING, :, :],
                                                 ACT.Sin, scale=ANGLE).then_inc(sines, 1)
                heads_of(act, body)

            @block.vector
            def _(dve):
                dve.wait_ge(table_in, 32)
                nc.vector.tensor_scalar(table_i[:], table[:, 1, :, :], TURN / TWO_PI, None, ALU.mult).then_inc(table_step, 1)
                dve.wait_ge(table_step, 1)
                nc.vector.tensor_scalar(table_i[:], table_i[:], WRAP, WRAP, ALU.logical_shift_left,
                                        ALU.arith_shift_right).then_inc(table_step, 1)
                dve.wait_ge(table_step, 2)
                nc.vector.tensor_copy(table[:, 1, :, :], table_i[:]).then_inc(table_step, 1)

                def scale(n, s, g, k):
                    if s == 0:
                        dve.wait_ge(const_ready, g + 1)
                    dve.wait_ge(drawn, n + 1)
                    wait_pos(dve, summed, n - RING + 1)
                    own = L - ACT_TURNS[s]
                    for f in range(NF):
                        cols = L if f < NF - 1 else own
                        if cols:
                            last = nc.vector.tensor_scalar(turn[:, s % RING, f, 0:cols], score[:, s % 2, 0:cols],
                                                           TURN / FREQS[f], head_c[:, k, 1, f:f + 1], ALU.mult, ALU.add)
                    last.then_inc(scaled, 1)

                def wrap(n, s):
                    dve.wait_ge(scaled, n + 1)
                    own = L - ACT_TURNS[s]
                    whole = turn[:, s % RING, :, :].rearrange("p f l -> p (f l)")[:, 0:NF * L - ACT_TURNS[s]]
                    last = nc.vector.tensor_scalar(whole, whole, WRAP, WRAP, *SHIFTS)
                    if ACT_TURNS[s]:
                        last = nc.vector.tensor_scalar(turn[:, s % RING, NF - 1, own:L], early[:, s % 2, own:L],
                                                       WRAP, WRAP, *SHIFTS)
                    last.then_inc(wrapped, 1)

                def finish(n, s, g, k):
                    dve.wait_ge(part_summed, n + 1)
                    dve.wait_ge(sines, n + 1)
                    if s % GROUPS == 0:
                        wait_pos(dve, weighted, 2 * g - 1 + s // GROUPS)
                    last = nc.vector.scalar_tensor_tensor(
                        weight[:, s, :], turn[:, s % RING, NF - 1, :].bitcast(FP32), head_c[:, k, 0, NF - 1:NF],
                        ps_sum[:, s % 2, :], ALU.mult, ALU.add)
                    if not FOURTH[s]:
                        last.then_inc(sum_step, 1)
                        dve.wait_ge(sum_step, g * SUM_STEPS + s + 1 - sum(FOURTH[:s]))
                        last = nc.vector.scalar_tensor_tensor(
                            weight[:, s, HALF:L], turn[:, s % RING, NF - 2, HALF:L].bitcast(FP32),
                            head_c[:, k, 0, NF - 2:NF - 1], weight[:, s, HALF:L], ALU.mult, ALU.add)
                    last.then_inc(summed, 1)

                scale(0, 0, 0, 0)
                wrap(0, 0)

                def body(g, k):
                    for s in range(U):
                        n = g * U + s
                        if s == 6 and after(g):
                            dve.wait_ge(turned, g)
                            wait_pos(dve, stored[1 - k], 8 * g - (16 if k == 0 else 8))
                            rows = ps_out[:, 0:LT * VW].rearrange("p (t c) -> p t c", c=VW)
                            nc.vector.tensor_copy(v_sum[:], ps_out[:, LT * VW:LT * VW + HD]).then_inc(norm_step, 1)
                            nc.vector.tensor_scalar(den[:, 0, :], rows[:, :, HD], float(L), 2 * EPS_DEN, ALU.add,
                                                    ALU.add).then_inc(norm_step, 1)
                            dve.wait_ge(norm_step, 4 * (g - 1) + 2)
                            nc.vector.reciprocal(den[:, 1, :], den[:, 0, :]).then_inc(norm_step, 1)
                            nc.vector.tensor_tensor(raised[:], rows[:, :, 0:HD], v_sum[:].unsqueeze(1).broadcast_to(
                                [P, LT, HD]), ALU.add).then_inc(norm_step, 1)
                            dve.wait_ge(norm_step, 4 * (g - 1) + 4)
                            nc.vector.tensor_tensor(out[:, 1 - k, :, :], raised[:],
                                                    den[:, 1, :].unsqueeze(2).broadcast_to([P, LT, HD]),
                                                    ALU.mult).then_inc(normed, 1)
                        if main(g) and unit_in(n + 1):
                            if s < U - 1:
                                scale(n + 1, s + 1, g, k)
                            else:
                                scale(n + 1, 0, g + 1, 1 - k)
                        if s > 1 and main(g):
                            finish(n - 2, s - 2, g, k)
                        if s < 2 and after(g):
                            finish(n - 2, U - 2 + s, g - 1, 1 - k)
                        if main(g) and unit_in(n + 1):
                            wrap(n + 1, (s + 1) % U)
                dve.wait_ge(table_step, 3)
                heads_of(dve, body)


def routed_block(nc, x, o_d, wo_a, bo, gamma, beta, mask, positions, router_w, router_b, wq, wk, wv, wo, w1, w2,
                 ln1, ln2, y_out):
    QH = 4
    C1 = 6.28125
    C2 = TWO_PI - C1
    ROUND = 1.5 * 2.0 ** 23
    PI_IN = float(np.nextafter(np.float32(np.pi), np.float32(0)))
    with ExitStack() as ctx:
        sb = lambda n, s, d=FP32: ctx.enter_context(nc.sbuf_tensor(n, s, d))
        sem = lambda n: ctx.enter_context(nc.semaphore(n))
        ident, tri, last_row = sb("ident", [P, P]), sb("tri", [P, P]), sb("last_row", [P, P])
        ones = sb("ones", [P, P])
        slot_i, slot = sb("slot_i", [P, P], I32), sb("slot", [P, P])
        tok_i, base_i = sb("tok_i", [P, LT], I32), sb("base_i", [P, B], I32)
        base = sb("base", [P, 2, B])
        pos_i, pos_f = sb("pos_i", [MB * LT, P], I32), sb("pos_f", [MB * LT, P])
        pos = sb("pos", [P, B, LT])
        inv_freq = sb("inv_freq", [P, NROT])
        rows = sb("rows", [P, 6, D])
        r_bias = sb("r_bias", [P, 1])
        woa_in, woa_t = sb("woa_in", [P, KC, D]), sb("woa_t", [P, KC, D])
        wqkv, wo_sb = sb("wqkv", [P, KC, 3 * D]), sb("wo_sb", [P, KC, D])
        w1_sb, w2_sb = sb("w1_sb", [P, KC, F]), sb("w2_sb", [P, FB, D])
        o_in, x_in = sb("o_in", [P, LT, D]), sb("x_in", [P, LT, D])
        o_t = sb("o_t", [P, KC, L])
        mix = sb("mix", [P, LT, D])
        x1 = sb("x1", [P, LT, D])
        dense = sb("dense", [P, LT, D])
        stats, moments = sb("stats", [P, 3, LT, 6]), sb("moments", [P, 3, LT, 2])
        spread = sb("spread", [P, 3, LT])
        dump, dump_b = sb("dump", [P, L]), sb("dump_b", [P, D])
        stats_b, moments_b = sb("stats_b", [P, 6]), sb("moments_b", [P, 2])
        w_col, w_diag, w_row = sb("w_col", [P, 2, LT]), sb("w_diag", [P, LT, P]), sb("w_row", [P, L])
        ahead, rank = sb("ahead", [P, LT, 3]), sb("rank", [P, LT])
        one_hot = sb("one_hot", [P, LT, P])
        ext = sb("ext", [P, LT, 3])
        xs, ext_s = sb("xs", [P, D]), sb("ext_s", [P, 3])
        mask_row = sb("mask_row", [P, 1], mybir.dt.uint32)
        out_row = sb("out_row", [P, 1], mybir.dt.uint32)
        m_row, m_t, m_sel = sb("m_row", [P, L]), sb("m_t", [P, LT, P]), sb("m_sel", [P, P])
        small = sb("small", [P, 16])
        hn, hn_t = sb("hn", [P, D]), sb("hn_t", [P, KC, P])
        qk, v_sb = sb("qk", [P, 2 * H, HD]), sb("v_sb", [P, D])
        ang, ang_r, trig = sb("ang", [P, 4, NROT]), sb("ang_r", [P, 2, NROT]), sb("trig", [P, 2, NROT])
        rot_a, rot_b = sb("rot_a", [P, 2 * H, HD]), sb("rot_b", [P, 2 * H, HD])
        qk_pad = sb("qk_pad", [P, 2 * H, 32])
        qk_t = sb("qk_t", [P, 2 * QH, P])
        logits, probs_t = sb("logits", [P, H, P]), sb("probs_t", [P, H, P])
        peak, total, inv_total = sb("peak", [P, H]), sb("total", [P, H]), sb("inv_total", [P, H])
        att, att_t = sb("att", [P, D]), sb("att_t", [P, KC, P])
        xa, h2, h2_t, g_t = sb("xa", [P, D]), sb("h2", [P, D]), sb("h2_t", [P, KC, P]), sb("g_t", [P, FB, P])
        xm, ys, res = sb("xm", [P, D]), sb("ys", [P, D]), sb("res", [P, D])
        A = ctx.enter_context(nc.psum_tensor("A", [P, 4, HALF], FP32))
        Bk = ctx.enter_context(nc.psum_tensor("Bk", [P, 4, HALF], FP32))

        names = ("in_loaded o_turned ot_drawn projected mix_added x_used var1 dev1 var2 dev2 diag_w w_spread w_drawn "
                 "hot gathered token_ready ms1 dev3 dense_var dense_dev dense_ready normed1 hn_turned hn_drawn "
                 "qkv qk_drawn angles trig_ready padded qk_turned qk_t_drawn mask_rows m_turned m_drawn "
                 "m_picked m_sel_drawn scored shifted exped p_turned p_lo p_hi attended att_ready att_turned "
                 "att_drawn mixed ms2 dev4 normed2 h2_turned h2_drawn up gelu_ready down var5 dev5 "
                 "res_ready dense_stored scattered thr_ready xb_ready out_row_ready").split()
        S = {n: sem("r_" + n) for n in names}
        const_in, const_set, pool_step, setup_pe = sem("const_in"), sem("const_set"), sem("pool_step"), sem("setup_pe")
        setup_dve, front_step, back_step = sem("setup_dve"), sem("front_step"), sem("back_step")
        gate_s, gated = sb("gate_s", [P, 2]), sem("gated")
        flat = lambda ap: ap.rearrange("p a b -> p (a b)")

        def batches(eng, body):
            body(None, 0)
            with eng.Fori(0, B - 1, 1) as b:
                body(b, b + 1)
            body(B - 1, None)

        def ready_of(eng, n):
            return lambda *names: [eng.wait_ge(S[name], n + 1) for name in names]

        with nc.Block() as block:

            @block.sync
            def _(sp):
                load = lambda dst, src: sp.dma_start(dst, src).then_inc(const_in, 16)
                load(woa_in[:], wo_a.rearrange("(m p) i -> p m i", p=P))
                for n, v in enumerate((bo, gamma, beta, router_w.rearrange("d o -> (d o)"), ln1, ln2)):
                    load(rows[:, n, :], v.partition_broadcast(P))
                load(r_bias[:], router_b.partition_broadcast(P))
                load(pos_i[:], positions.rearrange("b (t p) -> (b t) p", p=P))
                for n, w in enumerate((wq, wk, wv)):
                    load(wqkv[:, :, n * D:(n + 1) * D], w.rearrange("(c p) n -> p c n", p=P))
                load(wo_sb[:], wo.rearrange("(c p) n -> p c n", p=P))
                load(w1_sb[:], w1.rearrange("(c p) n -> p c n", p=P))
                load(w2_sb[:], w2.rearrange("(c p) n -> p c n", p=P))

                def fetch(n):
                    sp.dma_start(o_in[:], o_d[n, :, :, :]).then_inc(S["in_loaded"], 16)
                    sp.dma_start(x_in[:], x[n, :, :].rearrange("(t p) d -> p t d", p=P)).then_inc(S["in_loaded"], 16)

                def store(n):
                    sp.wait_ge(S["dense_ready"], n + 1)
                    sp.dma_start(y_out[n, :, :].rearrange("(t p) d -> p t d", p=P), dense[:]).then_inc(S["dense_stored"], 16)

                sp.sem_inc(S["dense_stored"], 16)
                fetch(0)
                with sp.Fori(0, B - 1, 1) as b:
                    sp.wait_ge(S["x_used"], b + 1)
                    fetch(b + 1)
                    store(b)
                store(B - 1)
                sp.wait_ge(S["dense_stored"], 16 * B + 16)

            @block.gpsimd
            def _(pool):
                nc.gpsimd.memset(ident[:], 0.0).then_inc(pool_step, 1)
                nc.gpsimd.memset(tri[:], 1.0).then_inc(pool_step, 1)
                nc.gpsimd.memset(last_row[:], 0.0).then_inc(pool_step, 1)
                nc.gpsimd.memset(ones[:], 1.0)
                nc.gpsimd.memset(gate_s[:], 1.0)
                pool.sem_inc(gated, 1)
                nc.gpsimd.memset(flat(qk_pad[:]), 0.0)
                for n in range(NROT):
                    nc.gpsimd.memset(inv_freq[:, n:n + 1], float(np.float32(1.0) / np.float32(ROPE_BASE) ** np.float32(2 * n / HD)))
                nc.gpsimd.iota(slot_i[:], pattern=[[1, P]], base=0, channel_multiplier=0)
                nc.gpsimd.iota(tok_i[:], pattern=[[P, LT]], base=0, channel_multiplier=1)
                nc.gpsimd.iota(base_i[:], pattern=[[L, B]], base=0, channel_multiplier=0).then_inc(pool_step, 1)
                pool.wait_ge(pool_step, 4)
                nc.gpsimd.affine_select(out=ident[:], in_=ident[:], compare_op=ALU.not_equal, fill=1.0, base=0,
                                        pattern=[[-1, P]], channel_multiplier=1)
                nc.gpsimd.affine_select(out=tri[:], in_=tri[:], compare_op=ALU.is_gt, fill=0.0, base=0,
                                        pattern=[[-1, P]], channel_multiplier=1)
                nc.gpsimd.affine_select(out=last_row[:], in_=last_row[:], compare_op=ALU.not_equal, fill=1.0,
                                        base=-KSEL, pattern=[[0, P]], channel_multiplier=1).then_inc(const_set, 1)
                pool.wait_ge(const_in, 16 * CONST_LOADS)

                def gate(n):
                    pool.wait_ge(gated, n + 1)
                    nc.gpsimd.tensor_tensor(gate_s[:, 1:2], gate_s[:, 0:1], gate_s[:, 0:1], ALU.mult).then_inc(gated, 1)

                def body(back, front):
                    passed = 0 if back is None else 3 * back + 1
                    if front is not None:
                        pool.wait_ge(S["in_loaded"], 32 * front + 32)
                        nc.gpsimd.tensor_tensor(x_in[:], x_in[:], rows[:, 2, :].unsqueeze(1).broadcast_to([P, LT, D]),
                                                ALU.add).then_inc(S["xb_ready"], 1)
                    if back is not None:
                        pool.wait_ge(S["out_row_ready"], back + 1)
                        pool.wait_ge(S["res_ready"], back + 1)
                        pool.wait_ge(S["dense_stored"], 16 * back + 32)
                        gate(passed)
                        passed += 1
                        pool.indirect_dma_start(
                            out=y_out.rearrange("b l d -> (b l) d"),
                            out_offset=bass.IndirectOffsetOnAxis(ap=out_row[0:KSEL, :], axis=0),
                            in_=res[0:KSEL, :], in_offset=None).then_inc(S["scattered"], 16)
                    if front is not None:
                        pool.wait_ge(S["token_ready"], front + 1)
                        wait_pos(pool, S["m_turned"], front)
                        gate(passed)
                        passed += 1
                        pool.indirect_dma_start(
                            out=m_row[:], out_offset=None, in_=mask.rearrange("b o q k -> (b o q) k"),
                            in_offset=bass.IndirectOffsetOnAxis(ap=mask_row[:, :], axis=0)).then_inc(S["mask_rows"], 16)
                    if back is not None:
                        pool.wait_ge(S["scattered"], 16 * back + 16)
                        gate(passed)
                batches(pool, body)

            @block.tensor
            def _(pe):
                mm, tr = nc.tensor.matmul, nc.tensor.transpose
                pe.wait_ge(const_set, 1)
                pe.wait_ge(const_in, 16 * CONST_LOADS)
                for i in range(KC):
                    for m in range(KC):
                        tr(A[:, 0, i * D + m * P:i * D + (m + 1) * P], woa_in[:, m, i * P:(i + 1) * P], ident[:])
                pe.wait_ge(setup_dve, 1)
                tr(A[:, 1, 0:MB * LT], pos_f[:], ident[0:MB * LT, 0:MB * LT]).then_inc(setup_pe, 1)
                pe.wait_ge(setup_dve, 2)

                def turn_two(out, src, done):
                    for c in range(KC):
                        ins = tr(out[:, c * P:(c + 1) * P], src[:, c * P:(c + 1) * P], ident[:])
                    ins.then_inc(S[done], 1)

                def body(back, front):
                    ready, ready_f = ready_of(pe, back), ready_of(pe, front)

                    def turn_o(half):
                        for c in range(KC):
                            for t in range(4):
                                ins = tr(A[:, c, t * P:(t + 1) * P], o_in[:, 4 * half + t, c * P:(c + 1) * P], ident[:])
                        ins.then_inc(S["o_turned"], 1)

                    def project(half):
                        for t in range(4):
                            for c in range(KC):
                                ins = mm(A[:, 2 + t // 2, (t % 2) * D:(t % 2 + 1) * D],
                                         o_t[:, c, half * HALF + t * P:half * HALF + (t + 1) * P],
                                         woa_t[:, c, :], start=(c == 0), stop=(c == KC - 1))
                        ins.then_inc(S["projected"], 1)

                    if back is not None:
                        ready("token_ready")
                        mm(Bk[:, 3, 0:1], last_row[:], ext_s[:, 0:1], start=True, stop=True).then_inc(S["thr_ready"], 1)
                        ready("normed1")
                        turn_two(Bk[:, 0, :], hn, "hn_turned")
                    if front is not None:
                        pe.wait_ge(S["in_loaded"], 32 * front + 32)
                        wait_pos(pe, S["w_drawn"], front)
                        turn_o(0)
                    if back is not None:
                        ready("hn_drawn")
                        for c in range(KC):
                            mm(Bk[:, 1, :], hn_t[:, c, :], wqkv[:, c, 0:2 * D], start=(c == 0), stop=(c == KC - 1))
                        for c in range(KC):
                            ins = mm(Bk[:, 2, 0:D], hn_t[:, c, :], wqkv[:, c, 2 * D:3 * D], start=(c == 0), stop=(c == KC - 1))
                        ins.then_inc(S["qkv"], 1)
                    if front is not None:
                        pe.wait_ge(S["ot_drawn"], 2 * front + 1)
                        wait_pos(pe, S["ms1"], front)
                        project(0)
                        turn_o(1)
                    if back is not None:
                        pe.wait_ge(S["mask_rows"], 16 * back + 16)
                        ready("qk_drawn")
                        for t in range(LT):
                            ins = tr(Bk[:, t // 4, (t % 4) * P:(t % 4 + 1) * P], m_row[:, t * P:(t + 1) * P], ident[:])
                        ins.then_inc(S["m_turned"], 1)
                    if front is not None:
                        pe.wait_ge(S["ot_drawn"], 2 * front + 2)
                        pe.wait_ge(S["mix_added"], 2 * front + 1)
                        project(1)
                    if back is not None:
                        ready("m_drawn")
                        for t in range(LT):
                            ins = mm(Bk[:, 2, 0:P], m_t[:, t, :], one_hot[:, t, :], start=(t == 0), stop=(t == LT - 1))
                        ins.then_inc(S["m_picked"], 1)
                        ready("padded")
                        for n in range(2 * QH):
                            ins = tr(Bk[:, n // 4, (n % 4) * P:(n % 4 + 1) * P],
                                     qk_pad[:, n * QH:(n + 1) * QH, :].rearrange("p a b -> p (a b)"), ident[:])
                        ins.then_inc(S["qk_turned"], 1)
                        ready("qk_t_drawn", "m_sel_drawn")
                        for n in range(QH):
                            for r in range(QH):
                                rows_r = slice(32 * r, 32 * r + HD)
                                ins = mm(Bk[:, r, n * P:(n + 1) * P], qk_t[rows_r, n, :], qk_t[rows_r, QH + n, :], start=True, stop=True)
                        ins.then_inc(S["scored"], 1)
                        ready("exped")
                        for n in range(H):
                            ins = tr(Bk[0:KSEL, n // 4, (n % 4) * P:(n % 4 + 1) * P], logits[:, n, 0:KSEL], ident[:])
                        ins.then_inc(S["p_turned"], 1)
                    if front is not None:
                        ready_f("diag_w")
                        for t in range(LT):
                            ins = mm(A[:, t // 4, (t % 4) * P:(t % 4 + 1) * P], ones[:], w_diag[:, t, :], start=True, stop=True)
                        ins.then_inc(S["w_spread"], 1)
                    if back is not None:
                        ready("p_lo", "p_hi")
                        for n in range(H):
                            h = 4 * (n % 4) + n // 4
                            ins = mm(Bk[:, 0, h * HD:(h + 1) * HD], probs_t[0:KSEL, n, :], v_sb[0:KSEL, h * HD:(h + 1) * HD],
                                     start=True, stop=True)
                        ins.then_inc(S["attended"], 1)
                        ready("att_ready")
                        turn_two(Bk[:, 1, :], att, "att_turned")
                        ready("att_drawn")
                        for c in range(KC):
                            ins = mm(Bk[:, 2, 0:D], att_t[:, c, :], wo_sb[:, c, :], start=(c == 0), stop=(c == KC - 1))
                        ins.then_inc(S["mixed"], 1)
                        ready("normed2")
                        turn_two(Bk[:, 3, :], h2, "h2_turned")
                        ready("h2_drawn")
                        for n in range(FB):
                            for c in range(KC):
                                ins = mm(Bk[:, n // 4, (n % 4) * P:(n % 4 + 1) * P], w1_sb[:, c, n * P:(n + 1) * P],
                                         h2_t[:, c, :], start=(c == 0), stop=(c == KC - 1))
                            if n % 4 == 3:
                                ins.then_inc(S["up"], 1)
                        for n in range(FB):
                            if n % 4 == 0:
                                pe.wait_ge(S["gelu_ready"], 2 * back + n // 4 + 1)
                            ins = mm(Bk[:, 2, 0:D], g_t[:, n, :], w2_sb[:, n, :], start=(n == 0), stop=(n == FB - 1))
                        ins.then_inc(S["down"], 1)
                    if front is not None:
                        ready_f("hot")
                        for t in range(LT):
                            mm(A[:, 2, 0:D], one_hot[:, t, :], x1[:, t, :], start=(t == 0), stop=(t == LT - 1))
                        for t in range(LT):
                            ins = mm(A[:, 3, 0:3], one_hot[:, t, :], ext[:, t, :], start=(t == 0), stop=(t == LT - 1))
                        ins.then_inc(S["gathered"], 1)
                batches(pe, body)

            @block.scalar
            def _(act):
                def body(back, front):
                    ready, ready_f = ready_of(act, back), ready_of(act, front)
                    run = lambda out, src, fn, done: nc.scalar.activation(out, src, fn).then_inc(S[done], 1)

                    def draw_o(half):
                        act.wait_ge(S["o_turned"], 2 * front + half + 1)
                        if half == 0:
                            wait_pos(act, S["projected"], 2 * front)
                        run(o_t[:, :, half * HALF:(half + 1) * HALF], A[:, 0:2, :], ACT.Copy, "ot_drawn")

                    if back is not None:
                        ready("ms1")
                        run(small[:, 1:2], small[:, 0:1], ACT.Sqrt, "dev3")
                        ready("hn_turned")
                        run(flat(hn_t[:]), Bk[:, 0, 0:D], ACT.Copy, "hn_drawn")
                    if front is not None:
                        draw_o(0)
                    if back is not None:
                        ready("qkv")
                        nc.scalar.activation(flat(qk[:]), Bk[:, 1, :], ACT.Copy)
                        run(v_sb[:], Bk[:, 2, 0:D], ACT.Copy, "qk_drawn")
                        ready("dense_var")
                        run(spread[:, 2, :], spread[:, 2, :], ACT.Sqrt, "dense_dev")
                        ready("angles")
                        run(trig[:], ang_r[:], ACT.Sin, "trig_ready")
                    if front is not None:
                        draw_o(1)
                    if back is not None:
                        ready("m_turned")
                        run(flat(m_t[:]), flat(Bk[:, 0:2, :]), ACT.Copy, "m_drawn")
                        ready("m_picked")
                        run(m_sel[:], Bk[:, 2, 0:P], ACT.Copy, "m_sel_drawn")
                        ready("qk_turned")
                        run(flat(qk_t[:]), flat(Bk[:, 0:2, :]), ACT.Copy, "qk_t_drawn")
                    if front is not None:
                        ready_f("var1")
                        run(spread[:, 0, :], spread[:, 0, :], ACT.Sqrt, "dev1")
                        ready_f("var2")
                        run(spread[:, 1, :], spread[:, 1, :], ACT.Sqrt, "dev2")
                    if back is not None:
                        ready("shifted")
                        run(logits[:, :, 0:KSEL], logits[:, :, 0:KSEL], ACT.Exp, "exped")
                        ready("p_turned")
                        run(probs_t[0:KSEL, 8:16, :].rearrange("p a b -> p (a b)"), flat(Bk[0:KSEL, 2:4, :]), ACT.Copy, "p_hi")
                    if front is not None:
                        ready_f("w_spread")
                        run(w_row[:], flat(A[:, 0:2, :]), ACT.Copy, "w_drawn")
                    if back is not None:
                        ready("att_turned")
                        run(flat(att_t[:]), Bk[:, 1, 0:D], ACT.Copy, "att_drawn")
                        ready("ms2")
                        run(small[:, 4:5], small[:, 3:4], ACT.Sqrt, "dev4")
                        ready("h2_turned")
                        run(flat(h2_t[:]), Bk[:, 3, 0:D], ACT.Copy, "h2_drawn")
                        for half in range(2):
                            act.wait_ge(S["up"], 2 * back + half + 1)
                            run(flat(g_t[:, 4 * half:4 * half + 4, :]), Bk[:, half, :], ACT.Gelu_apprx_tanh, "gelu_ready")
                        ready("var5")
                        run(small[:, 7:8], small[:, 6:7], ACT.Sqrt, "dev5")
                batches(act, body)

            @block.vector
            def _(dve):
                v = nc.vector
                setup = Chain(dve, sem("dve_setup"), 0, 0, 0)
                dve.wait_ge(const_set, 1)
                dve.wait_ge(const_in, 16 * CONST_LOADS)
                v.tensor_copy(slot[:], slot_i[:])
                v.tensor_copy(ext[:, :, 1], tok_i[:])
                setup.step(v.tensor_copy(base[:, 0, :], base_i[:]))
                v.tensor_scalar(base[:, 1, :], base[:, 0, :], float((MB - 1) * L), None, ALU.min)
                v.tensor_copy(pos_f[:], pos_i[:]).then_inc(setup_dve, 1)
                dve.wait_ge(setup_pe, 1)
                v.tensor_copy(flat(woa_t[:]), A[:, 0, :])
                for n in range(0, B, MB):
                    src = A[:, 1, 0:MB * LT].rearrange("p (b t) -> p b t", b=MB)
                    if n == 0:
                        setup.step(v.tensor_copy(pos[:, 0:MB, :], src))
                    else:
                        setup.step(v.tensor_copy(pos[:, n:n + MB, :], src[:, MB - 1:MB, :].broadcast_to([P, MB, LT])))
                v.tensor_copy(slot[:, 0:1], slot_i[:, 0:1]).then_inc(setup_dve, 1)
                dve.wait_ge(setup_dve, 2)

                def body(back, front):
                    ready, ready_f = ready_of(dve, back), ready_of(dve, front)
                    chain = Chain(dve, back_step, 0, BACK_STEPS, back)
                    chain_f = Chain(dve, front_step, 0, FRONT_STEPS, front)
                    step, step_f = chain.step, chain_f.step

                    def moments_of(step, src, n, name, eps):
                        for t in range(LT):
                            ins = v.bn_stats(stats[:, n, t, :], src[:, t, :])
                        step(ins)
                        v.memset(spread[:, n, :], 0.0)
                        for t in range(LT):
                            ins = v.bn_aggr(moments[:, n, t, :], stats[:, n, t, :])
                        step(ins)
                        v.tensor_scalar(spread[:, n, :], moments[:, n, :, 1], eps, None, ALU.add).then_inc(S[name], 1)

                    def ranks(tiles):
                        for t in tiles:
                            mine = w_col[:, 1, t:t + 1]
                            if t:
                                step_f(v.tensor_scalar(dump[:, 0:t * P], w_row[:, 0:t * P], mine, None, ALU.is_ge, ALU.add,
                                                     accum_out=ahead[:, t, 0:1]))
                            step_f(v.tensor_scalar(dump[:, t * P:L], w_row[:, t * P:L], mine, None, ALU.is_gt, ALU.add,
                                                 accum_out=ahead[:, t, 1:2]))
                            step_f(v.scalar_tensor_tensor(dump[:, 0:P], w_row[:, t * P:(t + 1) * P], mine, tri[:],
                                                        ALU.is_equal, ALU.mult, accum_out=ahead[:, t, 2:3]))

                    def add_bias(half):
                        dve.wait_ge(S["projected"], 2 * front + half + 1)
                        for n in range(2):
                            ins = v.tensor_tensor(mix[:, 4 * half + 2 * n:4 * half + 2 * n + 2, :],
                                                  A[:, 2 + n, :].rearrange("p (a b) -> p a b", a=2),
                                                  rows[:, 0, :].unsqueeze(1).broadcast_to([P, 2, D]), ALU.add)
                        ins.then_inc(S["mix_added"], 1)

                    if back is not None:
                        ready("dev3")
                        step(v.reciprocal(small[:, 5:6], small[:, 1:2]))
                        v.scalar_tensor_tensor(hn[:], xs[:], small[:, 5:6], rows[:, 4, :], ALU.mult, ALU.mult).then_inc(S["normed1"], 1)
                        step(v.tensor_scalar(ang[:, 0, :], inv_freq[:], ext_s[:, 2:3], None, ALU.mult))
                        step(v.tensor_scalar(ang[:, 1, :], ang[:, 0, :], 1.0 / TWO_PI, ROUND, ALU.mult, ALU.add))
                        step(v.tensor_scalar(ang[:, 2, :], ang[:, 1, :], ROUND, None, ALU.subtract))
                        step(v.scalar_tensor_tensor(ang[:, 3, :], ang[:, 2, :], -C1, ang[:, 0, :], ALU.mult, ALU.add))
                        step(v.scalar_tensor_tensor(ang[:, 1, :], ang[:, 2, :], -C2, ang[:, 3, :], ALU.mult, ALU.add))
                        step(v.tensor_scalar(ang_r[:, 0, :], ang[:, 1, :], PI_IN, -PI_IN, ALU.min, ALU.max))
                        step(v.scalar_tensor_tensor(ang[:, 2, :], ang_r[:, 0, :], -1.0, ang_r[:, 0, :], ALU.mult, ALU.max))
                        v.tensor_scalar(ang_r[:, 1, :], ang[:, 2, :], -1.0, float(np.pi / 2), ALU.mult, ALU.add).then_inc(S["angles"], 1)
                        ready("thr_ready")
                        step(v.tensor_scalar(small[:, 8:9], ext_s[:, 0:1], Bk[:, 3, 0:1], -1.0, ALU.is_gt, ALU.mult))
                        step(v.tensor_scalar(small[:, 9:10], small[:, 8:9], 2.0, None, ALU.add))
                        dve.wait_ge(gated, 3 * back + 2)
                        v.tensor_scalar(out_row[:], ext_s[:, 1:2], base[:, 0, bass.ds(back, 1)], None, ALU.add).then_inc(S["out_row_ready"], 1)
                        moments_of(step, x1, 2, "dense_var", EPS_LN / 4)
                    if front is not None:
                        add_bias(0)
                    if back is not None:
                        ready("dense_dev")
                        step(v.reciprocal(spread[:, 2, :], spread[:, 2, :]))
                        dve.wait_ge(S["dense_stored"], 16 * back + 16)
                        for t in range(LT):
                            ins = v.tensor_scalar(dense[:, t, :], x1[:, t, :], moments[:, 2, t, 0:1], spread[:, 2, t:t + 1],
                                                  ALU.subtract, ALU.mult)
                        ins.then_inc(S["dense_ready"], 1)
                    if front is not None:
                        add_bias(1)
                        dve.wait_ge(S["mix_added"], 2 * front + 2)
                        moments_of(step_f, mix, 0, "var1", EPS_LN)
                    if back is not None:
                        ready("qk_drawn", "trig_ready")
                        halves = lambda t: t[:].rearrange("p h (s f) -> p h s f", s=2)
                        cos, sin = (trig[:, n, :].unsqueeze(1).broadcast_to([P, 2 * H, NROT]) for n in (1, 0))
                        q2, a2, b2 = halves(qk), halves(rot_a), halves(rot_b)
                        for s in range(2):
                            v.tensor_tensor(a2[:, :, s, :], q2[:, :, s, :], cos, ALU.mult)
                            ins = v.tensor_tensor(b2[:, :, s, :], q2[:, :, 1 - s, :], sin, ALU.mult)
                        step(ins)
                        v.tensor_tensor(qk_pad[:, :, 0:NROT], a2[:, :, 0, :], b2[:, :, 0, :], ALU.subtract)
                        v.tensor_tensor(qk_pad[:, :, NROT:HD], a2[:, :, 1, :], b2[:, :, 1, :], ALU.add).then_inc(S["padded"], 1)
                    if front is not None:
                        for t in range(LT):
                            ins = v.scalar_tensor_tensor(mix[:, t, :], mix[:, t, :], moments[:, 0, t, 0:1], rows[:, 1, :],
                                                         ALU.subtract, ALU.mult)
                        step_f(ins)
                        ready_f("dev1")
                        step_f(v.reciprocal(spread[:, 0, :], spread[:, 0, :]))
                        ready_f("xb_ready")
                        for t in range(LT):
                            ins = v.scalar_tensor_tensor(mix[:, t, :], mix[:, t, :], spread[:, 0, t:t + 1], x_in[:, t, :],
                                                         ALU.mult, ALU.add)
                        ins.then_inc(S["x_used"], 1)
                        dve.wait_ge(S["x_used"], front + 1)
                        moments_of(step_f, mix, 1, "var2", EPS_LN)
                    if back is not None:
                        ready("scored", "m_sel_drawn")
                        for r in range(QH):
                            ins = v.scalar_tensor_tensor(logits[:, 4 * r:4 * r + 4, :], Bk[:, r, :].rearrange("p (a b) -> p a b", a=4),
                                                         1.0 / float(np.sqrt(HD)), m_sel[:].unsqueeze(1).broadcast_to([P, 4, P]),
                                                         ALU.mult, ALU.add)
                        step(ins)
                        step(v.tensor_reduce(peak[:], logits[:, :, 0:KSEL], AX.X, ALU.max))
                        v.tensor_tensor(logits[:, :, 0:KSEL], logits[:, :, 0:KSEL], peak[:].unsqueeze(2).broadcast_to([P, H, KSEL]),
                                        ALU.subtract).then_inc(S["shifted"], 1)
                    if front is not None:
                        ready_f("dev2")
                        step_f(v.reciprocal(spread[:, 1, :], spread[:, 1, :]))
                        for t in range(LT):
                            ins = v.tensor_scalar(x1[:, t, :], mix[:, t, :], moments[:, 1, t, 0:1], spread[:, 1, t:t + 1],
                                                  ALU.subtract, ALU.mult)
                        step_f(ins)
                    if back is not None:
                        ready("exped")
                        step(v.tensor_reduce(total[:], logits[:, :, 0:KSEL], AX.X, ALU.add))
                        step(v.reciprocal(inv_total[:].rearrange("p (n r) -> p r n", r=QH), total[:].rearrange("p (r n) -> p r n", r=QH)))
                    if front is not None:
                        for t in range(LT):
                            ins = v.tensor_tensor_reduce(out=dump[:, 0:D], in0=x1[:, t, :],
                                                         in1=rows[:, 3, :], scale=1.0, scalar=0.0, op0=ALU.mult, op1=ALU.add,
                                                         accum_out=w_col[:, 0, t:t + 1])
                            step_f(ins)
                        step_f(v.tensor_scalar(w_col[:, 1, :], w_col[:, 0, :], r_bias[:, 0:1], None, ALU.add))
                        v.tensor_copy(ext[:, :, 0], w_col[:, 1, :])
                        v.tensor_copy(ext[:, :, 2], pos[:, bass.ds(front, 1), :].rearrange("p a t -> p (a t)"))
                        for t in range(LT):
                            ins = v.tensor_scalar(w_diag[:, t, :], ident[:], w_col[:, 1, t:t + 1], None, ALU.mult)
                        ins.then_inc(S["diag_w"], 1)
                    if back is not None:
                        ready("p_turned")
                        v.tensor_copy(probs_t[0:KSEL, 0:8, :].rearrange("p a b -> p (a b)"), flat(Bk[0:KSEL, 0:2, :])).then_inc(S["p_lo"], 1)
                    if front is not None:
                        ready_f("w_drawn")
                        step_f(v.memset(ahead[:, 0, 0:1], 0.0))
                        ranks(range(3))
                    if back is not None:
                        ready("attended")
                        v.tensor_tensor(att[:].rearrange("p (h d) -> p h d", d=HD), Bk[:, 0, 0:D].rearrange("p (h d) -> p h d", d=HD),
                                        inv_total[:].unsqueeze(2).broadcast_to([P, H, HD]), ALU.mult).then_inc(S["att_ready"], 1)
                    if front is not None:
                        ranks(range(3, 4))
                    if back is not None:
                        ready("mixed")
                        step(v.tensor_tensor(xa[:], Bk[:, 2, 0:D], xs[:], ALU.add))
                        step(v.tensor_tensor_reduce(out=dump_b[:], in0=xa[:], in1=xa[:], scale=1.0 / D, scalar=0.0,
                                                    op0=ALU.mult, op1=ALU.add, accum_out=small[:, 10:11]))
                        v.tensor_scalar(small[:, 3:4], small[:, 10:11], EPS_RMS, None, ALU.add).then_inc(S["ms2"], 1)
                    if front is not None:
                        ranks(range(4, 5))
                    if back is not None:
                        ready("dev4")
                        step(v.reciprocal(small[:, 11:12], small[:, 4:5]))
                        v.scalar_tensor_tensor(h2[:], xa[:], small[:, 11:12], rows[:, 5, :], ALU.mult, ALU.mult).then_inc(S["normed2"], 1)
                    if front is not None:
                        ranks(range(5, LT))
                        step_f(v.tensor_reduce(rank[:], ahead[:], AX.X, ALU.add))
                        for t in range(LT):
                            ins = v.tensor_scalar(one_hot[:, t, :], slot[:], rank[:, t:t + 1], None, ALU.is_equal)
                        ins.then_inc(S["hot"], 1)
                    if back is not None:
                        ready("down")
                        step(v.tensor_tensor(xm[:], Bk[:, 2, 0:D], xa[:], ALU.add))
                        step(v.tensor_scalar(xm[:], xm[:], ext_s[:, 0:1], None, ALU.mult))
                        step(v.scalar_tensor_tensor(ys[:], xs[:], small[:, 9:10], xm[:], ALU.mult, ALU.add))
                        step(v.bn_stats(stats_b[:], ys[:]))
                        v.memset(small[:, 6:7], 0.0)
                        step(v.bn_aggr(moments_b[:], stats_b[:]))
                        v.tensor_scalar(small[:, 6:7], moments_b[:, 1:2], EPS_LN, None, ALU.add).then_inc(S["var5"], 1)
                        ready("dev5")
                        step(v.reciprocal(small[:, 12:13], small[:, 7:8]))
                        v.tensor_scalar(res[:], ys[:], moments_b[:, 0:1], small[:, 12:13], ALU.subtract, ALU.mult).then_inc(S["res_ready"], 1)
                    if front is not None:
                        ready_f("gathered")
                        step_f(v.tensor_copy(ext_s[:], A[:, 3, 0:3]))
                        v.tensor_scalar(mask_row[:], ext_s[:, 1:2], base[:, 1, bass.ds(front, 1)], None, ALU.add).then_inc(S["token_ready"], 1)
                        step_f(v.tensor_copy(xs[:], A[:, 2, 0:D]))
                        step_f(v.tensor_tensor_reduce(out=dump[:, 0:D], in0=xs[:], in1=xs[:], scale=1.0 / D, scalar=0.0,
                                                    op0=ALU.mult, op1=ALU.add, accum_out=small[:, 2:3]))
                        v.tensor_scalar(small[:, 0:1], small[:, 2:3], EPS_RMS, None, ALU.add).then_inc(S["ms1"], 1)
                    if back is not None:
                        chain.close()
                    if front is not None:
                        chain_f.close()
                batches(dve, body)


FRONT_STEPS, BACK_STEPS = 45, 27
CONST_LOADS = 15

_INS = [f"L0_attn_{n}" for n in "x Wq bq Wk bk Wv bv Wo bo alpha phi temperature gamma beta".split()] + \
       [f"L0_ffn_{n}" for n in "attention_mask position_ids router_w router_b wq wk wv wo w1 w2 ln1 ln2".split()]


def build(nc, t, out):
    scratch = lambda n, s, d=FP32: nc.dram_tensor(n, s, d, kind="Internal").ap()
    q_d, k_d = scratch("q_d", [B, PARTS, D, L], BF16), scratch("k_d", [B, PARTS, D, L], BF16)
    v_d, o_d = scratch("v_d", [B, P, LT, D]), scratch("o_d", [B, P, LT, D])
    a = lambda n: t[f"L0_attn_{n}"]
    f = lambda n: t[f"L0_ffn_{n}"]
    project_qkv(nc, a("x"), a("Wq"), a("bq"), a("Wk"), a("bk"), a("Wv"), a("bv"), a("temperature"), q_d, k_d, v_d)
    oscillatory_attention(nc, a("alpha"), a("phi"), q_d, k_d, v_d, o_d)
    routed_block(nc, a("x"), o_d, a("Wo"), a("bo"), a("gamma"), a("beta"), f("attention_mask"), f("position_ids"),
                 f("router_w"), f("router_b"), f("wq"), f("wk"), f("wv"), f("wo"), f("w1"), f("w2"), f("ln1"), f("ln2"), out)


def kernel(**inputs):
    import concourse.bacc as bacc
    from concourse.bass_utils import run_bass_kernel_spmd

    nc = bacc.Bacc("TRN2", target_bir_lowering=False, num_devices=1)
    arrays, t = {}, {}
    for name in _INS:
        v = np.ascontiguousarray(inputs[name])
        arrays[f"in_{name}"] = v
        t[name] = nc.dram_tensor(f"in_{name}", v.shape, mybir.dt.from_np(v.dtype), kind="ExternalInput").ap()
    out = nc.dram_tensor("out_0", (B, L, D), FP32, kind="ExternalOutput").ap()
    build(nc, t, out)
    r = run_bass_kernel_spmd(nc, [arrays], core_ids=[0])
    return r.results[0]["out_0"]
```
